# Optimizing a Trainium2 kernel written in Bass

```python
import numpy as np
import jax
import jax.numpy as jnp

def _softmax(x, axis=-1):
    return jax.nn.softmax(x, axis=axis)

def _gelu(x):
    return jax.nn.gelu(x, approximate=True)

def _silu(x):
    return jax.nn.silu(x)

def _sigmoid(x):
    return jax.nn.sigmoid(x)

def _layernorm(x, axis=-1, eps=1e-05):
    m = jnp.mean(x, axis=axis, keepdims=True)
    v = jnp.var(x, axis=axis, keepdims=True)
    return (x - m) / jnp.sqrt(v + eps)

def _scatter_add(tgt, idx, src, axis=0):
    return tgt.at[idx].add(src)

def _segment_sum(src, seg, n):
    return jax.ops.segment_sum(src, seg, n)
kernel_name = 'mk_adaln_d1_jaxref_r8_d39bb7'

def setup_inputs(seed: int=0):
    np.random.seed(seed)
    _w = jnp.asarray

    def _L0_attn_setup():
        import jax, jax.numpy as jnp
        import numpy as np
        N_HEAD = 16
        HEAD_SIZE = 128
        EMBED = 128
        MULTI_HEAD_SIZE = HEAD_SIZE // N_HEAD
        B, S = (4, 256)
        key = jax.random.key(seed)
        k1, k2, k3, k4 = jax.random.split(key, 4)
        x = jax.random.normal(k1, (B, S, EMBED), dtype=jnp.float32)
        w_qkv = jax.random.normal(k2, (3 * HEAD_SIZE, EMBED), dtype=jnp.float32) * 0.02
        w_proj = jax.random.normal(k3, (EMBED, HEAD_SIZE), dtype=jnp.float32) * 0.02
        b_proj = jax.random.normal(k4, (EMBED,), dtype=jnp.float32) * 0.02
        return {'x': x, 'w_qkv': w_qkv, 'w_proj': w_proj, 'b_proj': b_proj}
    _L0_attn_in = _L0_attn_setup()

    def _L0_ffn_setup():
        import jax, jax.numpy as jnp
        import numpy as np
        D = 128
        HQ = 16
        HKV = 4
        G = HQ // HKV
        K = 64
        V = 64
        E = 8
        TOPK = 2
        HID = 256
        CAP_FRAC = 0.125
        EPS = 1e-06

        def _rmsnorm(x, g):
            return x * jax.lax.rsqrt(jnp.mean(x * x, axis=-1, keepdims=True) + EPS) * g

        def _rotary_tables(t, dim):
            thetas = 10000.0 ** (-np.arange(0, dim, 2, dtype=np.float32) / dim)
            ticks = np.outer(np.arange(t, dtype=np.float32), thetas)
            ticks = np.tile(ticks, (1, 2))[None, :, None, :]
            return (jnp.asarray(np.cos(ticks)), jnp.asarray(np.sin(ticks)))

        def _neg_half(x):
            x1, x2 = jnp.split(x, 2, axis=-1)
            return jnp.concatenate([-x2, x1], axis=-1)

        def _attention(x, wq, wk, wv, wo):
            b, t, _ = x.shape
            q = (x @ wq).reshape(b, t, HQ, K)
            k = (x @ wk).reshape(b, t, HKV, K)
            v = (x @ wv).reshape(b, t, HKV, V)
            cos, sin = _rotary_tables(t, K)
            q = q * cos + _neg_half(q) * sin
            k = k * cos + _neg_half(k) * sin
            qg = q.reshape(b, t, G, HKV, K)
            scores = jnp.einsum('btghk,bThk->bghtT', qg, k)
            mask = jnp.tril(jnp.ones((t, t), bool))
            scores = jnp.where(mask, scores, -jnp.inf) / np.float32(np.sqrt(K))
            p = jax.nn.softmax(scores, axis=-1)
            out = jnp.einsum('bghtT,bThv->btghv', p, v).reshape(b, t, HQ * V)
            return out @ wo

        def _moe(x, router_w, router_b, w1, w2, w3):
            b, t, d = x.shape
            n = b * t
            xf = x.reshape(n, d)
            logits = xf @ router_w + router_b
            vals, idx = jax.lax.top_k(logits, TOPK)
            scores = jax.nn.softmax(vals, axis=-1)
            cap = int(np.floor(n * CAP_FRAC))
            oh = jax.nn.one_hot(idx, E, dtype=jnp.float32)
            pos = jnp.cumsum(jnp.cumsum(oh, axis=0), axis=1).astype(jnp.int32)
            emask = oh * (pos < cap)
            tmask = jnp.sum(emask, axis=-1)
            assign = jnp.einsum('tke,e->tk', emask, jnp.arange(E, dtype=jnp.float32)).astype(jnp.int32)
            m = jnp.max(assign, axis=-1)

            def ff(w1e, w2e, w3e):
                h = jax.nn.gelu(xf @ w2e * (xf @ w1e), approximate=False)
                return h @ w3e
            y_all = jax.vmap(ff)(w1, w2, w3)
            y = y_all[m, jnp.arange(n)]
            slot = jnp.where(tmask[..., None] > 0, y[:, None, :], xf[:, None, :])
            out = jnp.einsum('tkD,tk->tD', slot, scores)
            return out.reshape(b, t, d)
        key = jax.random.key(seed)
        ks = jax.random.split(key, 10)
        w = lambda k, shape: jax.random.normal(k, shape, jnp.float32) * 0.02
        return {'x': jax.random.normal(ks[0], (4, 64, D), jnp.float32), 'g1': jnp.ones((D,), jnp.float32), 'g2': jnp.ones((D,), jnp.float32), 'wq': w(ks[1], (D, HQ * K)), 'wk': w(ks[2], (D, HKV * K)), 'wv': w(ks[3], (D, HKV * V)), 'wo': w(ks[4], (HQ * V, D)), 'router_w': w(ks[5], (D, E)), 'router_b': jnp.zeros((E,), jnp.float32), 'w1': w(ks[6], (E, D, HID)), 'w2': w(ks[7], (E, D, HID)), 'w3': w(ks[8], (E, HID, D))}
    _L0_ffn_in = _L0_ffn_setup()
    _L0_c = _w((lambda *s: np.random.randn(*s).astype(np.float32) * 0.05)(4, 128))
    _L0_wmod = _w((lambda *s: np.random.randn(*s).astype(np.float32) * 0.05)(128, 6 * 128) * 128 ** (-0.5))
    _d = {'L0_attn_x': _L0_attn_in['x'], 'L0_attn_w_qkv': _L0_attn_in['w_qkv'], 'L0_attn_w_proj': _L0_attn_in['w_proj'], 'L0_attn_b_proj': _L0_attn_in['b_proj'], 'L0_ffn_g1': _L0_ffn_in['g1'], 'L0_ffn_g2': _L0_ffn_in['g2'], 'L0_ffn_wq': _L0_ffn_in['wq'], 'L0_ffn_wk': _L0_ffn_in['wk'], 'L0_ffn_wv': _L0_ffn_in['wv'], 'L0_ffn_wo': _L0_ffn_in['wo'], 'L0_ffn_router_w': _L0_ffn_in['router_w'], 'L0_ffn_router_b': _L0_ffn_in['router_b'], 'L0_ffn_w1': _L0_ffn_in['w1'], 'L0_ffn_w2': _L0_ffn_in['w2'], 'L0_ffn_w3': _L0_ffn_in['w3'], 'L0_c': _L0_c, 'L0_wmod': _L0_wmod}
    _x0 = _d['L0_attn_x']
    _d['L0_attn_x'] = jax.random.normal(jax.random.fold_in(jax.random.key(seed), 1), (4, 1024, 128), dtype=_x0.dtype)
    del _x0
    return _d

def reference(L0_attn_x, L0_attn_w_qkv, L0_attn_w_proj, L0_attn_b_proj, L0_ffn_g1, L0_ffn_g2, L0_ffn_wq, L0_ffn_wk, L0_ffn_wv, L0_ffn_wo, L0_ffn_router_w, L0_ffn_router_b, L0_ffn_w1, L0_ffn_w2, L0_ffn_w3, L0_c, L0_wmod):

    def _L0_attn_ref(x, w_qkv, w_proj, b_proj):
        import jax, jax.numpy as jnp
        import numpy as np
        N_HEAD = 16
        HEAD_SIZE = 128
        EMBED = 128
        MULTI_HEAD_SIZE = HEAD_SIZE // N_HEAD
        B, S = (4, 256)
        qkv = jnp.einsum('bse,he->bsh', x, w_qkv)
        q, k, v = jnp.split(qkv, 3, axis=-1)
        scale = 1.0 / np.sqrt(MULTI_HEAD_SIZE).astype(np.float32)
        scores = jnp.einsum('bqh,bkh->bqk', q, k) * scale
        probs = jax.nn.softmax(scores, axis=-1)
        out = jnp.einsum('bqk,bkh->bqh', probs, v)
        Bn, Sn, H = out.shape
        out = jnp.swapaxes(out, 1, 2).reshape(Bn, Sn, H)
        out = jnp.einsum('bsh,eh->bse', out, w_proj) + b_proj
        return out

    def _L0_ffn_ref(x, g1, g2, wq, wk, wv, wo, router_w, router_b, w1, w2, w3):
        import jax, jax.numpy as jnp
        import numpy as np
        D = 128
        HQ = 16
        HKV = 4
        G = HQ // HKV
        K = 64
        V = 64
        E = 8
        TOPK = 2
        HID = 256
        CAP_FRAC = 0.125
        EPS = 1e-06

        def _rmsnorm(x, g):
            return x * jax.lax.rsqrt(jnp.mean(x * x, axis=-1, keepdims=True) + EPS) * g

        def _rotary_tables(t, dim):
            thetas = 10000.0 ** (-np.arange(0, dim, 2, dtype=np.float32) / dim)
            ticks = np.outer(np.arange(t, dtype=np.float32), thetas)
            ticks = np.tile(ticks, (1, 2))[None, :, None, :]
            return (jnp.asarray(np.cos(ticks)), jnp.asarray(np.sin(ticks)))

        def _neg_half(x):
            x1, x2 = jnp.split(x, 2, axis=-1)
            return jnp.concatenate([-x2, x1], axis=-1)

        def _attention(x, wq, wk, wv, wo):
            b, t, _ = x.shape
            q = (x @ wq).reshape(b, t, HQ, K)
            k = (x @ wk).reshape(b, t, HKV, K)
            v = (x @ wv).reshape(b, t, HKV, V)
            cos, sin = _rotary_tables(t, K)
            q = q * cos + _neg_half(q) * sin
            k = k * cos + _neg_half(k) * sin
            qg = q.reshape(b, t, G, HKV, K)
            scores = jnp.einsum('btghk,bThk->bghtT', qg, k)
            mask = jnp.tril(jnp.ones((t, t), bool))
            scores = jnp.where(mask, scores, -jnp.inf) / np.float32(np.sqrt(K))
            p = jax.nn.softmax(scores, axis=-1)
            out = jnp.einsum('bghtT,bThv->btghv', p, v).reshape(b, t, HQ * V)
            return out @ wo

        def _moe(x, router_w, router_b, w1, w2, w3):
            b, t, d = x.shape
            n = b * t
            xf = x.reshape(n, d)
            logits = xf @ router_w + router_b
            vals, idx = jax.lax.top_k(logits, TOPK)
            scores = jax.nn.softmax(vals, axis=-1)
            cap = int(np.floor(n * CAP_FRAC))
            oh = jax.nn.one_hot(idx, E, dtype=jnp.float32)
            pos = jnp.cumsum(jnp.cumsum(oh, axis=0), axis=1).astype(jnp.int32)
            emask = oh * (pos < cap)
            tmask = jnp.sum(emask, axis=-1)
            assign = jnp.einsum('tke,e->tk', emask, jnp.arange(E, dtype=jnp.float32)).astype(jnp.int32)
            m = jnp.max(assign, axis=-1)

            def ff(w1e, w2e, w3e):
                h = jax.nn.gelu(xf @ w2e * (xf @ w1e), approximate=False)
                return h @ w3e
            y_all = jax.vmap(ff)(w1, w2, w3)
            y = y_all[m, jnp.arange(n)]
            slot = jnp.where(tmask[..., None] > 0, y[:, None, :], xf[:, None, :])
            out = jnp.einsum('tkD,tk->tD', slot, scores)
            return out.reshape(b, t, d)
        h = x + _attention(_rmsnorm(x, g1), wq, wk, wv, wo)
        return h + _moe(_rmsnorm(h, g2), router_w, router_b, w1, w2, w3)
    x = L0_attn_x
    mod = (_silu(L0_c) @ L0_wmod).reshape(L0_c.shape[0], 6, 1, -1)
    sa, ca, ga, sb, cb, gb = (mod[:, 0], mod[:, 1], mod[:, 2], mod[:, 3], mod[:, 4], mod[:, 5])
    ga = (2 * (ga >= 0) - 1) * jnp.maximum(jnp.abs(ga), 0.25)
    gb = (2 * (gb >= 0) - 1) * jnp.maximum(jnp.abs(gb), 0.25)
    h = _layernorm(x, axis=-1) * (1 + ca) + sa
    x = x + ga * _L0_attn_ref(h, L0_attn_w_qkv, L0_attn_w_proj, L0_attn_b_proj)
    h = _layernorm(x, axis=-1) * (1 + cb) + sb
    x = x + gb * _L0_ffn_ref(h, L0_ffn_g1, L0_ffn_g2, L0_ffn_wq, L0_ffn_wk, L0_ffn_wv, L0_ffn_wo, L0_ffn_router_w, L0_ffn_router_b, L0_ffn_w1, L0_ffn_w2, L0_ffn_w3)
    return x

_drawn_inputs = setup_inputs


def setup_inputs(seed=0):
    import zlib

    import numpy as np

    out = dict(_drawn_inputs(seed))
    spreads = {'L0_ffn_g1': (1.0, 0.6), 'L0_ffn_g2': (1.0, 0.2), 'L0_ffn_router_b': (0.0, 0.1)}
    factors = {'L0_attn_w_qkv': 8.0,
     'L0_attn_w_proj': 8.0,
     'L0_attn_b_proj': 5.668,
     'L0_ffn_wq': 8.0,
     'L0_ffn_wk': 8.0,
     'L0_ffn_wv': 5.471,
     'L0_ffn_wo': 4.919,
     'L0_ffn_w1': 8.0,
     'L0_ffn_w2': 8.0,
     'L0_ffn_w3': 8.0}
    for name, (base, spread) in spreads.items():
        noise = np.random.default_rng([zlib.crc32(name.encode()), seed]).standard_normal(out[name].shape)
        drawn = base * np.exp(spread * noise) if base else spread * noise
        out[name] = jnp.asarray(drawn.astype(out[name].dtype))
    for name, factor in factors.items():
        out[name] = (out[name] * factor).astype(out[name].dtype)
    return out
```

```python
from contextlib import ExitStack

import numpy as np

import concourse.bass as bass
from concourse import mybir

F32 = mybir.dt.float32
F16 = mybir.dt.float16
BF16 = mybir.dt.bfloat16
I32 = mybir.dt.int32
U32 = mybir.dt.uint32
ALU = mybir.AluOpType
ACT = mybir.ActivationFunctionType
AX = mybir.AxisListType

P = 128
B, S, D = 4, 1024, 128
NT = S // P
HKV, G, HD = 4, 4, 64
E, HID = 8, 256
TOPK = 2
CAP = B * S // 8
NTOK = B * S
NTT = NTOK // P
WQK = 2 * 2 * P + 2 * HD + HD
W_K = 4 * P
W_V = W_K + 2 * HD
SLOTS = 8
ETILES = 40
ROUNDS = ETILES // SLOTS
WE = 2 * HID + 2 * D
LN_EPS, RMS_EPS = 1e-5, 1e-6
A_SCALE = float(1.0 / np.sqrt(8.0).astype(np.float32))
ORDER = [7, 0, 6, 1, 5, 2, 4, 3]


class Steps:

    def __init__(self, widths):
        self.width = widths
        self.chunks = []
        self.first = []
        for s, w in enumerate(widths):
            self.first.append(len(self.chunks))
            for lo in range(0, w, 4):
                self.chunks.append((s, lo, min(4, w - lo)))
        self.first.append(len(self.chunks))
        self.n = len(widths)
        self.nchunks = len(self.chunks)

    def emptied(self, c, bank):
        return (c + 1 - bank) // 2


def build(nc, x, cT, wmod, w_qkvT, w_projT, b_proj, g1, g2, w_kv, w_o, router_w, router_b, w_exp, consts,
          cos_t, sin_t, consts8, consts16, out):
    ctx = ExitStack()
    with ctx:
        def sb(name, shape, dt=F32):
            return ctx.enter_context(nc.sbuf_tensor(name, shape, dt))

        def sem(name):
            return ctx.enter_context(nc.semaphore(name))

        rows_in = nc.dram_tensor("rows_in", [ETILES * P, D], F32).ap()
        rows_out = nc.dram_tensor("rows_out", [ETILES * P, D], F32).ap()

        psS = ctx.enter_context(nc.psum_tensor("psS", [P, 2, 1024], F32))
        psT = ctx.enter_context(nc.psum_tensor("psT", [P, 2, 512], F32))
        psO = ctx.enter_context(nc.psum_tensor("psO", [P, 2, 512], F32))
        psTf = psT[:, :, :].rearrange("p a b -> p (a b)")

        cst = sb("cst", [P, 3 * P + 8])
        ident, maskf = cst[:, 0:P], cst[:, P:2 * P]
        mhalf, iota8 = cst[:, 2 * P:2 * P + 8], cst[:, 3 * P:3 * P + 8]
        c8 = sb("c8", [8, 8 + 32 + ETILES + 1])
        lower8, k128, tile_no, ones8 = c8[:, 0:8], c8[:, 8:40], c8[:, 40:40 + ETILES], c8[:, 40 + ETILES:41 + ETILES]
        c16 = sb("c16", [16, 16])
        trig = sb("trig", [P, 4, S])
        cosb = trig[:, 0:2, :]
        sinb = trig[:, 2:4, :]
        identh = sb("identh", [P, P], BF16)
        maskh = sb("maskh", [P, P], BF16)
        ones16 = sb("ones16", [16, S])
        gb1 = sb("gb1", [P, D])
        gb2 = sb("gb2", [P, D])
        bpb = sb("bpb", [P, D])
        rbb = sb("rbb", [P, E])
        wqkv = sb("wqkv", [P, 3 * D])
        wproj = sb("wproj", [P, D])
        wo = sb("wo", [P, 2 * D])
        rw = sb("rw", [P, E])
        wm = sb("wm", [P, 6 * D])
        cs = sb("cs", [P, B])
        ce = sb("ce", [P, B])
        scB = sb("scB", [P, B, P])
        mod = sb("mod", [P, B, 6 * D])

        x_nat = sb("x_nat", [P, NT, D])
        x_row = sb("x_row", [P, NT, D])
        wk1 = sb("wk1", [P, NT, D])
        wk2 = sb("wk2", [P, NT, D])
        gneg = wk1[:, 0:B, :]
        st = sb("st", [P, 4, NT])
        rstd = sb("rstd", [P, NT])
        hT = sb("hT", [P, S])
        qkv = sb("qkv", [P, 3, S])
        qT, kT = qkv[:, 0, :], qkv[:, 1, :]
        va = qkv[:, 2, :].rearrange("p (j d) -> p j d", j=NT)
        prob = sb("prob", [P, 3, S])
        probT = sb("probT", [P, 3, S])
        nmax = sb("nmax", [P, 4])
        nmaxs = sb("nmaxs", [P, 4])
        sums = sb("sums", [P, G * NT])
        rsum = sb("rsum", [P, G * NT])
        Oj = sb("Oj", [P, 2, D])
        wkv = sb("wkv", [P, WQK])
        qs = sb("qs", [P, G, S], F16)
        kA = sb("kA", [P, S], F16)
        kB = sb("kB", [P, S], F16)
        vb = sb("vb", [P, NT, HD])
        rp = sb("rp", [P, 4, S])
        rp1, rp2 = rp[:, 0:2, :], rp[:, 2:4, :]
        att = sb("att", [P, NT, G * HD])
        x1 = sb("x1", [P, B, NT, D])
        hres = sb("hres", [P, B, NT, D])
        hf = sb("hf", [P, B, NT, D])
        expert = sb("expert", [P, B, NT])
        wy = sb("wy", [P, B, NT])
        wx = sb("wx", [P, B, NT])
        lg = sb("lg", [P, NT, E])
        v8 = sb("v8", [P, NT, 8])
        ix = sb("ix", [P, NT, 8], U32)
        ixf = sb("ixf", [P, NT * TOPK])
        oh = sb("oh", [P, NT * TOPK, E])
        em = sb("em", [P, NT * TOPK, E])
        ea = sb("ea", [P, NT * TOPK, E])
        ohT = sb("ohT", [16, S])
        cum = sb("cum", [16, 1 + S])
        sc = sb("sc", [P, NT, TOPK])
        tk = sb("tk", [P, NT * TOPK])
        asg = sb("asg", [P, NT, TOPK])
        asg2 = sb("asg2", [P, NT * TOPK])[:, :]
        chosen = sb("chosen", [P, 3, NT])
        sm1 = sb("sm1", [P, NT])
        sm2 = sb("sm2", [P, NT])
        ohm = sb("ohm", [P, NTT, E])
        ohmT = trig[0:8, :, :].rearrange("e a t -> e (a t)")
        rank = rp[0:8, :, :].rearrange("e a t -> e (a t)")
        few = sb("few", [8, 32])
        ntile = sb("ntile", [8, 1])
        base = sb("base", [8, 1])
        tend = sb("tend", [8, 1])
        past = sb("past", [8, ETILES])
        slot = sb("slot", [P, NTT], U32)
        texp = sb("texp", [1, ETILES], I32)
        wexp = qkv[:, :, :].rearrange("p a b -> p (a b)").rearrange("p (k n) -> p k n", k=SLOTS // 2)

        const_in, mod_e, mod_lhs, mod_mm, mod_cp, vec = (sem("const_in"), sem("mod_e"), sem("mod_lhs"),
                                                         sem("mod_mm"), sem("mod_cp"), sem("vec"))
        xnat_in, xrow_in, x_free = sem("xnat_in"), sem("xrow_in"), sem("x_free")
        var_ready, rstd_ready = sem("var_ready"), sem("rstd_ready")
        tok_ready, tok_t, tok_T = sem("tok_ready"), sem("tok_t"), sem("tok_T")
        a_qkv, a_qkv_cp = sem("a_qkv"), sem("a_qkv_cp")
        a_proj, a_proj_used = sem("a_proj"), sem("a_proj_used")
        wo_in, wkv_in, wkv_used = sem("wo_in"), sem("wkv_in"), sem("wkv_used")
        r_k, r_v, r_q = sem("r_k"), sem("r_v"), sem("r_q")
        r_prod, r_sum, r_hi, r_ready, v_ready = sem("r_prod"), sem("r_sum"), sem("r_hi"), sem("r_ready"), sem("v_ready")
        o_norm, o_t, o_T, o_T2, o_mm, o_add = (sem("o_norm"), sem("o_t"), sem("o_T"), sem("o_T2"), sem("o_mm"), sem("o_add"))
        rt_lg, rt_mm, rt_d, rt_e, rt_oh, rt_ohT, rt_ohTc, rt_cum, rt_pos = (sem("rt_lg"), sem("rt_mm"), sem("rt_d"), sem("rt_e"), sem("rt_oh"), sem("rt_ohT"),
                                                            sem("rt_ohTc"), sem("rt_cum"), sem("rt_pos"))
        vecb, veck, vecr, vece = sem("vecb"), sem("veck"), sem("vecr"), sem("vece")

        class Att:
            def __init__(self, n):
                self.S, self.M, self.E, self.T, self.TA, self.TV, self.PV = (sem(f"{n}_{w}") for w in (
                    "scores", "max", "exp", "turned", "turned_act", "turned_vec", "pv"))
        attA, attB = Att("a"), Att("b")
        a_onorm, rsum_ready, plan, final = sem("a_onorm"), sem("rsum_ready"), sem("plan"), sem("final")
        e_z, e_oh, e_ohT, e_ohTc, e_nt, e_base, e_slotm, e_slot, e_past, e_te, e_plan = (sem(n) for n in (
            "e_z", "e_oh", "e_ohT", "e_ohTc", "e_nt", "e_base", "e_slotm", "e_slot", "e_past", "e_te", "e_plan"))
        scat, w_in0, w_in1, xs_in0, xs_in1 = sem("scat"), sem("w_in0"), sem("w_in1"), sem("xs_in0"), sem("xs_in1")
        m_xT, m_xTc, m_ab, m_a, m_u, m_h, m_hT, m_hTc, m_y, m_yc, m_wfree, m_out0, m_out1 = (sem(n) for n in (
            "m_xT", "m_xTc", "m_ab", "m_a", "m_u", "m_h", "m_hT", "m_hTc", "m_y", "m_yc", "m_wfree", "m_out0", "m_out1"))
        gath, fin, out_done, zero_in = sem("gath"), sem("fin"), sem("out_done"), sem("zero_in")

        stepsA = Steps([NT] * NT)
        stepsB = Steps([i + 1 for _ in range(G) for i in ORDER])
        aT = rp1
        hfT = hT

        NCONST = 14
        block = ctx.enter_context(nc.Block())

        def bc_mod(b, k):
            return mod[:, b, k * D:(k + 1) * D].unsqueeze(1).to_broadcast([P, NT, D])

        def bc_tok(stat):
            return stat.unsqueeze(2).to_broadcast([P, NT, D])

        def bc_row(v):
            return v.unsqueeze(1).to_broadcast([P, NT, D])

        def m_w(k):
            return (wexp[:, k, :] if k < 4 else wexp_hi[:, k - 4, :])

        wexp_hi = prob[:, :, :].rearrange("p a b -> p (a b)")[:, 0:3 * S].rearrange("p (k n) -> p k n", k=4)
        assert 4 * WE == 3 * S

        def m_xs(k):
            return probT[:, 0, k * P:(k + 1) * P]

        m_xTs = probT[:, 1, 0:512].rearrange("p (k t) -> p k t", k=4)
        m_av = rp2[:, 0, :].rearrange("p (k n) -> p k n", k=4)
        m_uv = rp2[:, 1, :].rearrange("p (k n) -> p k n", k=4)
        m_hv = rp1[:, 0, :].rearrange("p (k n) -> p k n", k=4)
        m_hTs = rp1[:, 1, :].rearrange("p (k c t) -> p k c t", k=4, c=2)
        m_yv = att[:, 0:4, :].rearrange("p a b -> p (a b)").rearrange("p (k n) -> p k n", k=8)
        yg = [x_nat, x_row, wk1, wk2]

        def psE(k):
            return psS[:, k // 2, (k % 2) * 512:(k % 2) * 512 + 512]

        @block.sync
        def _(sp):
            def load_x(b):
                sp.dma_start(x_nat[:, :, :], x[b].rearrange("(j p) e -> p j e", p=P)).then_inc(xnat_in, 16)
                sp.dma_start(x_row[:, :, :], x[b].rearrange("(p j) e -> p j e", p=P)).then_inc(xrow_in, 16)

            load_x(0)
            n = 0
            for dst, src in ((cst[:, :], consts), (cs[:, :], cT), (wm[:, :], wmod), (wqkv[:, :], w_qkvT),
                             (wproj[:, :], w_projT), (bpb[:, :], b_proj.partition_broadcast(P)),
                             (gb1[:, :], g1.partition_broadcast(P)), (gb2[:, :], g2.partition_broadcast(P)),
                             (rbb[:, :], router_b.partition_broadcast(P)), (rw[:, :], router_w),
                             (cosb[:, :, :], cos_t), (sinb[:, :, :], sin_t), (c8[:, :], consts8), (c16[:, :], consts16)):
                sp.dma_start(dst, src).then_inc(const_in, 16)
                n += 1
            assert n == NCONST
            sp.dma_start(wkv[:, :], w_kv[0]).then_inc(wkv_in, 16)
            sp.dma_start(wo[:, :], w_o[0]).then_inc(wo_in, 16)

            def next_heads(b):
                with sp.Fori(0, HKV) as kv:
                    sp.wait_ge(wkv_used, b * HKV + kv + 1)
                    sp.dma_start(wkv[:, :], w_kv[kv + 1]).then_inc(wkv_in, 16)
                    sp.wait_ge(o_mm, b * HKV + kv + 1)
                    sp.dma_start(wo[:, :], w_o[kv + 1]).then_inc(wo_in, 16)

            with sp.Fori(0, B - 1) as b:
                sp.wait_ge(x_free, b + 1)
                load_x(b + 1)
                next_heads(b)
            next_heads(B - 1)

            sp.wait_ge(wkv_in, 16 * (B * HKV + 1))
            sp.wait_ge(wo_in, 16 * (B * HKV + 1))
            sp.wait_ge(e_plan, 1)
            sp.wait_ge(scat, 16 * NTT)

            def load_tile(k, u, half):
                e = sp.value_load(texp[0:1, bass.ds(u, 1)], min_val=0, max_val=E - 1)
                sp.dma_start(m_w(k), w_exp[bass.ds(e, 1)].rearrange("o p n -> (o p) n")).then_inc((w_in0, w_in1)[half], 16)
                sp.dma_start(m_xs(k), rows_in[bass.ds(u * P, P), :]).then_inc((xs_in0, xs_in1)[half], 16)

            for k in range(SLOTS):
                load_tile(k, k, k // 4)
            with sp.Fori(0, ROUNDS - 1) as r:
                for half in range(2):
                    sp.wait_ge(m_wfree, r * 2 + half + 1)
                    for k in range(4 * half, 4 * half + 4):
                        load_tile(k, (r + 1) * SLOTS + k, half)
            for b in range(B):
                sp.wait_ge(fin, b + 1)
                sp.dma_start(out[b].rearrange("(p j) e -> p j e", p=P), yg[b][:, :, :]).then_inc(out_done, 16)
            sp.wait_ge(out_done, 16 * B)

        @block.gpsimd
        def _(pool):
            pool.memset(ones16[:, :], 1.0).then_inc(e_z, 1)
            pool.memset(scB[:, :, :], 0.0).then_inc(e_z, 1)
            pool.wait_ge(e_z, 2)
            pool.memset(x1[:, :, :, :], 0.0).then_inc(e_z, 1)
            pool.wait_ge(e_z, 3)
            z = x1[:, :, :, :].rearrange("p b j d -> p (b j) d")
            pool.dma_start(rows_in[0:NTOK, :].rearrange("(t p) d -> p t d", p=P), z).then_inc(zero_in, 16)
            pool.dma_start(rows_in[NTOK:ETILES * P, :].rearrange("(t p) d -> p t d", p=P), z[:, 0:ETILES - NTT, :]
                           ).then_inc(zero_in, 16)
            pool.wait_ge(const_in, 16 * NCONST)

            def power(n):
                pool.wait_ge(var_ready, n)
                pool.tensor_tensor(rstd[:, :], st[:, 3, :], mhalf, ALU.pow).then_inc(rstd_ready, 1)

            with pool.Fori(0, B) as b:
                power(4 * b + 1)
                power(4 * b + 2)
                power(4 * b + 3)
                with pool.Fori(0, HKV) as kv:
                    it = b * HKV + kv
                    for c in range(3):
                        rows = HD if c == 0 else P
                        pool.wait_ge(r_prod, it * 3 + c + 1)
                        pool.tensor_tensor(rp1[0:rows, c % 2, :], rp1[0:rows, c % 2, :], rp2[0:rows, c % 2, :],
                                           ALU.add).then_inc(r_sum, 1)
                power(4 * b + 4)

            pool.wait_ge(e_slot, 2)
            pool.wait_ge(zero_in, 32)
            hff = hf[:, :, :, :].rearrange("p b j d -> p (b j) d")
            for t in range(NTT):
                pool.indirect_dma_start(rows_in, bass.IndirectOffsetOnAxis(slot[:, t:t + 1], 0), hff[:, t, :], None
                                        ).then_inc(scat, 16)
            with pool.Fori(0, ROUNDS) as rr:
                for h in range(2):
                    pool.wait_ge(m_yc, 2 * rr + h + 1)
                    pool.dma_start(rows_out[bass.ds((2 * rr + h) * 4 * P, 4 * P), :].rearrange("(k p) d -> p k d", p=P),
                                   m_yv[:, 4 * h:4 * h + 4, :]).then_inc((m_out0, m_out1)[h], 16)
            for h in range(2):
                pool.wait_ge((m_out0, m_out1)[h], 16 * ROUNDS)
            for t in range(NTT):
                pool.indirect_dma_start(yg[t // NT][:, t % NT, :], None, rows_out,
                                        bass.IndirectOffsetOnAxis(slot[:, t:t + 1], 0)).then_inc(gath, 16)

        @block.scalar
        def _(act):
            def attend(s, a, it, scale):
                def turned(st_, c):
                    sx, lo, n = s.chunks[c]
                    act.wait_ge(a.T, it * s.nchunks + c + 1)
                    act.activation(probT[:, sx % 3, lo * P:(lo + n) * P], psT[:, 0, 0:n * P], ACT.Copy).then_inc(a.TA, 1)

                done = 0
                for k in range(s.n + 2):
                    if k < s.n:
                        act.wait_ge(a.M, it * s.n + k + 1)
                        w = s.width[k] * P
                        act.activation(prob[:, k % 3, 0:w], psS[:, k % 2, 0:w], ACT.Exp,
                                       bias=(nmax if scale == 1.0 else nmaxs)[:, k % 4:k % 4 + 1], scale=scale,
                                       accum_out=sums[:, k:k + 1]).then_inc(a.E, 1)
                    if k >= 2:
                        for c in range(s.first[k - 2], s.first[k - 1]):
                            if c % 2 == 0:
                                turned(k - 2, c)

            act.wait_ge(const_in, 16 * NCONST)
            act.activation(ce[:, :], cs[:, :], ACT.Exp, scale=-1.0).then_inc(mod_e, 1)

            def to_features(n, dst, row):
                act.wait_ge(tok_t, n)
                if row:
                    act.activation(dst[:, :].rearrange("d (p j) -> d j p", j=NT),
                                   psS[:, 0, :].rearrange("d (j p) -> d j p", p=P), ACT.Copy).then_inc(tok_T, 1)
                else:
                    act.activation(dst[:, :], psS[:, 0, :], ACT.Copy).then_inc(tok_T, 1)

            with act.Fori(0, B) as b:
                to_features(3 * b + 1, hT, False)
                act.wait_ge(a_qkv, 3 * b + 1)
                act.activation(qT[:, :], psS[:, 1, :], ACT.Copy).then_inc(a_qkv_cp, 1)
                act.wait_ge(a_qkv, 3 * b + 2)
                act.activation(kT[:, :], psS[:, 0, :], ACT.Copy).then_inc(a_qkv_cp, 1)
                act.wait_ge(a_qkv, 3 * b + 3)
                act.activation(va[:, :, :].rearrange("p j d -> p (j d)"), psTf, ACT.Copy).then_inc(a_qkv_cp, 1)
                attend(stepsA, attA, b, A_SCALE)
                to_features(3 * b + 2, hT, True)
                with act.Fori(0, HKV) as kv:
                    it = b * HKV + kv
                    for c in range(3):
                        act.wait_ge(r_sum, it * 3 + c + 1)
                        src = rp1[:, c % 2, :]
                        if c == 0:
                            act.activation(kA[0:HD, :], src[0:HD, :], ACT.Copy).then_inc(r_hi, 1)
                            act.wait_ge(r_v, it + 1)
                            act.activation(vb[:, :, :].rearrange("p j d -> p (j d)"), psO[:, 0, :], ACT.Copy).then_inc(v_ready, 1)
                        else:
                            g = 2 * (c - 1)
                            act.activation(qs[0:HD, g, :], src[0:HD, :], ACT.Copy)
                            act.activation(qs[HD:P, g + 1, :], src[HD:P, :], ACT.Copy).then_inc(r_hi, 1)
                    attend(stepsB, attB, it, 1.0)
                    act.wait_ge(o_t, 2 * it + 1)
                    act.activation(aT[:, 0, :], psS[:, 0, :], ACT.Copy).then_inc(o_T, 1)
                to_features(3 * b + 3, hfT, False)
                act.wait_ge(rt_d, b + 1)
                act.activation(sm2[:, :], sm1[:, :], ACT.Exp).then_inc(rt_e, 1)
                act.wait_ge(rt_ohT, b + 1)
                act.activation(ohT[:, :].rearrange("r (p j) -> r j p", j=NT),
                               psS[0:16, 1, :].rearrange("r (j p) -> r j p", p=P), ACT.Copy).then_inc(rt_ohTc, 1)

            for b in range(B):
                act.wait_ge(e_ohT, b + 1)
                act.activation(ohmT[:, b * S:(b + 1) * S], psS[0:8, b % 2, :], ACT.Copy).then_inc(e_ohTc, 1)

            with act.Fori(0, ROUNDS * 2) as r:
                act.wait_ge(m_xT, r + 1)
                act.activation(m_xTs.rearrange("p k t -> p (k t)"), psO[:, 0, :], ACT.Copy).then_inc(m_xTc, 1)
                for k in range(4):
                    act.wait_ge(m_ab, r * 4 + k + 1)
                    act.activation(m_av[:, k, :], psE(k)[:, 0:HID], ACT.Copy).then_inc(m_a, 1)
                for k in range(4):
                    act.wait_ge(m_u, r * 4 + k + 1)
                    act.activation(m_hv[:, k, :], m_uv[:, k, :], ACT.Gelu).then_inc(m_h, 1)

        @block.tensor
        def _(pe):
            def attend(s, a, it, scores, values):
                def turn(k):
                    pe.wait_ge(a.E, it * s.n + k + 1)
                    for c in range(s.first[k], s.first[k + 1]):
                        _, lo, n = s.chunks[c]
                        if c >= 2:
                            half = s.emptied(c, c % 2)
                            cnt = s.emptied(s.nchunks, c % 2)
                            pe.wait_ge((a.TA, a.TV)[c % 2], it * cnt + half)
                        for j in range(n):
                            last = pe.transpose(psT[:, c % 2, j * P:(j + 1) * P],
                                                prob[:, k % 3, (lo + j) * P:(lo + j + 1) * P], ident)
                        last.then_inc(a.T, 1)

                def pv(k):
                    cl = s.first[k + 1]
                    for q in range(2):
                        cnt = s.emptied(s.nchunks, q)
                        n = s.emptied(cl, q)
                        if n:
                            pe.wait_ge((a.TA, a.TV)[q], it * cnt + n)
                    values(k)

                for k in range(s.n + 3):
                    if k < s.n:
                        if k >= 2:
                            pe.wait_ge(a.E, it * s.n + k - 1)
                        scores(k).then_inc(a.S, 1)
                    if 2 <= k < s.n + 2:
                        turn(k - 2)
                    if k >= 3:
                        pv(k - 3)

            pe.wait_ge(const_in, 16 * NCONST)
            for b in range(B):
                pe.wait_ge(mod_lhs, b + 1)
                if b >= 2:
                    pe.wait_ge(mod_cp, b - 1)
                for h in range(2):
                    mm = pe.matmul(psS[:, b % 2, h * 512:h * 512 + 3 * D], scB[:, b, :], wm[:, h * 3 * D:(h + 1) * 3 * D],
                                   start=True, stop=True)
                mm.then_inc(mod_mm, 1)

            def turn_tokens(n, src):
                pe.wait_ge(tok_ready, n)
                for j in range(NT):
                    last = pe.transpose(psS[:, 0, j * P:(j + 1) * P], src(j), ident)
                last.then_inc(tok_t, 1)

            with pe.Fori(0, B) as b:
                turn_tokens(3 * b + 1, lambda j: wk2[:, j, :])
                pe.wait_ge(tok_T, 3 * b + 1)
                for k, dst in ((0, psS[:, 1, :]), (1, psS[:, 0, :])):
                    for h in range(2):
                        mm = pe.matmul(dst[:, h * 512:(h + 1) * 512], wqkv[:, k * D:(k + 1) * D], hT[:, h * 512:(h + 1) * 512],
                                       start=True, stop=True)
                    mm.then_inc(a_qkv, 1)
                for j in range(NT):
                    mm = pe.matmul(psTf[:, j * P:(j + 1) * P], hT[:, j * P:(j + 1) * P], wqkv[:, 2 * D:3 * D], start=True, stop=True)
                mm.then_inc(a_qkv, 1)
                pe.wait_ge(a_qkv_cp, 3 * b + 3)

                def scoresA(i):
                    for h in range(2):
                        mm = pe.matmul(psS[:, i % 2, h * 512:(h + 1) * 512], qT[:, i * P:(i + 1) * P],
                                       kT[:, h * 512:(h + 1) * 512], start=True, stop=True)
                    return mm

                def projA(i):
                    pe.wait_ge(a_onorm, b * NT + i + 1)
                    pe.matmul(psO[:, i % 2, 256:256 + D], Oj[:, i % 2, :], wproj[:, :], start=True, stop=True).then_inc(a_proj, 1)

                def valuesA(i):
                    if i >= 2:
                        pe.wait_ge(a_proj_used, b * NT + i - 1)
                    for j in range(NT):
                        mm = pe.matmul(psO[:, i % 2, 0:D], probT[:, i % 3, j * P:(j + 1) * P], va[:, j, :],
                                       start=(j == 0), stop=(j == NT - 1))
                    mm.then_inc(attA.PV, 1)
                    if i >= 1:
                        projA(i - 1)

                attend(stepsA, attA, b, scoresA, valuesA)
                projA(NT - 1)

                turn_tokens(3 * b + 2, lambda j: wk2[:, j, :])
                with pe.Fori(0, HKV) as kv:
                    it = b * HKV + kv
                    pe.wait_ge(tok_T, 3 * b + 2)
                    pe.wait_ge(wkv_in, 16 * it + 16)
                    for h in range(2):
                        mm = pe.matmul(psT[:, h, :], wkv[:, W_K:W_K + P], hT[:, h * 512:(h + 1) * 512], start=True, stop=True)
                    mm.then_inc(r_k, 1)
                    for j in range(NT):
                        mm = pe.matmul(psO[:, 0, j * HD:(j + 1) * HD], hT[:, j * P:(j + 1) * P], wkv[:, W_V:W_V + HD],
                                       start=True, stop=True)
                    mm.then_inc(r_v, 1)
                    for c in range(2):
                        if c == 1:
                            pe.wait_ge(r_prod, it * 3 + 2)
                        for k in range(2):
                            for h in range(2):
                                w0 = (2 * c + k) * P
                                mm = pe.matmul(psS[:, k, h * 512:(h + 1) * 512], wkv[:, w0:w0 + P], hT[:, h * 512:(h + 1) * 512],
                                               start=True, stop=True)
                        mm.then_inc(r_q, 1)
                    pe.wait_ge(r_q, 2 * it + 2)
                    pe.sem_inc(wkv_used, 1)
                    pe.wait_ge(r_ready, it + 1)
                    pe.wait_ge(v_ready, it + 1)

                    def scoresB(k):
                        g, i = k // NT, ORDER[k % NT]
                        for h in range((i + 4) // 4):
                            n = min(4, i + 1 - 4 * h)
                            dst = psS[:, k % 2, h * 512:h * 512 + n * P]
                            diag = h == i // 4
                            pe.matmul(dst, qs[:, g, i * P:(i + 1) * P], kA[:, h * 512:h * 512 + n * P], start=True, stop=False)
                            mm = pe.matmul(dst, qs[:, g, i * P:(i + 1) * P], kB[:, h * 512:h * 512 + n * P], start=False, stop=not diag)
                            if diag:
                                d0 = i * P
                                mm = pe.matmul(psS[:, k % 2, d0:d0 + P], identh[:, :], maskh[:, :], start=False, stop=True)
                        return mm

                    def valuesB(k):
                        g, i = k // NT, ORDER[k % NT]
                        if k % NT == 0 and g >= 2:
                            pe.wait_ge(o_norm, it * G + g - 1)
                        for j in range(i + 1):
                            mm = pe.matmul(psO[:, g % 2, i * HD:(i + 1) * HD], probT[:, k % 3, j * P:(j + 1) * P], vb[:, j, :],
                                           start=(j == 0), stop=(j == i))
                        mm.then_inc(attB.PV, 1)

                    attend(stepsB, attB, it, scoresB, valuesB)
                    pe.wait_ge(o_norm, it * G + G)
                    for c in range(2):
                        for i in range(NT):
                            last = pe.transpose(psS[:, c, i * P:(i + 1) * P], att[:, i, c * P:(c + 1) * P], ident)
                        last.then_inc(o_t, 1)
                    pe.wait_ge(o_T, it + 1)
                    pe.wait_ge(o_T2, it + 1)
                    pe.wait_ge(wo_in, 16 * it + 16)
                    for j in range(NT):
                        for c in range(2):
                            mm = pe.matmul(psS[:, 0, j * D:(j + 1) * D],
                                           aT[:, c, :].rearrange("f (p j) -> f j p", j=NT)[:, j, :],
                                           wo[:, c * D:(c + 1) * D], start=(c == 0), stop=(c == 1))
                    mm.then_inc(o_mm, 1)
                    pe.wait_ge(o_add, it + 1)

                turn_tokens(3 * b + 3, lambda j: wk2[:, j, :])
                pe.wait_ge(tok_T, 3 * b + 3)
                for j in range(NT):
                    mm = pe.matmul(psT[:, 0, j * E:(j + 1) * E], hfT[:, j * P:(j + 1) * P], rw[:, :], start=True, stop=True)
                mm.then_inc(rt_mm, 1)
                pe.wait_ge(rt_oh, b + 1)
                for j in range(NT):
                    last = pe.transpose(psS[0:16, 1, j * P:(j + 1) * P],
                                        oh[:, j * TOPK:(j + 1) * TOPK, :].rearrange("p k e -> p (k e)"), ident)
                last.then_inc(rt_ohT, 1)
                pe.wait_ge(rt_cum, b + 1)
                for j in range(NT):
                    mm = pe.matmul(psT[:, 1, j * 16:(j + 1) * 16],
                                   cum[:, 1:1 + S].rearrange("r (p j) -> r j p", j=NT)[:, j, :], c16[:, :], start=True, stop=True)
                mm.then_inc(rt_pos, 1)

            pe.wait_ge(e_oh, 1)
            for b in range(B):
                if b >= 2:
                    pe.wait_ge(e_ohTc, b - 1)
                for j in range(NT):
                    last = pe.transpose(psS[0:8, b % 2, j * P:(j + 1) * P], ohm[:, b * NT + j, :], ident)
                last.then_inc(e_ohT, 1)
            pe.wait_ge(e_nt, 1)
            pe.matmul(psO[0:8, 0, 0:1], lower8, ntile[:, :], start=True, stop=True).then_inc(e_base, 1)
            pe.wait_ge(e_slotm, 1)
            for t in range(NTT):
                mm = pe.matmul(psO[:, 1, t:t + 1], ohmT[:, t * P:(t + 1) * P], ones8, start=True, stop=True)
            mm.then_inc(e_slot, 1)
            pe.wait_ge(e_past, 1)
            pe.matmul(psO[0:1, 0, 64:64 + ETILES], ones8, past[:, :], start=True, stop=True).then_inc(e_te, 1)
            pe.wait_ge(e_plan, 1)

            def group(r, half, w_in, xs_in, rr):
                pe.wait_ge(xs_in, 64 * rr + 64)
                for k in range(4):
                    last = pe.transpose(psO[:, 0, k * P:(k + 1) * P], m_xs(4 * half + k), ident)
                last.then_inc(m_xT, 1)
                pe.wait_ge(m_xTc, r + 1)
                pe.wait_ge(w_in, 64 * rr + 64)
                for k in range(4):
                    pe.matmul(psE(k), m_xTs[:, k, :], m_w(4 * half + k)[:, 0:2 * HID], start=True, stop=True).then_inc(m_ab, 1)
                for k in range(4):
                    pe.wait_ge(m_h, r * 4 + k + 1)
                    for c in range(2):
                        last = pe.transpose(psTf[:, (2 * k + c) * P:(2 * k + c + 1) * P], m_hv[:, k, c * P:(c + 1) * P], ident)
                    if k % 2:
                        last.then_inc(m_hT, 1)
                for k in range(4):
                    if k % 2 == 0:
                        pe.wait_ge(m_hTc, r * 2 + k // 2 + 1)
                    for c in range(2):
                        mm = pe.matmul(psO[:, 1, k * P:(k + 1) * P], m_hTs[:, k, c, :],
                                       m_w(4 * half + k)[:, 2 * HID + c * D:2 * HID + (c + 1) * D], start=(c == 0), stop=(c == 1))
                mm.then_inc(m_y, 1)
                pe.wait_ge(m_y, r + 1)
                pe.sem_inc(m_wfree, 1)
                pe.wait_ge(m_yc, r + 1)

            with pe.Fori(0, ROUNDS) as rr:
                group(2 * rr, 0, w_in0, xs_in0, rr)
                group(2 * rr + 1, 1, w_in1, xs_in1, rr)

        @block.vector
        def _(v):
            class Chain:
                def __init__(self, s, start, per):
                    self.s, self.start, self.n, self.per = s, start, 0, per

                def __call__(self, ins):
                    self.n += 1
                    ins.then_inc(self.s, 1)
                    v.wait_ge(self.s, self.start + self.n)

                def end(self):
                    assert self.n == self.per, (self.n, self.per)

            def attend(s, a, it, scale, norm):
                for k in range(s.n + 2):
                    if k < s.n:
                        w = s.width[k] * P
                        v.wait_ge(a.S, it * s.n + k + 1)
                        ins = v.tensor_reduce(nmax[:, k % 4:k % 4 + 1], psS[:, k % 2, 0:w], AX.X, ALU.max, negate=True)
                        if scale != 1.0:
                            ins.then_inc(vecr, 1)
                            v.wait_ge(vecr, it * s.n + k + 1)
                            ins = v.tensor_scalar(nmaxs[:, k % 4:k % 4 + 1], nmax[:, k % 4:k % 4 + 1], scale, None, ALU.mult)
                        ins.then_inc(a.M, 1)
                    if k >= 2:
                        for c in range(s.first[k - 2], s.first[k - 1]):
                            if c % 2 == 1:
                                sx, lo, n = s.chunks[c]
                                v.wait_ge(a.T, it * s.nchunks + c + 1)
                                v.tensor_copy(probT[:, sx % 3, lo * P:(lo + n) * P], psT[:, 1, 0:n * P]).then_inc(a.TV, 1)
                    norm(k)

            NVEC = 12
            ch = Chain(vec, 0, NVEC)
            v.wait_ge(const_in, 16 * NCONST)
            v.wait_ge(mod_e, 1)
            v.tensor_copy(identh[:, :], ident)
            v.tensor_copy(maskh[:, :], maskf)
            ch(v.tensor_scalar(ce[:, :], ce[:, :], 1.0, None, ALU.add))
            ch(v.reciprocal(ce[:, :], ce[:, :]))
            ch(v.tensor_tensor(cs[:, :], cs[:, :], ce[:, :], ALU.mult))
            v.wait_ge(e_z, 2)
            for b in range(B):
                v.tensor_scalar(scB[:, b, :], scB[:, b, :], cs[:, b:b + 1], None, ALU.add).then_inc(mod_lhs, 1)
            for b in range(B):
                v.wait_ge(mod_mm, b + 1)
                v.tensor_copy(mod[:, b, :].rearrange("p (h n) -> p h n", h=2),
                              psS[:, b % 2, :].rearrange("p (h n) -> p h n", h=2)[:, :, 0:3 * D]).then_inc(mod_cp, 1)
            v.wait_ge(mod_cp, B)
            ch(v.memset(cum[:, 0:1], 0.0))
            for k in (2, 5):
                gate = mod[:, :, k * D:(k + 1) * D]
                ch(v.tensor_scalar(gneg[:, :, :], gate, 0.0, 2.0, ALU.is_ge, ALU.mult))
                ch(v.tensor_scalar(scB[:, :, :], gate, -1.0, 0.25, ALU.mult, ALU.max))
                ch(v.tensor_tensor(scB[:, :, :], scB[:, :, :], gate, ALU.max))
                ch(v.scalar_tensor_tensor(gate, gneg[:, :, :], -1.0, scB[:, :, :], ALU.add, ALU.mult))
            ch.end()
            for k in (1, 4):
                ins = v.tensor_scalar(mod[:, :, k * D:(k + 1) * D], mod[:, :, k * D:(k + 1) * D], 1.0, None, ALU.add)
            ins.then_inc(mod_cp, 1)
            v.wait_ge(mod_cp, B + 1)
            v.wait_ge(zero_in, 32)

            NB = 47
            with v.Fori(0, B) as b:
                ch = Chain(vecb, b * NB, NB)

                def rstd_of(n, eps):
                    ch(v.tensor_scalar(st[:, 3, :], st[:, 2, :], 1.0 / D, eps, ALU.mult, ALU.add))
                    v.sem_inc(var_ready, 1)
                    v.wait_ge(rstd_ready, n)

                def layernorm(n, src, dst, k):
                    ch(v.tensor_reduce(st[:, 0, :], src, AX.X, ALU.add))
                    ch(v.tensor_scalar(st[:, 1, :], st[:, 0, :], -1.0 / D, None, ALU.mult))
                    ch(v.tensor_tensor(wk1[:, :, :], src, bc_tok(st[:, 1, :]), ALU.add))
                    ch(v.tensor_tensor(wk2[:, :, :], wk1[:, :, :], wk1[:, :, :], ALU.mult))
                    ch(v.tensor_reduce(st[:, 2, :], wk2[:, :, :], AX.X, ALU.add))
                    rstd_of(n, LN_EPS)
                    ch(v.tensor_tensor(wk1[:, :, :], wk1[:, :, :], bc_tok(rstd[:, :]), ALU.mult))
                    ch(v.tensor_tensor(wk1[:, :, :], wk1[:, :, :], bc_mod(b, k + 1), ALU.mult))
                    ch(v.tensor_tensor(dst, wk1[:, :, :], bc_mod(b, k), ALU.add))

                def rmsnorm(n, src, dst, gain):
                    ch(v.tensor_tensor(wk1[:, :, :], src, src, ALU.mult))
                    ch(v.tensor_reduce(st[:, 2, :], wk1[:, :, :], AX.X, ALU.add))
                    rstd_of(n, RMS_EPS)
                    ch(v.tensor_tensor(wk1[:, :, :], src, bc_tok(rstd[:, :]), ALU.mult))
                    ch(v.tensor_tensor(dst, wk1[:, :, :], bc_row(gain), ALU.mult))

                v.wait_ge(xnat_in, 16 * b + 16)
                layernorm(4 * b + 1, x_nat[:, :, :], wk2[:, :, :], 0)
                v.sem_inc(tok_ready, 1)

                def normA(k):
                    i = k - 3
                    if 0 <= i < NT:
                        v.wait_ge(attA.PV, b * NT + i + 1)
                        v.reciprocal(rsum[:, i:i + 1], sums[:, i:i + 1]).then_inc(veck, 1)
                        v.wait_ge(veck, b * NT + i + 1)
                        v.tensor_scalar(Oj[:, i % 2, :], psO[:, i % 2, 0:D], rsum[:, i:i + 1], None, ALU.mult).then_inc(a_onorm, 1)
                    i = k - 4
                    if 0 <= i < NT:
                        v.wait_ge(a_proj, b * NT + i + 1)
                        v.tensor_tensor(wk1[:, i, :], psO[:, i % 2, 256:256 + D], bpb[:, :], ALU.add).then_inc(a_proj_used, 1)

                attend(stepsA, attA, b, A_SCALE, normA)
                normA(NT + 2)
                normA(NT + 3)
                v.wait_ge(a_proj_used, b * NT + NT)
                ch(v.tensor_tensor(wk1[:, :, :], wk1[:, :, :], bc_mod(b, 2), ALU.mult))
                v.wait_ge(xrow_in, 16 * b + 16)
                ch(v.tensor_tensor(x1[:, b, :, :], wk1[:, :, :], x_row[:, :, :], ALU.add))
                v.sem_inc(x_free, 1)
                layernorm(4 * b + 2, x1[:, b, :, :], hres[:, b, :, :], 3)
                rmsnorm(4 * b + 3, hres[:, b, :, :], wk2[:, :, :], gb1[:, :])
                v.sem_inc(tok_ready, 1)

                with v.Fori(0, HKV) as kv:
                    it = b * HKV + kv
                    v.wait_ge(r_k, it + 1)
                    v.tensor_tensor(rp1[0:HD, 0, :], psTf[0:HD, :], cosb[0:HD, 1, :], ALU.mult)
                    v.tensor_tensor(rp2[0:HD, 0, :], psTf[HD:P, :], sinb[HD:P, 1, :], ALU.mult).then_inc(r_prod, 1)
                    v.wait_ge(r_q, 2 * it + 1)
                    v.tensor_tensor(rp1[:, 1, :], psS[:, 0, :], cosb[:, 0, :], ALU.mult)
                    v.tensor_tensor(rp2[:, 1, :], psS[:, 1, :], sinb[:, 0, :], ALU.mult).then_inc(r_prod, 1)
                    v.wait_ge(r_hi, it * 3 + 1)
                    v.tensor_tensor(kA[HD:P, :], rp1[0:HD, 0, :], kA[0:HD, :], ALU.subtract).then_inc(vece, 1)
                    v.wait_ge(vece, it + 1)
                    v.tensor_copy(kB[HD:P, :], kA[0:HD, :])
                    v.tensor_copy(kB[0:HD, :], kA[HD:P, :])
                    v.wait_ge(r_q, 2 * it + 2)
                    v.tensor_tensor(rp1[:, 0, :], psS[:, 0, :], cosb[:, 0, :], ALU.mult)
                    v.tensor_tensor(rp2[:, 0, :], psS[:, 1, :], sinb[:, 0, :], ALU.mult).then_inc(r_prod, 1)
                    for c in range(2):
                        g, t = 2 * c, (1, 0)[c]
                        v.wait_ge(r_hi, it * 3 + 2 + c)
                        v.tensor_tensor(qs[HD:P, g, :], rp1[0:HD, t, :], qs[0:HD, g, :], ALU.subtract)
                        ins = v.tensor_tensor(qs[0:HD, g + 1, :], rp1[HD:P, t, :], qs[HD:P, g + 1, :], ALU.subtract)
                    ins.then_inc(r_ready, 1)

                    def normB(k):
                        if k < 4 or (k - 3) % NT != NT - 1:
                            return
                        g = (k - 3) // NT
                        lo = g * NT
                        v.wait_ge(attB.PV, it * stepsB.n + lo + NT)
                        v.reciprocal(rsum[:, lo:lo + NT], sums[:, lo:lo + NT]).then_inc(rsum_ready, 1)
                        v.wait_ge(rsum_ready, it * G + g + 1)
                        for n, i in enumerate(ORDER):
                            ins = v.tensor_scalar(att[:, i, g * HD:(g + 1) * HD], psO[:, g % 2, i * HD:(i + 1) * HD],
                                                  rsum[:, lo + n:lo + n + 1], None, ALU.mult)
                        ins.then_inc(o_norm, 1)

                    attend(stepsB, attB, it, 1.0, normB)
                    normB(stepsB.n + 2)
                    v.wait_ge(o_t, 2 * it + 2)
                    v.tensor_copy(aT[:, 1, :], psS[:, 1, :]).then_inc(o_T2, 1)
                    v.wait_ge(o_mm, it + 1)
                    v.tensor_tensor(hres[:, b, :, :].rearrange("p j d -> p (j d)"),
                                    hres[:, b, :, :].rearrange("p j d -> p (j d)"), psS[:, 0, :], ALU.add).then_inc(o_add, 1)
                    v.wait_ge(o_add, it + 1)

                rmsnorm(4 * b + 4, hres[:, b, :, :], wk2[:, :, :], gb2[:, :])
                ch(v.tensor_copy(hf[:, b, :, :], wk2[:, :, :]))
                v.sem_inc(tok_ready, 1)

                v.wait_ge(rt_mm, b + 1)
                ch(v.tensor_tensor(lg[:, :, :], psT[:, 0, 0:NT * E].rearrange("p (j e) -> p j e", e=E),
                                   rbb[:, :].unsqueeze(1).to_broadcast([P, NT, E]), ALU.add))
                v.sem_inc(rt_lg, 1)
                for j in range(NT):
                    ins = v.max(v8[:, j, :], lg[:, j, :])
                ch(ins)
                v.sem_inc(rt_lg, 1)
                for j in range(NT):
                    ins = v.max_index(ix[:, j, :], v8[:, j, :], lg[:, j, :])
                ch(ins)
                v.tensor_tensor(sm1[:, :], v8[:, :, 1], v8[:, :, 0], ALU.subtract).then_inc(rt_d, 1)
                ch(v.tensor_copy(ixf[:, :].rearrange("p (j k) -> p j k", k=TOPK), ix[:, :, 0:TOPK]))
                v.tensor_tensor(oh[:, :, :], iota8.unsqueeze(1).to_broadcast([P, NT * TOPK, E]),
                                ixf[:, :].unsqueeze(2).to_broadcast([P, NT * TOPK, E]), ALU.is_equal).then_inc(rt_oh, 1)
                v.wait_ge(rt_e, b + 1)
                ch(v.tensor_scalar(sm1[:, :], sm2[:, :], 1.0, None, ALU.add))
                ch(v.reciprocal(sc[:, :, 0], sm1[:, :]))
                ch(v.tensor_tensor(sc[:, :, 1], sm2[:, :], sc[:, :, 0], ALU.mult))
                v.wait_ge(rt_ohTc, b + 1)
                ch(v.tensor_tensor_scan(cum[:, 1:1 + S], ones16[:, :], ohT[:, :], cum[:, 0:1], ALU.mult, ALU.add))
                v.sem_inc(rt_cum, 1)
                v.wait_ge(rt_pos, b + 1)
                ch(v.tensor_copy(cum[:, 0:1], cum[:, S:S + 1]))
                ch(v.scalar_tensor_tensor(em[:, :, :].rearrange("p a e -> p (a e)"), psT[:, 1, 0:NT * 16], float(CAP),
                                          oh[:, :, :].rearrange("p a e -> p (a e)"), ALU.is_lt, ALU.mult))
                v.tensor_reduce(tk[:, :], em[:, :, :], AX.X, ALU.add)
                ch(v.tensor_tensor(ea[:, :, :], em[:, :, :], iota8.unsqueeze(1).to_broadcast([P, NT * TOPK, E]), ALU.mult))
                ch(v.tensor_reduce(asg[:, :, :].rearrange("p j k -> p (j k)"), ea[:, :, :], AX.X, ALU.add))
                v.tensor_reduce(chosen[:, 0, :], asg[:, :, :], AX.X, ALU.max)
                ch(v.tensor_tensor(asg2, sc[:, :, :].rearrange("p j k -> p (j k)"), tk[:, :], ALU.mult))
                v.tensor_reduce(chosen[:, 1, :], asg2.rearrange("p (j k) -> p j k", k=TOPK), AX.X, ALU.add)
                ch(v.tensor_tensor(ixf[:, :], sc[:, :, :].rearrange("p j k -> p (j k)"), asg2, ALU.subtract))
                ch(v.tensor_reduce(chosen[:, 2, :], ixf[:, :].rearrange("p (j k) -> p j k", k=TOPK), AX.X, ALU.add))
                for k, dst in enumerate((expert, wy, wx)):
                    ins = v.tensor_scalar(dst[:, b, :], chosen[:, k, :], 1.0, None, ALU.mult)
                ch(ins)
                ch.end()

            ch = Chain(plan, 0, 12)
            ch(v.tensor_tensor(ohm[:, :, :], iota8.unsqueeze(1).to_broadcast([P, NTT, E]),
                               expert[:, :, :].rearrange("p b j -> p (b j)").unsqueeze(2).to_broadcast([P, NTT, E]), ALU.is_equal))
            v.sem_inc(e_oh, 1)
            for b in range(B):
                v.wait_ge(e_ohTc, b + 1)
                ch(v.tensor_tensor_scan(rank[:, b * S:(b + 1) * S], ones16[0:8, :], ohmT[:, b * S:(b + 1) * S],
                                        0.0 if b == 0 else rank[:, b * S - 1:b * S], ALU.mult, ALU.add))
            ch(v.tensor_scalar(few[:, :], k128, rank[:, NTOK - 1:NTOK], None, ALU.is_lt))
            ch(v.tensor_reduce(ntile[:, :], few[:, :], AX.X, ALU.add))
            v.sem_inc(e_nt, 1)
            v.wait_ge(e_base, 1)
            ch(v.tensor_tensor(tend[:, :], psO[0:8, 0, 0:1], ntile[:, :], ALU.add))
            ch(v.tensor_scalar(base[:, :], psO[0:8, 0, 0:1], float(P), -1.0, ALU.mult, ALU.add))
            ch(v.scalar_tensor_tensor(ohmT[:, :], rank, base[:, 0:1], ohmT[:, :], ALU.add, ALU.mult))
            v.sem_inc(e_slotm, 1)
            ch(v.tensor_scalar(past[:, :], tile_no, tend[:, 0:1], None, ALU.is_ge))
            v.sem_inc(e_past, 1)
            v.wait_ge(e_slot, 1)
            v.tensor_copy(slot[:, :], psO[:, 1, 0:NTT]).then_inc(e_slot, 1)
            v.wait_ge(e_te, 1)
            v.wait_ge(e_slot, 2)
            ch(v.tensor_scalar(texp[:, :], psO[0:1, 0, 64:64 + ETILES], float(E - 1), None, ALU.min))
            ch.end()
            v.sem_inc(e_plan, 1)

            def group(r, half, m_out, rr, first):
                for k in range(4):
                    v.wait_ge(m_a, r * 4 + k + 1)
                    v.tensor_tensor(m_uv[:, k, :], psE(k)[:, HID:2 * HID], m_av[:, k, :], ALU.mult).then_inc(m_u, 1)
                for q in range(2):
                    v.wait_ge(m_hT, r * 2 + q + 1)
                    v.tensor_copy(m_hTs[:, 2 * q:2 * q + 2, :, :].rearrange("p k c t -> p (k c t)"),
                                  psT[:, q, :]).then_inc(m_hTc, 1)
                v.wait_ge(m_y, r + 1)
                if not first:
                    v.wait_ge(m_out, 16 * rr)
                v.tensor_copy(m_yv[:, 4 * half:4 * half + 4, :].rearrange("p k n -> p (k n)"), psO[:, 1, :]).then_inc(m_yc, 1)

            for half in range(2):
                group(half, half, (m_out0, m_out1)[half], 0, True)
            with v.Fori(1, ROUNDS) as rr:
                for half in range(2):
                    group(2 * rr + half, half, (m_out0, m_out1)[half], rr, False)

            ch = Chain(final, 0, 6 * B)
            v.wait_ge(gath, 16 * NTT)
            for b in range(B):
                y = yg[b][:, :, :]
                ch(v.tensor_tensor(y, y, bc_tok(wy[:, b, :]), ALU.mult))
                ch(v.tensor_tensor(hf[:, b, :, :], hf[:, b, :, :], bc_tok(wx[:, b, :]), ALU.mult))
                ch(v.tensor_tensor(y, y, hf[:, b, :, :], ALU.add))
                ch(v.tensor_tensor(y, y, hres[:, b, :, :], ALU.add))
                ch(v.tensor_tensor(y, y, bc_mod(b, 5), ALU.mult))
                ch(v.tensor_tensor(y, y, x1[:, b, :, :], ALU.add))
                v.sem_inc(fin, 1)
            ch.end()



def kernel(**inputs):
    import concourse.bacc as _bacc
    from concourse.bass_utils import run_bass_kernel_spmd as _run

    inp = {k: np.asarray(v) for k, v in inputs.items()}

    def row(a):
        return np.ascontiguousarray(a.reshape(-1))

    half = HD // 2
    turned = np.concatenate([np.arange(half, HD), np.arange(half)])

    def heads(w, hs, rot):
        cols = np.concatenate([h * HD + (turned if rot else np.arange(HD)) for h in hs])
        return w[:, cols]

    wq, wk, wv, wo = (inp["L0_ffn_" + n] for n in ("wq", "wk", "wv", "wo"))
    w_kv, w_o = [], []
    for h in list(range(HKV)) + [0]:
        pairs = [(h, HKV + h), (2 * HKV + h, 3 * HKV + h)]
        w_kv.append(np.concatenate([heads(wq, pairs[0], False), heads(wq, pairs[0], True), heads(wq, pairs[1], False),
                                    heads(wq, pairs[1], True), heads(wk, [h], False), heads(wk, [h], True),
                                    heads(wv, [h], False)], axis=1))
    for h in range(HKV):
        rows = [np.concatenate([wo[q * HD:(q + 1) * HD] for q in pr]) for pr in ((h, HKV + h), (2 * HKV + h, 3 * HKV + h))]
        w_o.append(np.concatenate(rows, axis=1))
    w1, w2, w3 = (inp["L0_ffn_" + n] for n in ("w1", "w2", "w3"))
    w_exp = np.concatenate([w2, w1, w3[:, 0:P], w3[:, P:2 * P]], axis=2)

    thetas = 10000.0 ** (-np.arange(0, HD, 2, dtype=np.float32) / HD)
    ticks = np.outer(np.arange(S, dtype=np.float32), thetas)
    cos, sin = (np.tile(f(ticks), (1, 4)).T for f in (np.cos, np.sin))
    sign = np.where(np.arange(P) % HD < half, -1.0, 1.0)[:, None].astype(np.float32)
    scale = np.array([1.0 / np.sqrt(HD), 1.0], np.float32)[None, :, None]
    q = np.arange(P)
    consts = np.zeros((P, 3 * P + 8), np.float32)
    consts[:, 0:P] = np.eye(P)
    consts[:, P:2 * P] = np.where(q[None, :] > q[:, None], -1e30, 0.0)
    consts[:, 2 * P:2 * P + 8] = -0.5
    consts[:, 3 * P:] = np.arange(8)
    e = np.arange(8)
    consts8 = np.concatenate([(e[:, None] < e[None, :]), np.tile(np.arange(32) * P, (8, 1)),
                              np.tile(np.arange(ETILES), (8, 1)), np.ones((8, 1))], axis=1).astype(np.float32)
    eye = np.eye(8)
    consts16 = np.block([[eye, eye], [0 * eye, eye]]).astype(np.float32)

    arrays = {
        "x": inp["L0_attn_x"], "cT": inp["L0_c"].T, "wmod": inp["L0_wmod"], "w_qkvT": inp["L0_attn_w_qkv"].T,
        "w_projT": inp["L0_attn_w_proj"].T, "b_proj": row(inp["L0_attn_b_proj"]), "g1": row(inp["L0_ffn_g1"]),
        "g2": row(inp["L0_ffn_g2"]), "w_kv": np.stack(w_kv), "w_o": np.stack(w_o + w_o[:1]),
        "router_w": inp["L0_ffn_router_w"], "router_b": row(inp["L0_ffn_router_b"]), "w_exp": w_exp,
        "consts": consts, "cos_t": (cos[:, None, :] * scale).astype(np.float32),
        "sin_t": ((sin * sign)[:, None, :] * scale).astype(np.float32), "consts8": consts8, "consts16": consts16,
    }
    arrays = {k: np.ascontiguousarray(v) for k, v in arrays.items()}
    nc = _bacc.Bacc("TRN2", target_bir_lowering=False, num_devices=1)
    args = {k: nc.dram_tensor(k + "_dram", v.shape, mybir.dt.from_np(v.dtype), kind="ExternalInput").ap()
            for k, v in arrays.items()}
    out = nc.dram_tensor("out_dram", (B, S, D), F32, kind="ExternalOutput").ap()
    build(nc, *args.values(), out)
    r = _run(nc, [{k + "_dram": v for k, v in arrays.items()}], core_ids=[0])
    return r.results[0]["out_dram"]
```

```python
from contextlib import ExitStack

import numpy as np

import concourse.bass as bass
from concourse import mybir

F32 = mybir.dt.float32
F16 = mybir.dt.float16
BF16 = mybir.dt.bfloat16
I32 = mybir.dt.int32
U32 = mybir.dt.uint32
ALU = mybir.AluOpType
ACT = mybir.ActivationFunctionType
AX = mybir.AxisListType

P = 128
B, S, D = 4, 1024, 128
NT = S // P
HKV, G, HD = 4, 4, 64
E, HID = 8, 256
TOPK = 2
CAP = B * S // 8
NTOK = B * S
NTT = NTOK // P
WQK = 2 * 2 * P + 2 * HD + HD
W_K = 4 * P
W_V = W_K + 2 * HD
SLOTS = 8
ETILES = 40
ROUNDS = ETILES // SLOTS
WE = 2 * HID + 2 * D
LN_EPS, RMS_EPS = 1e-5, 1e-6
A_SCALE = float(1.0 / np.sqrt(8.0).astype(np.float32))
NKV = B * HKV
SPH = 5
SPR = G * SPH

STEP_TILES = [[(0, range(0, 8))], [(1, range(1, 8)), (7, range(7, 8))], [(2, range(2, 8)), (6, range(6, 8))],
              [(3, range(3, 8)), (5, range(5, 8))], [(4, range(4, 8))]]


def segments(step):
    out, at = [], 0
    for j, qs in STEP_TILES[step]:
        q, n = qs[0], len(qs)
        while n:
            m = min(n, 4 - at % 4)
            out.append((j, q, m, at))
            q, n, at = q + m, n - m, at + m
    return out


def width(step):
    return sum(len(qs) for _, qs in STEP_TILES[step])


PIECES = [(i, h) for i in range(NT - 1, -1, -1) for h in range(i // 4 + 1)]
READER = {"max": "V", "row": "A", "k": "V", "v": "A", "q": "V", "r": "V", "turn": None, "out": "V"}


def reader(entry):
    if entry[0] == "turn":
        return "AV"[entry[1] % 2]
    return READER[entry[0]]


PROJ = {3: [("k", 0), ("k", 1)], 4: [("v",), ("q", 0, 0), ("r", 0, 0)], 8: [("q", 0, 1), ("r", 0, 1)],
        9: [("q", 1, 0), ("r", 1, 0), ("q", 1, 1), ("r", 1, 1)]}
OUTP = {13: [("turn", 0), ("turn", 1), ("turn", 2)], 14: [("turn", 3)], 18: [("out", 0)], 19: [("out", 1)]}


def side_work(first, last):
    steps = []
    for s in range(SPR):
        h, c = divmod(s, SPH)
        now = []
        maxima = not (last and h == G - 1)
        if c < 3 and maxima:
            now += [("max", h, *PIECES[4 * c + n]) for n in range(4)]
        if not last:
            now += PROJ.get(s, [])
        if not first:
            now += OUTP.get(s, [])
        if c == 3 and maxima:
            now.append(("row", h))
        steps.append(now)
    return steps


PROLOGUE = [e for s in sorted(PROJ) for e in PROJ[s]] + [("max", G - 1, *p) for p in PIECES] + [("row", G - 1)]
EPILOGUE = [e for s in sorted(OUTP) for e in OUTP[s]]


def count(entries, eng=None):
    return sum(1 for e in entries if eng is None or reader(e) == eng)


def flat(steps):
    return [e for st in steps for e in st]


def start(it, eng=None):
    if isinstance(it, int) and it == 0:
        return count(PROLOGUE, eng)
    if isinstance(it, int) and it == NKV:
        return start(NKV - 1, eng) + count(flat(side_work(False, True)), eng)
    return it * count(flat(side_work(False, False)), eng) + (count(PROLOGUE, eng) - count(EPILOGUE, eng))


class Steps:

    def __init__(self, widths):
        self.width = widths
        self.chunks = []
        self.first = []
        for s, w in enumerate(widths):
            self.first.append(len(self.chunks))
            for lo in range(0, w, 4):
                self.chunks.append((s, lo, min(4, w - lo)))
        self.first.append(len(self.chunks))
        self.n = len(widths)
        self.nchunks = len(self.chunks)

    def emptied(self, c, bank):
        return (c + 1 - bank) // 2


def build(nc, x, cT, wmod, w_qkvT, w_projT, b_proj, g1, g2, w_kv, w_o, router_w, router_b, w_exp, consts,
          cos_t, sin_t, consts8, consts16, out):
    ctx = ExitStack()
    with ctx:
        def sb(name, shape, dt=F32):
            return ctx.enter_context(nc.sbuf_tensor(name, shape, dt))

        def sem(name):
            return ctx.enter_context(nc.semaphore(name))

        rows_in = nc.dram_tensor("rows_in", [ETILES * P, D], F32).ap()
        xnT_d = nc.dram_tensor("xnT_d", [B, P, S], F32).ap()
        rows_out = nc.dram_tensor("rows_out", [ETILES * P, D], F32).ap()

        psS = ctx.enter_context(nc.psum_tensor("psS", [P, 2, 1024], F32))
        psT = ctx.enter_context(nc.psum_tensor("psT", [P, 2, 512], F32))
        psO = ctx.enter_context(nc.psum_tensor("psO", [P, 2, 512], F32))
        psX = psT
        psTf = psT[:, :, :].rearrange("p a b -> p (a b)")

        cst = sb("cst", [P, 3 * P + 16])
        ident, maskf = cst[:, 0:P], cst[:, P:2 * P]
        mhalf, iota8 = cst[:, 2 * P:2 * P + 8], cst[:, 2 * P + 8:2 * P + 16]
        c8 = sb("c8", [8, 8 + 32 + ETILES + 1])
        lower8, k128, tile_no, ones8 = c8[:, 0:8], c8[:, 8:40], c8[:, 40:40 + ETILES], c8[:, 40 + ETILES:41 + ETILES]
        c16 = sb("c16", [16, 16])
        trig = sb("trig", [P, 4, S])
        cosb = trig[:, 0:2, :]
        sinb = trig[:, 2:4, :]
        identh = sb("identh", [P, P], BF16)
        maskh = sb("maskh", [P, P], BF16)
        maskt = sb("maskt", [P, P], BF16)
        ones16 = sb("ones16", [16, S])
        gb1 = sb("gb1", [P, D])
        gb2 = sb("gb2", [P, D])
        bpb = sb("bpb", [P, D])
        rbb = sb("rbb", [P, E])
        wqkv = sb("wqkv", [P, 3 * D])
        wproj = sb("wproj", [P, D])
        rw = sb("rw", [P, E])
        cs = sb("cs", [P, B])
        ce = sb("ce", [P, B])
        mod = sb("mod", [P, B, 6 * D])

        arena = sb("arena", [P, 27 * S])
        taken = [0]

        def carve(words, restart=False):
            if restart:
                taken[0] = 0
            a = arena[:, taken[0]:taken[0] + words]
            taken[0] += words
            assert taken[0] <= 27 * S, taken[0]
            return a

        def tiles(a, n=D):
            return a.rearrange("p (j d) -> p j d", d=n)

        x_nat = tiles(carve(S))
        x_row = tiles(carve(S))
        hT = carve(S)
        qkv = carve(3 * S).rearrange("p (a n) -> p a n", a=3)
        qT, kT, va = qkv[:, 0, :], qkv[:, 1, :], tiles(qkv[:, 2, :])
        prob = carve(3 * S).rearrange("p (a n) -> p a n", a=3)
        probT = carve(3 * S).rearrange("p (a n) -> p a n", a=3)
        xn = carve(S)
        wm = carve(6 * D)
        scB = carve(B * P).rearrange("p (b n) -> p b n", b=B)
        def half16(words):
            return carve(words).bitcast(F16)

        qA = half16(2 * G * S // 2).rearrange("p (r g n) -> p r g n", r=2, g=G)
        taken[0] = 0
        qA = half16(2 * G * S // 2).rearrange("p (r g n) -> p r g n", r=2, g=G)
        qB = half16(2 * G * S // 2).rearrange("p (r g n) -> p r g n", r=2, g=G)
        kA = half16(S).rearrange("p (r n) -> p r n", r=2)
        kB = half16(S).rearrange("p (r n) -> p r n", r=2)
        kC = half16(S).rearrange("p (r n) -> p r n", r=2)
        pT = carve(2 * S).rearrange("p (r n) -> p r n", r=2)
        rp1 = carve(2 * S).rearrange("p (r n) -> p r n", r=2)
        rp2 = carve(2 * S).rearrange("p (r n) -> p r n", r=2)
        qhi = half16(S).rearrange("p (c n) -> p c n", c=2)
        qlo = half16(S).rearrange("p (c n) -> p c n", c=2)
        aT = carve(2 * S).rearrange("p (c n) -> p c n", c=2)
        xs = carve(2 * S).rearrange("p (r n) -> p r n", r=2)
        att = carve(4 * S).rearrange("p (r j n) -> p r j n", r=2, j=NT)
        wexp_all = carve(SLOTS * WE, True).rearrange("p (k n) -> p k n", k=SLOTS)
        exp_xs = carve(SLOTS * P)
        m_xTs = carve(4 * P).rearrange("p (k t) -> p k t", k=4)
        m_av, m_uv, m_hv = (carve(S).rearrange("p (k n) -> p k n", k=4) for _ in range(3))
        m_hTs = carve(S).rearrange("p (k c t) -> p k c t", k=4, c=2)
        m_yv = tiles(carve(S))
        counts = carve(4 * S)
        rank, ohT, cum = counts[0:8, :], counts[0:16, 0:S], counts[0:16, S:2 * S + 1]
        yg = [tiles(carve(S)) for _ in range(B)]
        hfT = carve(S)
        hf = carve(4 * S).rearrange("p (b j d) -> p b j d", b=B, j=NT)

        wk1 = sb("wk1", [P, NT, D])
        wk2 = sb("wk2", [P, NT, D])
        gneg = wk1[:, 0:B, :]
        st = sb("st", [P, 4, NT])
        rstd = sb("rstd", [P, NT])
        nmax = sb("nmax", [P, 4])
        nmaxs = sb("nmaxs", [P, 4])
        sums = sb("sums", [P, NT])
        rsum = sb("rsum", [P, NT])
        Oj = sb("Oj", [P, 2, D])
        wkv = sb("wkv", [P, 2, WQK])
        wo = sb("wo", [P, 2, 2 * D])
        vb = sb("vb", [P, 2, NT, HD + 1])
        pmax = sb("pmax", [P, 2, NT, 2])
        hmax = sb("hmax", [P, 2, NT])
        hrow = sb("hrow", [NT, 2, P], F16)
        oinv = sb("oinv", [P, NT])
        x1 = sb("x1", [P, B, NT, D])
        hres = sb("hres", [P, B, NT, D])
        expert = sb("expert", [P, B, NT])
        wy = sb("wy", [P, B, NT])
        wx = sb("wx", [P, B, NT])
        lg = sb("lg", [P, NT, E])
        v8 = sb("v8", [P, NT, 8])
        ix = sb("ix", [P, NT, 8], U32)
        ixf = sb("ixf", [P, NT * TOPK])
        oh = sb("oh", [P, NT * TOPK, E])
        em = sb("em", [P, NT * TOPK, E])
        ea = sb("ea", [P, NT * TOPK, E])
        sc = sb("sc", [P, NT, TOPK])
        tk = sb("tk", [P, NT * TOPK])
        asg = sb("asg", [P, NT, TOPK])
        asg2 = sb("asg2", [P, NT * TOPK])[:, :]
        chosen = sb("chosen", [P, 3, NT])
        sm1 = sb("sm1", [P, NT])
        sm2 = sb("sm2", [P, NT])
        ohm = sb("ohm", [P, NTT, E])
        ohmT = trig[0:8, :, :].rearrange("e a t -> e (a t)")
        few = sb("few", [8, 32])
        ntile = sb("ntile", [8, 1])
        base = sb("base", [8, 1])
        tend = sb("tend", [8, 1])
        past = sb("past", [8, ETILES])
        slot = sb("slot", [P, NTT], U32)
        texp = sb("texp", [1, ETILES], I32)

        const_in, mod_e, mod_lhs, mod_mm, mod_cp, vec = (sem("const_in"), sem("mod_e"), sem("mod_lhs"),
                                                         sem("mod_mm"), sem("mod_cp"), sem("vec"))
        xnat_in, xrow_in, x_free = sem("xnat_in"), sem("xrow_in"), sem("x_free")
        var_ready, rstd_ready = sem("var_ready"), sem("rstd_ready")
        tok_ready, tok_t, tok_T = sem("tok_ready"), sem("tok_t"), sem("tok_T")
        a_qkv, a_qkv_cp = sem("a_qkv"), sem("a_qkv_cp")
        a_proj, a_proj_used = sem("a_proj"), sem("a_proj_used")
        wo_in, loads_in = [sem("wo_in0"), sem("wo_in1")], [sem("loads_in0"), sem("loads_in1")]
        xn_out, xn_free = sem("xn_out"), sem("xn_free")
        projected, wo_used = sem("projected"), sem("wo_used")
        side_full, side_V, side_A = sem("side_full"), sem("side_read_vec"), sem("side_read_act")
        r_sum, r_hi, r_lo, qk_in = sem("rotated"), sem("high_halves"), sem("low_halves"), sem("qk_in")
        max_ready, row_in = sem("max_ready"), sem("row_in")
        b_scores, b_exp, b_out, b_sum, b_norm, ones_set = (sem("b_scores"), sem("b_exp"), sem("b_out"), sem("b_sum"),
                                                           sem("b_norm"), sem("ones_set"))
        rt_lg, rt_mm, rt_d, rt_e, rt_oh, rt_ohT, rt_ohTc, rt_cum, rt_pos = (sem("rt_lg"), sem("rt_mm"), sem("rt_d"), sem("rt_e"), sem("rt_oh"), sem("rt_ohT"),
                                                            sem("rt_ohTc"), sem("rt_cum"), sem("rt_pos"))
        vecc, vecb, veck, vecr, vece = sem("vecc"), sem("vecb"), sem("veck"), sem("vecr"), sem("vece")

        class Att:
            def __init__(self, n):
                self.S, self.M, self.E, self.T, self.TA, self.TV, self.PV = (sem(f"{n}_{w}") for w in (
                    "scores", "max", "exp", "turned", "turned_act", "turned_vec", "pv"))
        attA = Att("a")
        a_onorm, rsum_ready, plan, final = sem("a_onorm"), sem("rsum_ready"), sem("plan"), sem("final")
        e_z, e_oh, e_ohT, e_ohTc, e_nt, e_base, e_slotm, e_slot, e_past, e_te, e_plan = (sem(n) for n in (
            "e_z", "e_oh", "e_ohT", "e_ohTc", "e_nt", "e_base", "e_slotm", "e_slot", "e_past", "e_te", "e_plan"))
        scat, w_in0, w_in1, xs_in0, xs_in1 = sem("scat"), sem("w_in0"), sem("w_in1"), sem("xs_in0"), sem("xs_in1")
        m_xT, m_xTc, m_ab, m_a, m_u, m_h, m_hT, m_hTc, m_y, m_yc, m_wfree, m_out0, m_out1 = (sem(n) for n in (
            "m_xT", "m_xTc", "m_ab", "m_a", "m_u", "m_h", "m_hT", "m_hTc", "m_y", "m_yc", "m_wfree", "m_out0", "m_out1"))
        gath, fin, out_done, zero_in = sem("gath"), sem("fin"), sem("out_done"), sem("zero_in")

        stepsA = Steps([NT] * NT)

        NCONST = 14
        def start_parity(p, first):
            return (start(0) if first else start(p if p else 2)) % 2

        block = ctx.enter_context(nc.Block())

        def bc_mod(b, k):
            return mod[:, b, k * D:(k + 1) * D].unsqueeze(1).to_broadcast([P, NT, D])

        def bc_tok(stat):
            return stat.unsqueeze(2).to_broadcast([P, NT, D])

        def bc_row(v):
            return v.unsqueeze(1).to_broadcast([P, NT, D])

        def m_w(k):
            return wexp_all[:, k, :]

        def m_xs(k):
            return exp_xs[:, k * P:(k + 1) * P]

        def psE(k):
            return psS[:, k // 2, (k % 2) * 512:(k % 2) * 512 + 512]

        @block.sync
        def _(sp):
            def load_x(b):
                sp.dma_start(x_nat[:, :, :], x[b].rearrange("(j p) e -> p j e", p=P)).then_inc(xnat_in, 16)
                sp.dma_start(x_row, x[b].rearrange("(p j) e -> p j e", p=P)).then_inc(xrow_in, 16)

            load_x(0)
            n = 0
            for dst, src in ((cst[:, :], consts), (cs[:, :], cT), (wm[:, :], wmod), (wqkv[:, :], w_qkvT),
                             (wproj[:, :], w_projT), (bpb[:, :], b_proj.partition_broadcast(P)),
                             (gb1[:, :], g1.partition_broadcast(P)), (gb2[:, :], g2.partition_broadcast(P)),
                             (rbb[:, :], router_b.partition_broadcast(P)), (rw[:, :], router_w),
                             (cosb[:, :, :], cos_t), (sinb[:, :, :], sin_t), (c8[:, :], consts8), (c16[:, :], consts16)):
                sp.dma_start(dst, src).then_inc(const_in, 16)
                n += 1
            assert n == NCONST

            with sp.Fori(0, B - 1) as b:
                sp.wait_ge(x_free, b + 1)
                load_x(b + 1)
                sp.wait_ge(tok_T, 2 * b + 2)
                sp.dma_start(xnT_d[b], xn).then_inc(xn_out, 16)
                sp.wait_ge(xn_out, 16 * b + 16)
                sp.sem_inc(xn_free, 1)
            sp.wait_ge(x_free, B)
            sp.wait_ge(tok_T, 2 * B)
            sp.dma_start(xnT_d[B - 1], xn).then_inc(xn_out, 16)
            sp.wait_ge(xn_out, 16 * B)

            def load_round(it, p):
                sp.dma_start(xs[:, p, :], xnT_d[it // HKV]).then_inc(loads_in[p], 16)
                sp.dma_start(wkv[:, p, :], w_kv[it % HKV]).then_inc(loads_in[p], 16)

            def load_wo(it, p):
                sp.dma_start(wo[:, p, :], w_o[it % HKV]).then_inc(wo_in[p], 16)

            def spread_qk(n, p):
                def move(dst, src):
                    sp.dma_start(dst, src).then_inc(qk_in, 16)

                sp.wait_ge(r_hi, 3 * n + 1)
                sp.wait_ge(r_lo, 3 * n + 1)
                move(kA[0:HD, p, :], kB[0:HD, p, :])
                move(kA[HD:P, p, :], kC[0:HD, p, :])
                move(kC[HD:P, p, :], kB[0:HD, p, :])
                sp.wait_ge(r_hi, 3 * n + 3)
                for h in range(2):
                    src = qhi[HD * h:HD * h + HD, :, :]
                    move(qB[0:HD, p, h::2, :], src)
                    move(qA[HD:P, p, h::2, :], src)
                sp.wait_ge(r_lo, 3 * n + 3)
                for h in range(2):
                    move(qA[0:HD, p, h::2, :], qlo[HD * h:HD * h + HD, :, :])

            def spread_row(read, p, g):
                sp.wait_ge(side_A, read)
                sp.dma_start(qB[HD:HD + 1, p, g, :].rearrange("o (i t) -> o i t", t=P),
                             hrow[:, g % 2, :]).then_inc(row_in, 16)

            for it in range(2):
                load_round(it, it)
                load_wo(it, it)
            spread_qk(0, 0)
            spread_row(start(0, "A"), 0, 0)

            def round_loads(it, p, first, last, ahead):
                if ahead:
                    sp.wait_ge(projected, it + 1)
                    load_round(it + 2, p)
                work = [e for e in flat(side_work(first, last)) if reader(e) == "A"]

                def row_of(h):
                    return start(it, "A") + work.index(("row", h)) + 1

                spread_row(row_of(0), p, 1)
                spread_row(row_of(1), p, 2)
                if not last:
                    spread_qk(it + 1, 1 - p)
                spread_row(row_of(2), p, 3)
                if not last:
                    spread_row(row_of(3), 1 - p, 0)
                if not first and not last:
                    sp.wait_ge(wo_used, it)
                    load_wo(it + 1, 1 - p)

            round_loads(0, 0, True, False, True)
            with sp.Fori(1, NKV - 3, 2) as it:
                round_loads(it, 1, False, False, True)
                round_loads(it + 1, 0, False, False, True)
            round_loads(NKV - 3, 1, False, False, True)
            round_loads(NKV - 2, 0, False, False, False)
            round_loads(NKV - 1, 1, False, True, False)

            sp.wait_ge(e_plan, 1)
            sp.wait_ge(scat, 16 * NTT)

            def load_tile(k, u, half):
                e = sp.value_load(texp[0:1, bass.ds(u, 1)], min_val=0, max_val=E - 1)
                sp.dma_start(m_w(k), w_exp[bass.ds(e, 1)].rearrange("o p n -> (o p) n")).then_inc((w_in0, w_in1)[half], 16)
                sp.dma_start(m_xs(k), rows_in[bass.ds(u * P, P), :]).then_inc((xs_in0, xs_in1)[half], 16)

            for k in range(SLOTS):
                load_tile(k, k, k // 4)
            with sp.Fori(0, ROUNDS - 1) as r:
                for half in range(2):
                    sp.wait_ge(m_wfree, r * 2 + half + 1)
                    for k in range(4 * half, 4 * half + 4):
                        load_tile(k, (r + 1) * SLOTS + k, half)
            for b in range(B):
                sp.wait_ge(fin, b + 1)
                sp.dma_start(out[b].rearrange("(p j) e -> p j e", p=P), yg[b][:, :, :]).then_inc(out_done, 16)
            sp.wait_ge(out_done, 16 * B)

        @block.gpsimd
        def _(pool):
            pool.memset(ones16[:, :], 1.0).then_inc(e_z, 1)
            pool.memset(scB[:, :, :], 0.0).then_inc(e_z, 1)
            pool.wait_ge(e_z, 2)
            pool.memset(x1[:, :, :, :], 0.0).then_inc(e_z, 1)
            pool.wait_ge(e_z, 3)
            z = x1[:, :, :, :].rearrange("p b j d -> p (b j) d")
            pool.dma_start(rows_in[0:NTOK, :].rearrange("(t p) d -> p t d", p=P), z).then_inc(zero_in, 16)
            pool.dma_start(rows_in[NTOK:ETILES * P, :].rearrange("(t p) d -> p t d", p=P), z[:, 0:ETILES - NTT, :]
                           ).then_inc(zero_in, 16)
            pool.wait_ge(const_in, 16 * NCONST)

            def power(n):
                pool.wait_ge(var_ready, n)
                pool.tensor_tensor(rstd[:, :], st[:, 3, :], mhalf, ALU.pow).then_inc(rstd_ready, 1)

            with pool.Fori(0, B) as b:
                for k in range(3):
                    power(3 * b + k + 1)

            def rotate(n, base, p):
                for c in range(3):
                    rows = HD if c == 0 else P
                    t = (0, 1, 0)[c]
                    done = [e[0] in "kqr" and (e[0] == "k" or e[1] == c - 1) for e in PROJ_V]
                    last = max(i for i, e in enumerate(done) if e and (PROJ_V[i][0] == "k") == (c == 0))
                    pool.wait_ge(side_V, base + VEC_AT[PROJ_V[last]] + 1)
                    pool.tensor_tensor(rp1[0:rows, t, :], rp1[0:rows, t, :], rp2[0:rows, t, :], ALU.add).then_inc(r_sum, 1)
                    pool.wait_ge(r_hi, 3 * n + c + 1)
                    if c == 0:
                        pool.tensor_tensor(kC[0:HD, p, :], rp1[0:HD, t, :], kB[0:HD, p, :], ALU.subtract).then_inc(r_lo, 1)
                    else:
                        pool.tensor_tensor(qlo[:, c - 1, :], rp1[:, t, :], qhi[:, c - 1, :], ALU.subtract).then_inc(r_lo, 1)

            PROJ_V = [e for e in flat(PROJ.values()) if reader(e) == "V"]
            VEC_AT = {e: i for i, e in enumerate(x for x in PROLOGUE if reader(x) == "V")}
            pool.wait_ge(xn_out, 16 * B)
            pool.memset(kB[HD:HD + 1, :, :], 1.0).then_inc(ones_set, 1)
            rotate(0, 0, 0)

            def pool_round(it, p, first):
                VEC_AT.clear()
                VEC_AT.update({e: i for i, e in enumerate(x for x in flat(side_work(first, False)) if reader(x) == "V")})
                rotate(it + 1, start(it, "V"), 1 - p)

            pool_round(0, 0, True)
            with pool.Fori(1, NKV - 1, 2) as it:
                pool_round(it, 1, False)
                pool_round(it + 1, 0, False)
            with pool.Fori(0, B) as b:
                power(b + 3 * B + 1)

            pool.wait_ge(e_slot, 2)
            pool.wait_ge(zero_in, 32)
            hff = hf[:, :, :, :].rearrange("p b j d -> p (b j) d")
            for t in range(NTT):
                pool.indirect_dma_start(rows_in, bass.IndirectOffsetOnAxis(slot[:, t:t + 1], 0), hff[:, t, :], None
                                        ).then_inc(scat, 16)
            with pool.Fori(0, ROUNDS) as rr:
                for h in range(2):
                    pool.wait_ge(m_yc, 2 * rr + h + 1)
                    pool.dma_start(rows_out[bass.ds((2 * rr + h) * 4 * P, 4 * P), :].rearrange("(k p) d -> p k d", p=P),
                                   m_yv[:, 4 * h:4 * h + 4, :]).then_inc((m_out0, m_out1)[h], 16)
            for h in range(2):
                pool.wait_ge((m_out0, m_out1)[h], 16 * ROUNDS)
            for t in range(NTT):
                pool.indirect_dma_start(yg[t // NT][:, t % NT, :], None, rows_out,
                                        bass.IndirectOffsetOnAxis(slot[:, t:t + 1], 0)).then_inc(gath, 16)

        @block.scalar
        def _(act):
            def attend(s, a, it, scale):
                def turned(st_, c):
                    sx, lo, n = s.chunks[c]
                    act.wait_ge(a.T, it * s.nchunks + c + 1)
                    act.activation(probT[:, sx % 3, lo * P:(lo + n) * P], psT[:, 0, 0:n * P], ACT.Copy).then_inc(a.TA, 1)

                done = 0
                for k in range(s.n + 2):
                    if k < s.n:
                        act.wait_ge(a.M, it * s.n + k + 1)
                        w = s.width[k] * P
                        act.activation(prob[:, k % 3, 0:w], psS[:, k % 2, 0:w], ACT.Exp,
                                       bias=(nmax if scale == 1.0 else nmaxs)[:, k % 4:k % 4 + 1], scale=scale,
                                       accum_out=sums[:, k:k + 1]).then_inc(a.E, 1)
                    if k >= 2:
                        for c in range(s.first[k - 2], s.first[k - 1]):
                            if c % 2 == 0:
                                turned(k - 2, c)

            act.wait_ge(const_in, 16 * NCONST)
            act.activation(ce[:, :], cs[:, :], ACT.Exp, scale=-1.0).then_inc(mod_e, 1)

            def to_features(n, dst, row):
                act.wait_ge(tok_t, n)
                if row:
                    act.activation(dst.rearrange("d (p j) -> d j p", j=NT),
                                   psS[:, 0, :].rearrange("d (j p) -> d j p", p=P), ACT.Copy).then_inc(tok_T, 1)
                else:
                    act.activation(dst, psS[:, 0, :], ACT.Copy).then_inc(tok_T, 1)

            with act.Fori(0, B) as b:
                to_features(2 * b + 1, hT, False)
                act.wait_ge(a_qkv, 3 * b + 1)
                act.activation(qT, psS[:, 1, :], ACT.Copy).then_inc(a_qkv_cp, 1)
                act.wait_ge(a_qkv, 3 * b + 2)
                act.activation(kT, psS[:, 0, :], ACT.Copy).then_inc(a_qkv_cp, 1)
                act.wait_ge(a_qkv, 3 * b + 3)
                act.activation(va.rearrange("p j d -> p (j d)"), psTf, ACT.Copy).then_inc(a_qkv_cp, 1)
                attend(stepsA, attA, b, A_SCALE)
                act.wait_ge(xn_free, b + 1)
                to_features(2 * b + 2, xn, True)

            def read(e, bank, full, p):
                act.wait_ge(side_full, full)
                src = psX[:, bank, :]
                if e[0] == "v":
                    ins = act.activation(vb[:, p, :, 0:HD], src.rearrange("p (j d) -> p j d", d=HD), ACT.Copy)
                elif e[0] == "turn":
                    c, h = divmod(e[1], 2)
                    ins = act.activation(aT[:, c, h * 512:(h + 1) * 512], src, ACT.Copy)
                else:
                    g = (e[1] + 1) % 2
                    ins = act.activation(hrow[:, g, :], src[0:NT, 0:P], ACT.Copy)
                ins.then_inc(side_A, 1)

            def high_half(c, n, p):
                act.wait_ge(r_sum, 3 * n + c + 1)
                t = (0, 1, 0)[c]
                if c == 0:
                    act.activation(kB[0:HD, p, :], rp1[0:HD, t, :], ACT.Copy).then_inc(r_hi, 1)
                else:
                    act.activation(qhi[:, c - 1, :], rp1[:, t, :], ACT.Copy).then_inc(r_hi, 1)

            p0 = list(PROLOGUE)
            for i, e in enumerate(p0):
                if reader(e) == "A":
                    if e[0] == "row":
                        for c in range(3):
                            high_half(c, 0, 0)
                    read(e, i % 2, i + 1, 0)

            HIGH_AT = {6: 0, 10: 1, 12: 2}

            def act_round(it, p, first, last):
                steps = side_work(first, last)
                i = 0
                for s in range(SPR):
                    act.wait_ge(b_scores, it * SPR + s + 1)
                    w = width(s % SPH) * P
                    act.activation(pT[:, s % 2, 0:w], psS[:, s % 2, 0:w], ACT.Exp).then_inc(b_exp, 1)
                    for e in steps[s]:
                        if reader(e) == "A":
                            read(e, (start_parity(p, first) + i) % 2, start(it) + i + 1, 1 - p)
                        i += 1
                    if s in HIGH_AT and not last:
                        high_half(HIGH_AT[s], it + 1, 1 - p)

            act_round(0, 0, True, False)
            with act.Fori(1, NKV - 1, 2) as it:
                act_round(it, 1, False, False)
                act_round(it + 1, 0, False, False)
            act_round(NKV - 1, 1, False, True)
            for i, e in enumerate(EPILOGUE):
                if reader(e) == "A":
                    read(e, (start(NKV) + i) % 2, start(NKV) + i + 1, 0)

            with act.Fori(0, B) as b:
                to_features(b + 2 * B + 1, hfT, False)
                act.wait_ge(rt_d, b + 1)
                act.activation(sm2[:, :], sm1[:, :], ACT.Exp).then_inc(rt_e, 1)
                act.wait_ge(rt_ohT, b + 1)
                act.activation(ohT[:, :].rearrange("r (p j) -> r j p", j=NT),
                               psS[0:16, 1, :].rearrange("r (j p) -> r j p", p=P), ACT.Copy).then_inc(rt_ohTc, 1)

            for b in range(B):
                act.wait_ge(e_ohT, b + 1)
                act.activation(ohmT[:, b * S:(b + 1) * S], psS[0:8, b % 2, :], ACT.Copy).then_inc(e_ohTc, 1)

            with act.Fori(0, ROUNDS * 2) as r:
                act.wait_ge(m_xT, r + 1)
                act.activation(m_xTs.rearrange("p k t -> p (k t)"), psO[:, 0, :], ACT.Copy).then_inc(m_xTc, 1)
                for k in range(4):
                    act.wait_ge(m_ab, r * 4 + k + 1)
                    act.activation(m_av[:, k, :], psE(k)[:, 0:HID], ACT.Copy).then_inc(m_a, 1)
                for k in range(4):
                    act.wait_ge(m_u, r * 4 + k + 1)
                    act.activation(m_hv[:, k, :], m_uv[:, k, :], ACT.Gelu).then_inc(m_h, 1)

        @block.tensor
        def _(pe):
            def attend(s, a, it, scores, values):
                def turn(k):
                    pe.wait_ge(a.E, it * s.n + k + 1)
                    for c in range(s.first[k], s.first[k + 1]):
                        _, lo, n = s.chunks[c]
                        if c >= 2:
                            half = s.emptied(c, c % 2)
                            cnt = s.emptied(s.nchunks, c % 2)
                            pe.wait_ge((a.TA, a.TV)[c % 2], it * cnt + half)
                        for j in range(n):
                            last = pe.transpose(psT[:, c % 2, j * P:(j + 1) * P],
                                                prob[:, k % 3, (lo + j) * P:(lo + j + 1) * P], ident)
                        last.then_inc(a.T, 1)

                def pv(k):
                    cl = s.first[k + 1]
                    for q in range(2):
                        cnt = s.emptied(s.nchunks, q)
                        n = s.emptied(cl, q)
                        if n:
                            pe.wait_ge((a.TA, a.TV)[q], it * cnt + n)
                    values(k)

                for k in range(s.n + 3):
                    if k < s.n:
                        if k >= 2:
                            pe.wait_ge(a.E, it * s.n + k - 1)
                        scores(k).then_inc(a.S, 1)
                    if 2 <= k < s.n + 2:
                        turn(k - 2)
                    if k >= 3:
                        pv(k - 3)

            pe.wait_ge(const_in, 16 * NCONST)
            for b in range(B):
                pe.wait_ge(mod_lhs, b + 1)
                if b >= 2:
                    pe.wait_ge(mod_cp, b - 1)
                for h in range(2):
                    mm = pe.matmul(psS[:, b % 2, h * 512:h * 512 + 3 * D], scB[:, b, :], wm[:, h * 3 * D:(h + 1) * 3 * D],
                                   start=True, stop=True)
                mm.then_inc(mod_mm, 1)

            def turn_tokens(n, src):
                pe.wait_ge(tok_ready, n)
                for j in range(NT):
                    last = pe.transpose(psS[:, 0, j * P:(j + 1) * P], src(j), ident)
                last.then_inc(tok_t, 1)

            with pe.Fori(0, B) as b:
                turn_tokens(2 * b + 1, lambda j: wk2[:, j, :])
                pe.wait_ge(tok_T, 2 * b + 1)
                for k, dst in ((0, psS[:, 1, :]), (1, psS[:, 0, :])):
                    for h in range(2):
                        mm = pe.matmul(dst[:, h * 512:(h + 1) * 512], wqkv[:, k * D:(k + 1) * D], hT[:, h * 512:(h + 1) * 512],
                                       start=True, stop=True)
                    mm.then_inc(a_qkv, 1)
                for j in range(NT):
                    mm = pe.matmul(psTf[:, j * P:(j + 1) * P], hT[:, j * P:(j + 1) * P], wqkv[:, 2 * D:3 * D], start=True, stop=True)
                mm.then_inc(a_qkv, 1)
                pe.wait_ge(a_qkv_cp, 3 * b + 3)

                def scoresA(i):
                    for h in range(2):
                        mm = pe.matmul(psS[:, i % 2, h * 512:(h + 1) * 512], qT[:, i * P:(i + 1) * P],
                                       kT[:, h * 512:(h + 1) * 512], start=True, stop=True)
                    return mm

                def projA(i):
                    pe.wait_ge(a_onorm, b * NT + i + 1)
                    pe.matmul(psO[:, i % 2, 256:256 + D], Oj[:, i % 2, :], wproj[:, :], start=True, stop=True).then_inc(a_proj, 1)

                def valuesA(i):
                    if i >= 2:
                        pe.wait_ge(a_proj_used, b * NT + i - 1)
                    for j in range(NT):
                        mm = pe.matmul(psO[:, i % 2, 0:D], probT[:, i % 3, j * P:(j + 1) * P], va[:, j, :],
                                       start=(j == 0), stop=(j == NT - 1))
                    mm.then_inc(attA.PV, 1)
                    if i >= 1:
                        projA(i - 1)

                attend(stepsA, attA, b, scoresA, valuesA)
                projA(NT - 1)

                turn_tokens(2 * b + 2, lambda j: wk2[:, j, :])
                pe.wait_ge(tok_T, 2 * b + 2)

            def fill(e, bank, p, n):
                dst = psX[:, bank, :]
                kind = e[0]
                if kind in "kqrv":
                    if e == ("k", 0):
                        pe.wait_ge(loads_in[p], 32 * (n // 2) + 32)
                    if kind == "v":
                        for j in range(NT):
                            mm = pe.matmul(dst[:, j * HD:(j + 1) * HD], xs[:, p, j * P:(j + 1) * P], wkv[:, p, W_V:W_V + HD],
                                           start=True, stop=True)
                        return mm
                    h = e[-1]
                    w0 = W_K if kind == "k" else (2 * e[1] + (kind == "r")) * P
                    return pe.matmul(dst, wkv[:, p, w0:w0 + P], xs[:, p, h * 512:(h + 1) * 512], start=True, stop=True)
                if kind == "max":
                    g, i, h = (e[1] + 1) % G, e[2], e[3]
                    if g == 0 and (i, h) == PIECES[0]:
                        pe.wait_ge(qk_in, 144 * n + 144)
                    w = min(4, i + 1 - 4 * h) * P
                    diag = h == i // 4
                    mm = pe.matmul(dst[:, 0:w], qA[:, p, g, i * P:(i + 1) * P], kC[:, p, h * 512:h * 512 + w],
                                   start=True, stop=not diag)
                    if diag:
                        mm = pe.matmul(dst[:, w - P:w], identh[:, :], maskh[:, :], start=False, stop=True)
                    return mm
                if kind == "row":
                    g = (e[1] + 1) % G
                    pe.wait_ge(max_ready, n * G + g + 1)
                    return pe.transpose(dst[0:NT, 0:P], hmax[:, g % 2, :], ident)
                if kind == "turn":
                    c, h = divmod(e[1], 2)
                    for i in range(4):
                        mm = pe.transpose(dst[:, i * P:(i + 1) * P], att[:, p, 4 * h + i, c * P:(c + 1) * P], ident)
                    return mm
                for j in range(4):
                    for c in range(2):
                        mm = pe.matmul(dst[:, j * D:(j + 1) * D],
                                       aT[:, c, :].rearrange("f (p j) -> f j p", j=NT)[:, 4 * e[1] + j, :],
                                       wo[:, p, c * D:(c + 1) * D], start=(c == 0), stop=(c == 1))
                return mm

            def before(entries, i, base):
                if i < 2:
                    for eng, sm in (("V", side_V), ("A", side_A)):
                        if not (isinstance(base[eng], int) and base[eng] == 0):
                            pe.wait_ge(sm, base[eng])
                    return
                eng = reader(entries[i - 2])
                pe.wait_ge({"V": side_V, "A": side_A}[eng], base[eng] + count(entries[:i - 1], eng))

            def side(entries, i, base, p0, p, it):
                e = entries[i]
                before(entries, i, base)
                bank = (p0 + i) % 2
                nxt = e[0] in ("k", "q", "r", "v") or (e[0] in ("max", "row") and e[1] == G - 1)
                prev = e[0] in ("turn", "out")
                if prev:
                    if e == ("turn", 0):
                        pe.wait_ge(b_norm, 2 * G * it)
                        pe.wait_ge(wo_in[1 - p], 16 * ((it + 1) // 2))
                    if e == ("out", 0):
                        k = entries.index(("turn", 3))
                        for eng, sm in (("V", side_V), ("A", side_A)):
                            pe.wait_ge(sm, base[eng] + count(entries[:k + 1], eng))
                mm = fill(e, bank, (1 - p) if (nxt or prev) else p, it + 1 if nxt else it)
                mm.then_inc(side_full, 1)
                if e == ("r", 1, 1):
                    pe.wait_ge(side_full, base["n"] + i + 1)
                    pe.sem_inc(projected, 1)
                if e == ("out", 1):
                    pe.wait_ge(side_full, base["n"] + i + 1)
                    pe.sem_inc(wo_used, 1)

            def scoresB(it, p, s):
                g, c = divmod(s, SPH)
                if c == 0:
                    pe.wait_ge(row_in, 16 * (it * G + g) + 16)
                for j, i0, n, at in segments(c):
                    dst = psS[:, s % 2, at * P:(at + n) * P]
                    diag = i0 == j
                    pe.matmul(dst, kA[:, p, j * P:(j + 1) * P], qA[:, p, g, i0 * P:(i0 + n) * P], start=True, stop=False)
                    mm = pe.matmul(dst, kB[0:HD + 1, p, j * P:(j + 1) * P], qB[0:HD + 1, p, g, i0 * P:(i0 + n) * P],
                                   start=False, stop=not diag)
                    if diag:
                        mm = pe.matmul(dst[:, 0:P], identh[:, :], maskt[:, :], start=False, stop=True)
                mm.then_inc(b_scores, 1)

            def out_tile(i):
                return psO[:, i // 4, (i % 4) * (HD + 1):(i % 4 + 1) * (HD + 1)]

            def values_parts(it, p, s):
                g, c = divmod(s, SPH)
                todo = [(j, i) for j, qs in STEP_TILES[c] for i in qs]

                def part(lo, hi, last):
                    for n in range(lo, hi):
                        j, i = todo[n]
                        if c == 0 and i in (0, 4) and not (isinstance(it, int) and it == 0 and g == 0):
                            pe.wait_ge(b_norm, 2 * (it * G + g) - 1 + i // 4)
                        mm = pe.matmul(out_tile(i), pT[:, s % 2, n * P:(n + 1) * P], vb[:, p, j, :],
                                       start=(c == 0 and i % 4 == 0), stop=(c == SPH - 1), skip_group_check=True)
                    if last and c == SPH - 1:
                        mm.then_inc(b_out, 1)

                h = (len(todo) + 1) // 2
                return [lambda: part(0, h, False), lambda: part(h, len(todo), True)]

            zero = {"V": 0, "A": 0, "n": 0}
            pe.wait_ge(x_free, B)
            pe.wait_ge(tok_T, 2 * B)
            pe.wait_ge(ones_set, 3)
            for i in range(len(PROLOGUE)):
                side(PROLOGUE, i, zero, 0, 1, -1)

            def pe_round(it, p, first, last):
                steps = side_work(first, last)
                work = flat(steps)
                base = {"V": start(it, "V"), "A": start(it, "A"), "n": start(it)}
                p0 = start_parity(p, first)
                i = 0
                for s in range(SPR):
                    scoresB(it, p, s)
                    n = len(steps[s])
                    todo = [lambda k=k: side(work, k, base, p0, p, it) for k in range(i, i + n)]
                    i += n
                    parts = []
                    if s > 0:
                        pe.wait_ge(b_exp, it * SPR + s)
                        parts = values_parts(it, p, s - 1)
                    elif not first:
                        pe.wait_ge(b_exp, it * SPR)
                        parts = values_parts(it - 1, 1 - p, SPR - 1)
                    order = todo[0:2] + parts[0:1] + todo[2:3] + parts[1:2] + todo[3:]
                    for f in order:
                        f()

            pe_round(0, 0, True, False)
            with pe.Fori(1, NKV - 1, 2) as it:
                pe_round(it, 1, False, False)
                pe_round(it + 1, 0, False, False)
            pe_round(NKV - 1, 1, False, True)
            pe.wait_ge(b_exp, NKV * SPR)
            for f in values_parts(NKV - 1, 1, SPR - 1):
                f()
            base = {"V": start(NKV, "V"), "A": start(NKV, "A"), "n": start(NKV)}
            for i in range(len(EPILOGUE)):
                side(EPILOGUE, i, base, start(NKV) % 2, 0, NKV)

            with pe.Fori(0, B) as b:
                turn_tokens(2 * B + b + 1, lambda j: wk2[:, j, :])
                pe.wait_ge(tok_T, 2 * B + b + 1)
                for j in range(NT):
                    mm = pe.matmul(psT[:, 0, j * E:(j + 1) * E], hfT[:, j * P:(j + 1) * P], rw[:, :], start=True, stop=True)
                mm.then_inc(rt_mm, 1)
                pe.wait_ge(rt_oh, b + 1)
                for j in range(NT):
                    last = pe.transpose(psS[0:16, 1, j * P:(j + 1) * P],
                                        oh[:, j * TOPK:(j + 1) * TOPK, :].rearrange("p k e -> p (k e)"), ident)
                last.then_inc(rt_ohT, 1)
                pe.wait_ge(rt_cum, b + 1)
                for j in range(NT):
                    mm = pe.matmul(psT[:, 1, j * 16:(j + 1) * 16],
                                   cum[:, 1:1 + S].rearrange("r (p j) -> r j p", j=NT)[:, j, :], c16[:, :], start=True, stop=True)
                mm.then_inc(rt_pos, 1)

            pe.wait_ge(e_oh, 1)
            for b in range(B):
                if b >= 2:
                    pe.wait_ge(e_ohTc, b - 1)
                for j in range(NT):
                    last = pe.transpose(psS[0:8, b % 2, j * P:(j + 1) * P], ohm[:, b * NT + j, :], ident)
                last.then_inc(e_ohT, 1)
            pe.wait_ge(e_nt, 1)
            pe.matmul(psO[0:8, 0, 0:1], lower8, ntile[:, :], start=True, stop=True).then_inc(e_base, 1)
            pe.wait_ge(e_slotm, 1)
            for t in range(NTT):
                mm = pe.matmul(psO[:, 1, t:t + 1], ohmT[:, t * P:(t + 1) * P], ones8, start=True, stop=True)
            mm.then_inc(e_slot, 1)
            pe.wait_ge(e_past, 1)
            pe.matmul(psO[0:1, 0, 64:64 + ETILES], ones8, past[:, :], start=True, stop=True).then_inc(e_te, 1)
            pe.wait_ge(e_plan, 1)

            def group(r, half, w_in, xs_in, rr):
                pe.wait_ge(xs_in, 64 * rr + 64)
                for k in range(4):
                    last = pe.transpose(psO[:, 0, k * P:(k + 1) * P], m_xs(4 * half + k), ident)
                last.then_inc(m_xT, 1)
                pe.wait_ge(m_xTc, r + 1)
                pe.wait_ge(w_in, 64 * rr + 64)
                for k in range(4):
                    pe.matmul(psE(k), m_xTs[:, k, :], m_w(4 * half + k)[:, 0:2 * HID], start=True, stop=True).then_inc(m_ab, 1)
                for k in range(4):
                    pe.wait_ge(m_h, r * 4 + k + 1)
                    for c in range(2):
                        last = pe.transpose(psTf[:, (2 * k + c) * P:(2 * k + c + 1) * P], m_hv[:, k, c * P:(c + 1) * P], ident)
                    if k % 2:
                        last.then_inc(m_hT, 1)
                for k in range(4):
                    if k % 2 == 0:
                        pe.wait_ge(m_hTc, r * 2 + k // 2 + 1)
                    for c in range(2):
                        mm = pe.matmul(psO[:, 1, k * P:(k + 1) * P], m_hTs[:, k, c, :],
                                       m_w(4 * half + k)[:, 2 * HID + c * D:2 * HID + (c + 1) * D], start=(c == 0), stop=(c == 1))
                mm.then_inc(m_y, 1)
                pe.wait_ge(m_y, r + 1)
                pe.sem_inc(m_wfree, 1)
                pe.wait_ge(m_yc, r + 1)

            with pe.Fori(0, ROUNDS) as rr:
                group(2 * rr, 0, w_in0, xs_in0, rr)
                group(2 * rr + 1, 1, w_in1, xs_in1, rr)

        @block.vector
        def _(v):
            class Chain:
                def __init__(self, s, start, per):
                    self.s, self.start, self.n, self.per = s, start, 0, per

                def __call__(self, ins):
                    self.n += 1
                    ins.then_inc(self.s, 1)
                    v.wait_ge(self.s, self.start + self.n)

                def end(self):
                    assert self.n == self.per, (self.n, self.per)

            def attend(s, a, it, scale, norm):
                for k in range(s.n + 2):
                    if k < s.n:
                        w = s.width[k] * P
                        v.wait_ge(a.S, it * s.n + k + 1)
                        ins = v.tensor_reduce(nmax[:, k % 4:k % 4 + 1], psS[:, k % 2, 0:w], AX.X, ALU.max, negate=True)
                        if scale != 1.0:
                            ins.then_inc(vecr, 1)
                            v.wait_ge(vecr, it * s.n + k + 1)
                            ins = v.tensor_scalar(nmaxs[:, k % 4:k % 4 + 1], nmax[:, k % 4:k % 4 + 1], scale, None, ALU.mult)
                        ins.then_inc(a.M, 1)
                    if k >= 2:
                        for c in range(s.first[k - 2], s.first[k - 1]):
                            if c % 2 == 1:
                                sx, lo, n = s.chunks[c]
                                v.wait_ge(a.T, it * s.nchunks + c + 1)
                                v.tensor_copy(probT[:, sx % 3, lo * P:(lo + n) * P], psT[:, 1, 0:n * P]).then_inc(a.TV, 1)
                    norm(k)

            NVEC = 11
            ch = Chain(vec, 0, NVEC)
            v.wait_ge(const_in, 16 * NCONST)
            v.wait_ge(mod_e, 1)
            v.tensor_copy(identh[:, :], ident)
            v.tensor_copy(maskh[:, :], maskf)
            v.tensor_copy(maskt[:, :], cst[:, 2 * P + 16:3 * P + 16])
            v.memset(vb[:, :, :, HD], 1.0).then_inc(ones_set, 1)
            v.sem_inc(ones_set, 1)
            v.sem_inc(xn_free, 1)
            ch(v.tensor_scalar(ce[:, :], ce[:, :], 1.0, None, ALU.add))
            ch(v.reciprocal(ce[:, :], ce[:, :]))
            ch(v.tensor_tensor(cs[:, :], cs[:, :], ce[:, :], ALU.mult))
            v.wait_ge(e_z, 2)
            for b in range(B):
                v.tensor_scalar(scB[:, b, :], scB[:, b, :], cs[:, b:b + 1], None, ALU.add).then_inc(mod_lhs, 1)
            for b in range(B):
                v.wait_ge(mod_mm, b + 1)
                v.tensor_copy(mod[:, b, :].rearrange("p (h n) -> p h n", h=2),
                              psS[:, b % 2, :].rearrange("p (h n) -> p h n", h=2)[:, :, 0:3 * D]).then_inc(mod_cp, 1)
            v.wait_ge(mod_cp, B)
            for k in (2, 5):
                gate = mod[:, :, k * D:(k + 1) * D]
                ch(v.tensor_scalar(gneg[:, :, :], gate, 0.0, 2.0, ALU.is_ge, ALU.mult))
                ch(v.tensor_scalar(scB[:, :, :], gate, -1.0, 0.25, ALU.mult, ALU.max))
                ch(v.tensor_tensor(scB[:, :, :], scB[:, :, :], gate, ALU.max))
                ch(v.scalar_tensor_tensor(gate, gneg[:, :, :], -1.0, scB[:, :, :], ALU.add, ALU.mult))
            ch.end()
            for k in (1, 4):
                ins = v.tensor_scalar(mod[:, :, k * D:(k + 1) * D], mod[:, :, k * D:(k + 1) * D], 1.0, None, ALU.add)
            ins.then_inc(mod_cp, 1)
            v.wait_ge(mod_cp, B + 1)
            v.wait_ge(zero_in, 32)

            NB = 25
            with v.Fori(0, B) as b:
                ch = Chain(vecb, b * NB, NB)

                def rstd_of(n, eps):
                    ch(v.tensor_scalar(st[:, 3, :], st[:, 2, :], 1.0 / D, eps, ALU.mult, ALU.add))
                    v.sem_inc(var_ready, 1)
                    v.wait_ge(rstd_ready, n)

                def layernorm(n, src, dst, k):
                    ch(v.tensor_reduce(st[:, 0, :], src, AX.X, ALU.add))
                    ch(v.tensor_scalar(st[:, 1, :], st[:, 0, :], -1.0 / D, None, ALU.mult))
                    ch(v.tensor_tensor(wk1[:, :, :], src, bc_tok(st[:, 1, :]), ALU.add))
                    ch(v.tensor_tensor(wk2[:, :, :], wk1[:, :, :], wk1[:, :, :], ALU.mult))
                    ch(v.tensor_reduce(st[:, 2, :], wk2[:, :, :], AX.X, ALU.add))
                    rstd_of(n, LN_EPS)
                    ch(v.tensor_tensor(wk1[:, :, :], wk1[:, :, :], bc_tok(rstd[:, :]), ALU.mult))
                    ch(v.tensor_tensor(wk1[:, :, :], wk1[:, :, :], bc_mod(b, k + 1), ALU.mult))
                    ch(v.tensor_tensor(dst, wk1[:, :, :], bc_mod(b, k), ALU.add))

                def rmsnorm(n, src, dst, gain):
                    ch(v.tensor_tensor(wk1[:, :, :], src, src, ALU.mult))
                    ch(v.tensor_reduce(st[:, 2, :], wk1[:, :, :], AX.X, ALU.add))
                    rstd_of(n, RMS_EPS)
                    ch(v.tensor_tensor(wk1[:, :, :], src, bc_tok(rstd[:, :]), ALU.mult))
                    ch(v.tensor_tensor(dst, wk1[:, :, :], bc_row(gain), ALU.mult))

                v.wait_ge(xnat_in, 16 * b + 16)
                layernorm(3 * b + 1, x_nat, wk2[:, :, :], 0)
                v.sem_inc(tok_ready, 1)

                def normA(k):
                    i = k - 3
                    if 0 <= i < NT:
                        v.wait_ge(attA.PV, b * NT + i + 1)
                        v.reciprocal(rsum[:, i:i + 1], sums[:, i:i + 1]).then_inc(veck, 1)
                        v.wait_ge(veck, b * NT + i + 1)
                        v.tensor_scalar(Oj[:, i % 2, :], psO[:, i % 2, 0:D], rsum[:, i:i + 1], None, ALU.mult).then_inc(a_onorm, 1)
                    i = k - 4
                    if 0 <= i < NT:
                        v.wait_ge(a_proj, b * NT + i + 1)
                        v.tensor_tensor(wk1[:, i, :], psO[:, i % 2, 256:256 + D], bpb[:, :], ALU.add).then_inc(a_proj_used, 1)

                attend(stepsA, attA, b, A_SCALE, normA)
                normA(NT + 2)
                normA(NT + 3)
                v.wait_ge(a_proj_used, b * NT + NT)
                ch(v.tensor_tensor(wk1[:, :, :], wk1[:, :, :], bc_mod(b, 2), ALU.mult))
                v.wait_ge(xrow_in, 16 * b + 16)
                ch(v.tensor_tensor(x1[:, b, :, :], wk1[:, :, :], x_row[:, :, :], ALU.add))
                v.sem_inc(x_free, 1)
                layernorm(3 * b + 2, x1[:, b, :, :], hres[:, b, :, :], 3)
                rmsnorm(3 * b + 3, hres[:, b, :, :], wk2[:, :, :], gb1[:, :])
                v.sem_inc(tok_ready, 1)
                v.wait_ge(tok_t, 2 * b + 2)
                ch.end()

            v.wait_ge(ones_set, 3)
            v.memset(pmax[:, :, :, :], -3e38).then_inc(ones_set, 1)
            v.wait_ge(ones_set, 4)

            def read(e, bank, full, p, it, own):
                v.wait_ge(side_full, full)
                src = psX[:, bank, :]
                kind = e[0]
                if kind == "k":
                    h = slice(e[1] * 512, (e[1] + 1) * 512)
                    v.tensor_tensor(rp1[0:HD, 0, h], src[0:HD, :], cosb[0:HD, 1, h], ALU.mult)
                    ins = v.tensor_tensor(rp2[0:HD, 0, h], src[HD:P, :], sinb[HD:P, 1, h], ALU.mult)
                elif kind in "qr":
                    h = slice(e[2] * 512, (e[2] + 1) * 512)
                    dst, tab = (rp1, cosb) if kind == "q" else (rp2, sinb)
                    if e == ("q", 1, 0):
                        v.wait_ge(r_lo, 3 * it + 1)
                    ins = v.tensor_tensor(dst[:, 1 - e[1], h], src, tab[:, 0, h], ALU.mult)
                elif kind == "max":
                    g, i, h = (e[1] + 1) % G, e[2], e[3]
                    w = min(4, i + 1 - 4 * h) * P
                    ins = v.tensor_reduce(pmax[:, g % 2, i, h:h + 1], src[:, 0:w], AX.X, ALU.max)
                elif kind == "turn":
                    c, h = divmod(e[1], 2)
                    ins = v.tensor_copy(aT[:, c, h * 512:(h + 1) * 512], src)
                else:
                    row = (it // HKV if not isinstance(it, int) else it // HKV)
                    dst = hres[:, row, 4 * e[1]:4 * e[1] + 4, :].rearrange("p j d -> p (j d)")
                    ins = v.tensor_tensor(dst, dst, src, ALU.add)
                ins.then_inc(side_V, 1)
                if kind == "max" and (e[2], e[3]) == PIECES[-1]:
                    g = (e[1] + 1) % G
                    v.wait_ge(side_V, own + 1)
                    v.tensor_reduce(hmax[:, g % 2, :], pmax[:, g % 2, :, :], AX.X, ALU.max, negate=True).then_inc(max_ready, 1)

            def norm(n, p, g):
                v.wait_ge(b_out, n + 1)
                for h in range(2):
                    v.reciprocal(oinv[:, 4 * h:4 * h + 4], outs(h)[:, :, HD]).then_inc(b_sum, 1)
                v.wait_ge(b_sum, 2 * n + 2)
                for h in range(2):
                    v.tensor_tensor(att[:, p, 4 * h:4 * h + 4, g * HD:(g + 1) * HD], outs(h)[:, :, 0:HD],
                                    oinv[:, 4 * h:4 * h + 4].unsqueeze(2).to_broadcast([P, 4, HD]), ALU.mult).then_inc(b_norm, 1)

            def outs(h):
                return psO[:, h, 0:4 * (HD + 1)].rearrange("p (i d) -> p i d", d=HD + 1)

            own = 0
            for i, e in enumerate(PROLOGUE):
                if reader(e) == "V":
                    read(e, i % 2, i + 1, 0, 0, own)
                    own += 1

            def vec_round(it, p, first, last):
                steps = side_work(first, last)
                i, own = 0, 0
                for s in range(SPR):
                    h, c = divmod(s, SPH)
                    if c == 1:
                        if h > 0:
                            norm(it * G + h - 1, p, h - 1)
                        elif not first:
                            norm(it * G - 1, 1 - p, G - 1)
                    for e in steps[s]:
                        if reader(e) == "V":
                            n = it - 1 if e[0] == "out" else it + 1
                            read(e, (start_parity(p, first) + i) % 2, start(it) + i + 1, 1 - p, n, start(it, "V") + own)
                            own += 1
                        i += 1

            vec_round(0, 0, True, False)
            with v.Fori(1, NKV - 1, 2) as it:
                vec_round(it, 1, False, False)
                vec_round(it + 1, 0, False, False)
            vec_round(NKV - 1, 1, False, True)
            norm(NKV * G - 1, 1, G - 1)
            own = 0
            for i, e in enumerate(EPILOGUE):
                if reader(e) == "V":
                    read(e, (start(NKV) + i) % 2, start(NKV) + i + 1, 0, NKV - 1, start(NKV, "V") + own)
                    own += 1
            v.wait_ge(side_V, start(NKV, "V") + count(EPILOGUE, "V"))

            NB2 = 22
            v.memset(cum[:, 0:1], 0.0).then_inc(ones_set, 1)
            v.wait_ge(ones_set, 5)
            with v.Fori(0, B) as b:
                ch = Chain(vecc, b * NB2, NB2)
                rmsnorm(b + 3 * B + 1, hres[:, b, :, :], wk2[:, :, :], gb2[:, :])
                ch(v.tensor_copy(hf[:, b, :, :], wk2[:, :, :]))
                v.sem_inc(tok_ready, 1)

                v.wait_ge(rt_mm, b + 1)
                ch(v.tensor_tensor(lg[:, :, :], psT[:, 0, 0:NT * E].rearrange("p (j e) -> p j e", e=E),
                                   rbb[:, :].unsqueeze(1).to_broadcast([P, NT, E]), ALU.add))
                v.sem_inc(rt_lg, 1)
                for j in range(NT):
                    ins = v.max(v8[:, j, :], lg[:, j, :])
                ch(ins)
                v.sem_inc(rt_lg, 1)
                for j in range(NT):
                    ins = v.max_index(ix[:, j, :], v8[:, j, :], lg[:, j, :])
                ch(ins)
                v.tensor_tensor(sm1[:, :], v8[:, :, 1], v8[:, :, 0], ALU.subtract).then_inc(rt_d, 1)
                ch(v.tensor_copy(ixf[:, :].rearrange("p (j k) -> p j k", k=TOPK), ix[:, :, 0:TOPK]))
                v.tensor_tensor(oh[:, :, :], iota8.unsqueeze(1).to_broadcast([P, NT * TOPK, E]),
                                ixf[:, :].unsqueeze(2).to_broadcast([P, NT * TOPK, E]), ALU.is_equal).then_inc(rt_oh, 1)
                v.wait_ge(rt_e, b + 1)
                ch(v.tensor_scalar(sm1[:, :], sm2[:, :], 1.0, None, ALU.add))
                ch(v.reciprocal(sc[:, :, 0], sm1[:, :]))
                ch(v.tensor_tensor(sc[:, :, 1], sm2[:, :], sc[:, :, 0], ALU.mult))
                v.wait_ge(rt_ohTc, b + 1)
                ch(v.tensor_tensor_scan(cum[:, 1:1 + S], ones16[:, :], ohT[:, :], cum[:, 0:1], ALU.mult, ALU.add))
                v.sem_inc(rt_cum, 1)
                v.wait_ge(rt_pos, b + 1)
                ch(v.tensor_copy(cum[:, 0:1], cum[:, S:S + 1]))
                ch(v.scalar_tensor_tensor(em[:, :, :].rearrange("p a e -> p (a e)"), psT[:, 1, 0:NT * 16], float(CAP),
                                          oh[:, :, :].rearrange("p a e -> p (a e)"), ALU.is_lt, ALU.mult))
                v.tensor_reduce(tk[:, :], em[:, :, :], AX.X, ALU.add)
                ch(v.tensor_tensor(ea[:, :, :], em[:, :, :], iota8.unsqueeze(1).to_broadcast([P, NT * TOPK, E]), ALU.mult))
                ch(v.tensor_reduce(asg[:, :, :].rearrange("p j k -> p (j k)"), ea[:, :, :], AX.X, ALU.add))
                v.tensor_reduce(chosen[:, 0, :], asg[:, :, :], AX.X, ALU.max)
                ch(v.tensor_tensor(asg2, sc[:, :, :].rearrange("p j k -> p (j k)"), tk[:, :], ALU.mult))
                v.tensor_reduce(chosen[:, 1, :], asg2.rearrange("p (j k) -> p j k", k=TOPK), AX.X, ALU.add)
                ch(v.tensor_tensor(ixf[:, :], sc[:, :, :].rearrange("p j k -> p (j k)"), asg2, ALU.subtract))
                ch(v.tensor_reduce(chosen[:, 2, :], ixf[:, :].rearrange("p (j k) -> p j k", k=TOPK), AX.X, ALU.add))
                for k, dst in enumerate((expert, wy, wx)):
                    ins = v.tensor_scalar(dst[:, b, :], chosen[:, k, :], 1.0, None, ALU.mult)
                ch(ins)
                ch.end()

            ch = Chain(plan, 0, 12)
            ch(v.tensor_tensor(ohm[:, :, :], iota8.unsqueeze(1).to_broadcast([P, NTT, E]),
                               expert[:, :, :].rearrange("p b j -> p (b j)").unsqueeze(2).to_broadcast([P, NTT, E]), ALU.is_equal))
            v.sem_inc(e_oh, 1)
            for b in range(B):
                v.wait_ge(e_ohTc, b + 1)
                ch(v.tensor_tensor_scan(rank[:, b * S:(b + 1) * S], ones16[0:8, :], ohmT[:, b * S:(b + 1) * S],
                                        0.0 if b == 0 else rank[:, b * S - 1:b * S], ALU.mult, ALU.add))
            ch(v.tensor_scalar(few[:, :], k128, rank[:, NTOK - 1:NTOK], None, ALU.is_lt))
            ch(v.tensor_reduce(ntile[:, :], few[:, :], AX.X, ALU.add))
            v.sem_inc(e_nt, 1)
            v.wait_ge(e_base, 1)
            ch(v.tensor_tensor(tend[:, :], psO[0:8, 0, 0:1], ntile[:, :], ALU.add))
            ch(v.tensor_scalar(base[:, :], psO[0:8, 0, 0:1], float(P), -1.0, ALU.mult, ALU.add))
            ch(v.scalar_tensor_tensor(ohmT[:, :], rank, base[:, 0:1], ohmT[:, :], ALU.add, ALU.mult))
            v.sem_inc(e_slotm, 1)
            ch(v.tensor_scalar(past[:, :], tile_no, tend[:, 0:1], None, ALU.is_ge))
            v.sem_inc(e_past, 1)
            v.wait_ge(e_slot, 1)
            v.tensor_copy(slot[:, :], psO[:, 1, 0:NTT]).then_inc(e_slot, 1)
            v.wait_ge(e_te, 1)
            v.wait_ge(e_slot, 2)
            ch(v.tensor_scalar(texp[:, :], psO[0:1, 0, 64:64 + ETILES], float(E - 1), None, ALU.min))
            ch.end()
            v.sem_inc(e_plan, 1)

            def group(r, half, m_out, rr, first):
                for k in range(4):
                    v.wait_ge(m_a, r * 4 + k + 1)
                    v.tensor_tensor(m_uv[:, k, :], psE(k)[:, HID:2 * HID], m_av[:, k, :], ALU.mult).then_inc(m_u, 1)
                for q in range(2):
                    v.wait_ge(m_hT, r * 2 + q + 1)
                    v.tensor_copy(m_hTs[:, 2 * q:2 * q + 2, :, :].rearrange("p k c t -> p (k c t)"),
                                  psT[:, q, :]).then_inc(m_hTc, 1)
                v.wait_ge(m_y, r + 1)
                if not first:
                    v.wait_ge(m_out, 16 * rr)
                v.tensor_copy(m_yv[:, 4 * half:4 * half + 4, :].rearrange("p k n -> p (k n)"), psO[:, 1, :]).then_inc(m_yc, 1)

            for half in range(2):
                group(half, half, (m_out0, m_out1)[half], 0, True)
            with v.Fori(1, ROUNDS) as rr:
                for half in range(2):
                    group(2 * rr + half, half, (m_out0, m_out1)[half], rr, False)

            ch = Chain(final, 0, 6 * B)
            v.wait_ge(gath, 16 * NTT)
            for b in range(B):
                y = yg[b][:, :, :]
                ch(v.tensor_tensor(y, y, bc_tok(wy[:, b, :]), ALU.mult))
                ch(v.tensor_tensor(hf[:, b, :, :], hf[:, b, :, :], bc_tok(wx[:, b, :]), ALU.mult))
                ch(v.tensor_tensor(y, y, hf[:, b, :, :], ALU.add))
                ch(v.tensor_tensor(y, y, hres[:, b, :, :], ALU.add))
                ch(v.tensor_tensor(y, y, bc_mod(b, 5), ALU.mult))
                ch(v.tensor_tensor(y, y, x1[:, b, :, :], ALU.add))
                v.sem_inc(fin, 1)
            ch.end()



def kernel(**inputs):
    import concourse.bacc as _bacc
    from concourse.bass_utils import run_bass_kernel_spmd as _run

    inp = {k: np.asarray(v) for k, v in inputs.items()}

    def row(a):
        return np.ascontiguousarray(a.reshape(-1))

    half = HD // 2
    turned = np.concatenate([np.arange(half, HD), np.arange(half)])

    def heads(w, hs, rot):
        cols = np.concatenate([h * HD + (turned if rot else np.arange(HD)) for h in hs])
        return w[:, cols]

    wq, wk, wv, wo = (inp["L0_ffn_" + n] for n in ("wq", "wk", "wv", "wo"))
    w_kv, w_o = [], []
    for h in range(HKV):
        pairs = [(h, HKV + h), (2 * HKV + h, 3 * HKV + h)]
        w_kv.append(np.concatenate([heads(wq, pairs[0], False), heads(wq, pairs[0], True), heads(wq, pairs[1], False),
                                    heads(wq, pairs[1], True), heads(wk, [h], False), heads(wk, [h], True),
                                    heads(wv, [h], False)], axis=1))
    for h in range(HKV):
        rows = [np.concatenate([wo[q * HD:(q + 1) * HD] for q in pr]) for pr in ((h, HKV + h), (2 * HKV + h, 3 * HKV + h))]
        w_o.append(np.concatenate(rows, axis=1))
    w1, w2, w3 = (inp["L0_ffn_" + n] for n in ("w1", "w2", "w3"))
    w_exp = np.concatenate([w2, w1, w3[:, 0:P], w3[:, P:2 * P]], axis=2)

    thetas = 10000.0 ** (-np.arange(0, HD, 2, dtype=np.float32) / HD)
    ticks = np.outer(np.arange(S, dtype=np.float32), thetas)
    cos, sin = (np.tile(f(ticks), (1, 4)).T for f in (np.cos, np.sin))
    sign = np.where(np.arange(P) % HD < half, -1.0, 1.0)[:, None].astype(np.float32)
    scale = np.array([1.0 / np.sqrt(HD), 1.0], np.float32)[None, :, None]
    q = np.arange(P)
    consts = np.zeros((P, 3 * P + 16), np.float32)
    consts[:, 0:P] = np.eye(P)
    consts[:, P:2 * P] = np.where(q[None, :] > q[:, None], -1e30, 0.0)
    consts[:, 2 * P:2 * P + 8] = -0.5
    consts[:, 2 * P + 8:2 * P + 16] = np.arange(8)
    consts[:, 2 * P + 16:] = consts[:, P:2 * P].T
    e = np.arange(8)
    consts8 = np.concatenate([(e[:, None] < e[None, :]), np.tile(np.arange(32) * P, (8, 1)),
                              np.tile(np.arange(ETILES), (8, 1)), np.ones((8, 1))], axis=1).astype(np.float32)
    eye = np.eye(8)
    consts16 = np.block([[eye, eye], [0 * eye, eye]]).astype(np.float32)

    arrays = {
        "x": inp["L0_attn_x"], "cT": inp["L0_c"].T, "wmod": inp["L0_wmod"], "w_qkvT": inp["L0_attn_w_qkv"].T,
        "w_projT": inp["L0_attn_w_proj"].T, "b_proj": row(inp["L0_attn_b_proj"]), "g1": row(inp["L0_ffn_g1"]),
        "g2": row(inp["L0_ffn_g2"]), "w_kv": np.stack(w_kv), "w_o": np.stack(w_o),
        "router_w": inp["L0_ffn_router_w"], "router_b": row(inp["L0_ffn_router_b"]), "w_exp": w_exp,
        "consts": consts, "cos_t": (cos[:, None, :] * scale).astype(np.float32),
        "sin_t": ((sin * sign)[:, None, :] * scale).astype(np.float32), "consts8": consts8, "consts16": consts16,
    }
    arrays = {k: np.ascontiguousarray(v) for k, v in arrays.items()}
    nc = _bacc.Bacc("TRN2", target_bir_lowering=False, num_devices=1)
    args = {k: nc.dram_tensor(k + "_dram", v.shape, mybir.dt.from_np(v.dtype), kind="ExternalInput").ap()
            for k, v in arrays.items()}
    out = nc.dram_tensor("out_dram", (B, S, D), F32, kind="ExternalOutput").ap()
    build(nc, *args.values(), out)
    r = _run(nc, [{k + "_dram": v for k, v in arrays.items()}], core_ids=[0])
    return r.results[0]["out_dram"]
```

```python
from contextlib import ExitStack

import numpy as np

import concourse.bass as bass
from concourse import mybir

F32 = mybir.dt.float32
F16 = mybir.dt.float16
BF16 = mybir.dt.bfloat16
I32 = mybir.dt.int32
U32 = mybir.dt.uint32
ALU = mybir.AluOpType
ACT = mybir.ActivationFunctionType
AX = mybir.AxisListType

P = 128
B, S, D = 4, 1024, 128
NT = S // P
HKV, G, HD = 4, 4, 64
E, HID = 8, 256
TOPK = 2
CAP = B * S // 8
NTOK = B * S
NTT = NTOK // P
WQK = 2 * 2 * P + 2 * HD + HD
W_K = 4 * P
W_V = W_K + 2 * HD
SLOTS = 8
AHEAD = 3
ETILES = 40
ROUNDS = ETILES // SLOTS
WE = 2 * HID + 2 * D
DW = D + 1
LN_EPS, RMS_EPS = 1e-5, 1e-6
A_SCALE = float(1.0 / np.sqrt(8.0).astype(np.float32))
NKV = B * HKV
OBANK = [range(0, 3), range(3, 6), range(6, 8)]

BLOCKS = [(j, i) for bank in OBANK for j in range(NT) for i in bank if i >= j]
SPH = len(BLOCKS) // 4
SPR = G * SPH
VW = 2 * HD + 2


def segments(c):
    out = []
    for at, (j, i) in enumerate(BLOCKS[4 * c:4 * c + 4]):
        if out and out[-1][0] == j and out[-1][1] + out[-1][2] == i:
            out[-1][2] += 1
        else:
            out.append([j, i, 1, at])
    return out


PIECES = [(i, h) for i in range(NT - 1, -1, -1) for h in range(i // 4 + 1)]
READER = {"max": "V", "row": "A", "k": "V", "v": "V", "q": "V", "r": "V", "turn": "A", "out": "V"}


def reader(entry):
    return READER[entry[0]]


PROJ = {6: ("k", 0), 7: ("k", 1), 8: ("q", 0, 0), 9: ("r", 0, 0), 10: ("q", 0, 1), 11: ("r", 0, 1), 12: ("v",),
        14: ("q", 1, 0), 15: ("r", 1, 0), 16: ("q", 1, 1), 17: ("r", 1, 1)}
OUTP = {18: ("turn", 0), 20: ("turn", 1), 22: ("turn", 2), 24: ("turn", 3), 25: ("out", 0), 34: ("out", 1)}
SUM_AT = {9: 0, 13: 1, 18: 2}
HIGH_AT = {11: 0, 16: 1, 21: 2}
LOW_AT = {12: 0, 17: 1, 22: 2}


def side_work(first, last):
    steps = []
    for s in range(SPR):
        h, c = divmod(s, SPH)
        now = []
        maxima = not (last and h == G - 1)
        if c < 6 and maxima:
            now += [("max", h, *PIECES[2 * c + n]) for n in range(2)]
        if not last and s in PROJ:
            now.append(PROJ[s])
        if not first and s in OUTP:
            now.append(OUTP[s])
        if c == 6 and maxima:
            now.append(("row", h))
        steps.append(now)
    return steps


PROLOGUE = [PROJ[s] for s in sorted(PROJ)] + [("max", G - 1, *p) for p in PIECES] + [("row", G - 1)]
EPILOGUE = [OUTP[s] for s in sorted(OUTP)]


def count(entries, eng=None):
    return sum(1 for e in entries if eng is None or reader(e) == eng)


HIGH_AFTER = {("r", 0, 0): 0, ("v",): 1, ("r", 1, 1): 2}

NORM_AFTER = {("k", 1): 2, ("r", 0, 0): 3, ("v",): 4, ("r", 1, 1): 5}

LOW_V = [s for s in range(SPR) if s % SPH in (1, 5, 7)]


def lows(it, s, eng):
    mine = [k for k in range(SPR) if (k in LOW_V) == (eng == "V")]
    return it * len(mine) + sum(1 for k in mine if k < s)


def flat(steps):
    return [e for st in steps for e in st]


def start(it, eng=None):
    if isinstance(it, int) and it == 0:
        return count(PROLOGUE, eng)
    if isinstance(it, int) and it == NKV:
        return start(NKV - 1, eng) + count(flat(side_work(False, True)), eng)
    return it * count(flat(side_work(False, False)), eng) + (count(PROLOGUE, eng) - count(EPILOGUE, eng))


SB = 3
assert all(count(w) % SB == 0 for w in (PROLOGUE, flat(side_work(True, False)), flat(side_work(False, False))))


class Steps:

    def __init__(self, widths):
        self.width = widths
        self.chunks = []
        self.first = []
        for s, w in enumerate(widths):
            self.first.append(len(self.chunks))
            for lo in range(0, w, 4):
                self.chunks.append((s, lo, min(4, w - lo)))
        self.first.append(len(self.chunks))
        self.n = len(widths)
        self.nchunks = len(self.chunks)

    def emptied(self, c, bank):
        return (c + 1 - bank) // 2


def build(nc, x, cT, wmod, w_qkvT, w_projT, b_proj, g1, g2, w_kv, w_o, router_w, router_b, w_exp, consts,
          cos_t, sin_t, out):
    ctx = ExitStack()
    with ctx:
        def sb(name, shape, dt=F32):
            return ctx.enter_context(nc.sbuf_tensor(name, shape, dt))

        def sem(name):
            return ctx.enter_context(nc.semaphore(name))

        rows_in = nc.dram_tensor("rows_in", [ETILES * P, DW], F32).ap()
        xnT_d = nc.dram_tensor("xnT_d", [B, P, 2, S], F16).ap()
        w_d = nc.dram_tensor("w_d", [HKV, P, 2, WQK], F16).ap()
        rows_out = nc.dram_tensor("rows_out", [NTOK + ETILES * P, D], F32).ap()

        psS = ctx.enter_context(nc.psum_tensor("psS", [P, 2, 1024], F32))
        psT = ctx.enter_context(nc.psum_tensor("psT", [P, 2, 512], F32))
        psO = ctx.enter_context(nc.psum_tensor("psO", [P, 2, 512], F32))
        score_banks = [psS[:, 0, 0:512], psS[:, 0, 512:1024]]
        out_banks = [psS[:, 1, 0:512], psS[:, 1, 512:1024], psO[:, 0, :]]
        side_banks = [psT[:, 0, :], psT[:, 1, :], psO[:, 1, :]]
        psTf = psT[:, :, :].rearrange("p a b -> p (a b)")

        cst = sb("cst", [P, 3 * P + 48 + 2 * ETILES + NTT])
        ident, maskf = cst[:, 0:P], cst[:, P:2 * P]
        masktf = cst[:, 2 * P:3 * P]
        mhalf, iota8 = cst[:, 3 * P:3 * P + 8], cst[:, 3 * P + 8:3 * P + 16]
        k128 = cst[:, 3 * P + 16:3 * P + 48]
        tile_no = cst[:, 3 * P + 48:3 * P + 48 + ETILES]
        token_no = cst[:, 3 * P + 48 + ETILES:3 * P + 48 + ETILES + NTT]
        empty_no = cst[:, 3 * P + 48 + ETILES + NTT:]
        trig = sb("trig", [P, 4, S])
        cosb = trig[:, 0:2, :]
        sinb = trig[:, 2:4, :]
        identh = sb("identh", [P, P], BF16)
        maskh = sb("maskh", [P, P], BF16)
        maskt = sb("maskt", [P, P], BF16)
        earlier = sb("earlier", [P, P], BF16)
        every = sb("every", [P, P], BF16)
        gb1 = sb("gb1", [P, D])
        gb2 = sb("gb2", [P, D])
        bpb = sb("bpb", [P, D])
        rbb = sb("rbb", [P, E])
        wqkv = sb("wqkv", [P, 3 * D])
        wproj = sb("wproj", [P, D])
        rw = sb("rw", [P, E])
        cs = sb("cs", [P, B])
        ce = sb("ce", [P, B])
        ones32 = sb("ones32", [P, NTT])
        mod = sb("mod", [P, B, 6 * D])

        arena = sb("arena", [P, 27 * S])
        taken = [0]

        def carve(words, restart=False):
            if restart:
                taken[0] = 0
            a = arena[:, taken[0]:taken[0] + words]
            taken[0] += words
            assert taken[0] <= 27 * S, taken[0]
            return a

        def tiles(a, n=D):
            return a.rearrange("p (j d) -> p j d", d=n)

        x_nat = tiles(carve(S))
        x_row = tiles(carve(S))
        hT = carve(S)
        qkv = carve(3 * S).rearrange("p (a n) -> p a n", a=3)
        qT, kT, va = qkv[:, 0, :], qkv[:, 1, :], tiles(qkv[:, 2, :])
        prob = carve(3 * S).rearrange("p (a n) -> p a n", a=3)
        probT = carve(3 * S).rearrange("p (a n) -> p a n", a=3)
        xn = carve(S)
        xhl = arena[:, 19 * S:20 * S].bitcast(F16).rearrange("p (a n) -> p a n", a=2)
        wraw = arena[:, 20 * S + 64:20 * S + 64 + HKV * WQK].rearrange("p (h n) -> p h n", h=HKV)
        empty = arena[:, 15 * S:15 * S + ETILES * DW].rearrange("p (t d) -> p t d", d=DW)
        wm = carve(6 * D)
        scB = carve(B * P).rearrange("p (b n) -> p b n", b=B)
        taken[0] = 23 * S
        n1, sq1, n2, sq2 = (tiles(carve(S)) for _ in range(4))
        def half16(words):
            return carve(words).bitcast(F16)

        taken[0] = 0
        qA = half16(2 * G * S // 2).rearrange("p (r g n) -> p r g n", r=2, g=G)
        qB = half16(2 * G * S // 2).rearrange("p (r g n) -> p r g n", r=2, g=G)
        kA = half16(S).rearrange("p (r n) -> p r n", r=2)
        kB = half16(S).rearrange("p (r n) -> p r n", r=2)
        kC = half16(S).rearrange("p (r n) -> p r n", r=2)
        pf = carve(2 * S).rearrange("p (r n) -> p r n", r=4)
        rp1 = carve(2 * S).rearrange("p (r n) -> p r n", r=2)
        rp2 = carve(2 * S).rearrange("p (r n) -> p r n", r=2)
        qhi = half16(S).rearrange("p (c n) -> p c n", c=2)
        qlo = half16(S).rearrange("p (c n) -> p c n", c=2)
        aT = carve(2 * S).rearrange("p (c n) -> p c n", c=2)
        xs = half16(2 * S).rearrange("p (r a n) -> p r a n", r=2, a=2)
        att = carve(4 * S).rearrange("p (r j n) -> p r j n", r=2, j=NT)
        wexp_all = carve(SLOTS * WE, True).rearrange("p (k n) -> p k n", k=SLOTS)
        exp_xs = carve(SLOTS * DW)
        m_xTs = carve(4 * P).rearrange("p (k t) -> p k t", k=4)
        m_av, m_uv, m_hv = (carve(S).rearrange("p (k n) -> p k n", k=4) for _ in range(3))
        m_yv = tiles(carve(S))
        yg = [tiles(carve(S)) for _ in range(B)]
        hfT = carve(2 * S).rearrange("p (r n) -> p r n", r=2)
        hf = carve(NTT * DW).rearrange("p (b j d) -> p b j d", b=B, j=NT)
        rsq = yg[2:4]
        NE = NTT * E
        oh, cnt, em, ea = (carve(TOPK * NE).rearrange("p (n k e) -> p n k e", k=TOPK, e=E) for _ in range(4))
        lg, v8 = (carve(NE).rearrange("p (n e) -> p n e", e=E) for _ in range(2))
        ix = carve(NE).bitcast(U32).rearrange("p (n e) -> p n e", e=E)
        ixf, sc, tk, asg, asg2 = (carve(TOPK * NTT).rearrange("p (n k) -> p n k", k=TOPK) for _ in range(5))
        row_sum = carve(B * 16).rearrange("p (b a) -> p b a", b=B)
        start_c = carve(B * 16).rearrange("p (b a) -> p b a", b=B)
        ohm, upto, past_e = (carve(NE).rearrange("p (e n) -> p e n", e=E) for _ in range(3))
        few = carve(E * 32).rearrange("p (e n) -> p e n", e=E)
        past = carve(ETILES * E).rearrange("p (t e) -> p t e", e=E)

        wk1 = sb("wk1", [P, NT, D])
        wk2 = sb("wk2", [P, NT, D])
        ph = wk2[:, :, :].rearrange("p j d -> p (j d)").bitcast(F16).rearrange("p (r n) -> p r n", r=4)
        pl = wk1[:, :, :].rearrange("p j d -> p (j d)").bitcast(F16).rearrange("p (r n) -> p r n", r=4)
        gneg = wk1[:, 0:B, :]
        st1, st2 = sb("st1", [P, 4, NT]), sb("st2", [P, 4, NT])
        rstd1, rstd2 = sb("rstd1", [P, NT]), sb("rstd2", [P, NT])
        nmax = sb("nmax", [P, 4])
        nmaxs = sb("nmaxs", [P, 4])
        sums = sb("sums", [P, NT])
        rsum = sb("rsum", [P, NT])
        Oj = sb("Oj", [P, 2, D])
        wkv = sb("wkv", [P, 2, 2, WQK], F16)
        wo = sb("wo", [P, 2, 2 * D])
        vb = sb("vb", [P, 2, NT, VW], F16)
        pmax = sb("pmax", [P, 2, NT, 2])
        hmax = sb("hmax", [P, 2, NT])
        hrow = sb("hrow", [NT, 2, P], F16)
        oinv = sb("oinv", [P, NT])
        x1 = sb("x1", [P, B, NT, D])
        hres = sb("hres", [P, B, NT, D])
        wsplit = hres[:, :, :, :].rearrange("p b j d -> p (b j d)").bitcast(F16)[:, 0:2 * HKV * WQK].rearrange(
            "p (h a n) -> p h a n", h=HKV, a=2)
        expert = sb("expert", [P, B, NT])
        wy = sb("wy", [P, B, NT])
        wx = sb("wx", [P, B, NT])
        st4 = sb("st4", [P, B, 2, NT])
        rstd4 = sb("rstd4", [P, B, NT])
        sm1, sm2 = sb("sm1", [P, NTT]), sb("sm2", [P, NTT])
        row_sum16 = sb("row_sum16", [P, B * 16], BF16)
        carry = sb("carry", [P, B, 16])
        ohm16 = sb("ohm16", [P, NTT * E], BF16)
        ntile, tend, base = (sb(n, [P, E]) for n in ("ntile", "tend", "base"))
        past7, slotf = sb("past7", [P, ETILES]), sb("slotf", [P, NTT])
        back = sb("back", [P, SLOTS], U32)
        slot = sb("slot", [P, NTT], U32)
        texp = sb("texp", [1, ETILES], I32)

        late_in = sem("late_in")
        const_in, mod_e, mod_lhs, mod_mm, mod_cp, vec = (sem("const_in"), sem("mod_e"), sem("mod_lhs"),
                                                         sem("mod_mm"), sem("mod_cp"), sem("vec"))
        xnat_in, xrow_in = sem("xnat_in"), sem("xrow_in")
        n1_V, n1_P, n1_t, n1_T = sem("norm1_vec"), sem("norm1_pool"), sem("norm1_turned"), sem("norm1_T")
        n2_V, n2_P, n2_t, n2_T = sem("norm2_vec"), sem("norm2_pool"), sem("norm2_turned"), sem("norm2_T")
        a_qkv, a_qkv_cp = sem("a_qkv"), sem("a_qkv_cp")
        a_proj, a_proj_used = sem("a_proj"), sem("a_proj_used")
        wo_in, loads_in = [sem("wo_in0"), sem("wo_in1")], [sem("loads_in0"), sem("loads_in1")]
        xn_out, xn_hi, xn_lo = sem("xn_out"), sem("xn_high"), sem("xn_low")
        wraw_in, w_hi, w_lo, w_out = sem("wraw_in"), sem("w_high"), sem("w_low"), sem("w_out")
        waited = sem("waited")
        projected, wo_used = sem("projected"), sem("wo_used")
        side_full, side_V, side_A = sem("side_full"), sem("side_read_vec"), sem("side_read_act")
        r_sum, r_hi, r_lo, qk_in = sem("rotated"), sem("high_halves"), sem("low_halves"), sem("qk_in")
        max_ready, row_in = sem("max_ready"), sem("row_in")
        b_low = sem("low_values_out")
        b_hi, lo_V, lo_P, b_read, v_hi = (sem("high_probs"), sem("low_probs_vec"), sem("low_probs_pool"),
                                          sem("outputs_read"), sem("high_values"))
        b_scores, b_exp, b_out, b_sum, b_norm, ones_set = (sem("b_scores"), sem("b_exp"), sem("b_out"), sem("b_sum"),
                                                           sem("b_norm"), sem("ones_set"))
        rt_sq = sem("rt_squares")
        rt_var, rt_rstd, rt_ready, rt_t, rt_T, rt_mm, rt_d, rt_e, rt_sum, rt_cnt = (sem(n) for n in (
            "rt_var", "rt_rstd", "rt_ready", "rt_turned", "rt_T", "rt_logits", "rt_diff", "rt_exp", "rt_row_sums", "rt_counts"))
        vecc, veck, vecr = sem("vecc"), sem("veck"), sem("vecr")

        class Att:
            def __init__(self, n):
                self.S, self.M, self.E, self.T, self.TA, self.TV, self.PV = (sem(f"{n}_{w}") for w in (
                    "scores", "max", "exp", "turned", "turned_act", "turned_vec", "pv"))
        attA = Att("a")
        a_onorm, rsum_ready, plan, final = sem("a_onorm"), sem("rsum_ready"), sem("plan"), sem("final")
        e_z, e_oh, e_rank, e_slot = sem("e_z"), sem("e_one_hot"), sem("e_ranks"), sem("e_slot")
        scat = sem("scat")
        weighted, fin_P = sem("weighted"), sem("fin_pool")
        weights_in = [sem(f"weights_in{k}") for k in range(SLOTS)]
        tile_in = [sem(f"tile_in{k}") for k in range(SLOTS)]
        m_xT, m_xTc, m_ab, m_a, m_u, m_h, m_y, m_yc = (sem(n) for n in (
            "m_xT", "m_xTc", "m_ab", "m_a", "m_u", "m_h", "m_y", "m_yc"))
        m_out = [sem(f"m_out{k}") for k in range(SLOTS)]
        gath = [sem(f"gathered{b}") for b in range(B)]
        fin, out_done, zero_in, fill_ready = sem("fin"), sem("out_done"), sem("zero_in"), sem("fill_ready")

        stepsA = Steps([NT] * NT)

        N1V, N1P, N2V, N2P = 6, 4, 9, 9
        NCONST, NLATE = 3, 9
        block = ctx.enter_context(nc.Block())

        def bc_mod(b, k):
            return mod[:, b, k * D:(k + 1) * D].unsqueeze(1).to_broadcast([P, NT, D])

        def bc_tok(stat):
            return stat.unsqueeze(2).to_broadcast([P, NT, D])

        def bc_row(v):
            return v.unsqueeze(1).to_broadcast([P, NT, D])

        def m_w(k):
            return wexp_all[:, k, :]

        def m_xs(k):
            return exp_xs[:, k * DW:k * DW + D]

        def psE(k):
            return psS[:, k // 2, (k % 2) * 512:(k % 2) * 512 + 512]

        @block.sync
        def _(sp):
            def load_nat(b):
                sp.dma_start(x_nat[:, :, :], x[b].rearrange("(j p) e -> p j e", p=P)).then_inc(xnat_in, 16)

            def load_row(b):
                sp.dma_start(x_row, x[b].rearrange("(p j) e -> p j e", p=P)).then_inc(xrow_in, 16)

            n = 0
            for dst, src in ((cs[:, :], cT), (cst[:, :], consts), (wm[:, :], wmod)):
                sp.dma_start(dst, src).then_inc(const_in, 16)
                n += 1
            load_nat(0)
            late = 0
            for dst, src in ((wqkv[:, :], w_qkvT), (wproj[:, :], w_projT), (bpb[:, :], b_proj.partition_broadcast(P)),
                             (gb1[:, :], g1.partition_broadcast(P)), (gb2[:, :], g2.partition_broadcast(P)),
                             (rbb[:, :], router_b.partition_broadcast(P)), (rw[:, :], router_w),
                             (cosb[:, :, :], cos_t), (sinb[:, :, :], sin_t)):
                sp.dma_start(dst, src).then_inc(late_in, 16)
                late += 1
            sp.dma_start(wraw, w_kv.rearrange("h p n -> p h n")).then_inc(wraw_in, 16)
            assert (n, late) == (NCONST, NLATE)

            def load_round(it, p):
                sp.dma_start(xs[:, p, :, :], xnT_d[it // HKV]).then_inc(loads_in[p], 16)
                sp.dma_start(wkv[:, p, :, :], w_d[it % HKV]).then_inc(loads_in[p], 16)

            def load_wo(it, p):
                sp.dma_start(wo[:, p, :], w_o[it % HKV]).then_inc(wo_in[p], 16)

            def spread_qk(n, p):
                def move(dst, src):
                    sp.dma_start(dst, src).then_inc(qk_in, 16)

                sp.wait_ge(r_hi, 3 * n + 1)
                sp.wait_ge(r_lo, 3 * n + 1)
                move(kA[0:HD, p, :], kB[0:HD, p, :])
                move(kA[HD:P, p, :], kC[0:HD, p, :])
                move(kC[HD:P, p, :], kB[0:HD, p, :])
                sp.wait_ge(r_hi, 3 * n + 3)
                for h in range(2):
                    src = qhi[HD * h:HD * h + HD, :, :]
                    move(qB[0:HD, p, h::2, :], src)
                    move(qA[HD:P, p, h::2, :], src)

            def spread_q_low(n, p):
                sp.wait_ge(r_lo, 3 * n + 3)
                for h in range(2):
                    sp.dma_start(qA[0:HD, p, h::2, :], qlo[HD * h:HD * h + HD, :, :]).then_inc(qk_in, 16)

            def spread_row(read, p, g):
                sp.wait_ge(side_A, read)
                sp.dma_start(qB[HD:HD + 1, p, g, :].rearrange("o (i t) -> o i t", t=P),
                             hrow[:, g % 2, :]).then_inc(row_in, 16)

            load_row(0)
            sp.wait_ge(n1_V, 3)
            load_nat(1)
            sp.wait_ge(w_lo, 1)
            sp.dma_start(w_d.rearrange("h p a n -> p h a n"), wsplit).then_inc(w_out, 16)
            for b in range(B):
                if b < B - 2:
                    sp.wait_ge(n1_V, N1V * (b + 1) + 3)
                    load_nat(b + 2)
                if b < B - 1:
                    sp.wait_ge(n2_P, N2P * b + 2)
                    load_row(b + 1)
                else:
                    sp.wait_ge(w_out, 16)
                    sp.wait_ge(xn_out, 16 * (B - 2))
                    for it in range(2):
                        load_round(it, it)
                        load_wo(it, it)
                if b > 0:
                    sp.wait_ge(xn_lo, b)
                    sp.dma_start(xnT_d[b - 1], xhl).then_inc(xn_out, 16)
            spread_qk(0, 0)
            spread_q_low(0, 0)
            sp.wait_ge(xn_lo, B)
            sp.dma_start(xnT_d[B - 1], xhl).then_inc(xn_out, 16)
            spread_row(start(0, "A"), 0, 0)
            sp.wait_ge(xn_out, 16 * B)

            def round_loads(it, p, first, last, ahead):
                if ahead:
                    sp.wait_ge(projected, it + 1)
                    load_round(it + 2, p)
                work = [e for e in flat(side_work(first, last)) if reader(e) == "A"]

                def row_of(h):
                    return start(it, "A") + work.index(("row", h)) + 1

                spread_row(row_of(0), p, 1)
                spread_row(row_of(1), p, 2)
                if not last:
                    spread_qk(it + 1, 1 - p)
                spread_row(row_of(2), p, 3)
                if not last:
                    spread_q_low(it + 1, 1 - p)
                    spread_row(row_of(3), 1 - p, 0)
                if not first and not last:
                    sp.wait_ge(wo_used, it)
                    load_wo(it + 1, 1 - p)

            round_loads(0, 0, True, False, True)
            with sp.Fori(1, NKV - 3, 2) as it:
                round_loads(it, 1, False, False, True)
                round_loads(it + 1, 0, False, False, True)
            round_loads(NKV - 3, 1, False, False, True)
            round_loads(NKV - 2, 0, False, False, False)
            round_loads(NKV - 1, 1, False, True, False)

            def load_rows(k, u):
                sp.dma_start(exp_xs[:, k * DW:(k + 1) * DW], rows_in[bass.ds(u * P, P), :]).then_inc(tile_in[k], 16)

            def expert_of(u):
                return sp.value_load(texp[0:1, bass.ds(u, 1)], min_val=0, max_val=E - 1)

            def load_weights(k, e):
                sp.dma_start(m_w(k), w_exp[bass.ds(e, 1)].rearrange("o p n -> (o p) n")).then_inc(weights_in[k], 16)

            sp.wait_ge(e_slot, 1)
            for k in range(SLOTS):
                load_weights(k, expert_of(k))
            sp.wait_ge(scat, 16 * NTT)
            for k in range(SLOTS):
                load_rows(k, k)
            for k in range(AHEAD):
                sp.wait_ge(m_xTc, k + 1)
                load_rows(k, SLOTS + k)

            def next_round(r, last):
                for k in range(SLOTS):
                    e = expert_of((r + 1) * SLOTS + k)
                    sp.wait_ge(m_y, r * SLOTS + k + 1)
                    if not (last and k + AHEAD >= SLOTS):
                        load_rows((k + AHEAD) % SLOTS, (r + 1) * SLOTS + k + AHEAD)
                    load_weights(k, e)

            with sp.Fori(0, ROUNDS - 2) as r:
                next_round(r, False)
            next_round(ROUNDS - 2, True)
            for k in range(SLOTS):
                sp.wait_ge(m_out[k], 16 * ROUNDS)
            for b in range(B):
                sp.dma_start(yg[b], rows_out[b * S:(b + 1) * S, :].rearrange("(p j) d -> p j d", p=P)).then_inc(gath[b], 16)
            for b in range(B):
                if b < 2:
                    sp.wait_ge(fin_P, b + 1)
                else:
                    sp.wait_ge(fin, b - 1)
                sp.dma_start(out[b].rearrange("(p j) e -> p j e", p=P), yg[b]).then_inc(out_done, 16)
            sp.wait_ge(out_done, 16 * B)

        @block.gpsimd
        def _(pool):
            pool.memset(ones32[:, :], 1.0)
            pool.memset(every[:, :], 1.0).then_inc(e_z, 1)
            pool.memset(scB[:, :, :], 0.0).then_inc(e_z, 1)
            pool.wait_ge(e_z, 2)
            pool.memset(empty, 0.0).then_inc(e_z, 1)
            pool.wait_ge(fill_ready, 1)
            pool.dma_start(rows_in.rearrange("(t p) d -> p t d", p=P), empty).then_inc(zero_in, 16)
            pool.wait_ge(const_in, 16 * NCONST)

            def power(dst, st):
                return pool.tensor_tensor(dst[:, :], st[:, 3, :], mhalf, ALU.pow)

            def norm1(c, part):
                if part == 0:
                    pool.wait_ge(n1_V, N1V * c + 3)
                    pool.tensor_tensor(sq1, n1, n1, ALU.mult).then_inc(n1_P, 1)
                elif part == 1:
                    pool.wait_ge(n1_V, N1V * c + 5)
                    power(rstd1, st1).then_inc(n1_P, 1)
                else:
                    pool.wait_ge(n1_V, N1V * c + 6)
                    pool.tensor_tensor(n1, n1, bc_mod(c, 1), ALU.mult).then_inc(n1_P, 1)
                    pool.wait_ge(n1_P, N1P * c + 3)
                    pool.tensor_tensor(n1, n1, bc_mod(c, 0), ALU.add).then_inc(n1_P, 1)

            def norm2(c, part):
                xb, hb = x1[:, c, :, :], hres[:, c, :, :]
                if part == 0:
                    pool.wait_ge(a_proj_used, NT * (c + 1))
                    pool.tensor_tensor(xb, xb, bc_mod(c, 2), ALU.mult).then_inc(n2_P, 1)
                    pool.wait_ge(n2_P, N2P * c + 1)
                    pool.wait_ge(xrow_in, 16 * c + 16)
                    pool.tensor_tensor(xb, xb, x_row, ALU.add).then_inc(n2_P, 1)
                elif part == 1:
                    pool.wait_ge(n2_V, N2V * c + 3)
                    pool.tensor_tensor(sq2, n2, n2, ALU.mult).then_inc(n2_P, 1)
                elif part == 2:
                    pool.wait_ge(n2_V, N2V * c + 5)
                    power(rstd2, st2).then_inc(n2_P, 1)
                elif part == 3:
                    pool.wait_ge(n2_V, N2V * c + 6)
                    pool.tensor_tensor(n2, n2, bc_mod(c, 4), ALU.mult).then_inc(n2_P, 1)
                    pool.wait_ge(n2_P, N2P * c + 5)
                    pool.tensor_tensor(hb, n2, bc_mod(c, 3), ALU.add).then_inc(n2_P, 1)
                    pool.wait_ge(n2_P, N2P * c + 6)
                    pool.tensor_tensor(sq2, hb, hb, ALU.mult).then_inc(n2_P, 1)
                elif part == 4:
                    pool.wait_ge(n2_V, N2V * c + 8)
                    power(rstd2, st2).then_inc(n2_P, 1)
                else:
                    pool.wait_ge(n2_V, N2V * c + 9)
                    pool.tensor_tensor(n2, n2, bc_row(gb1[:, :]), ALU.mult).then_inc(n2_P, 1)

            def norms(b, first, last):
                for which, part in ((2, 0), (1, 0), (2, 1), (1, 1), (2, 2), (1, 2), (2, 3), (2, 4), (2, 5)):
                    if which == 1 and not last:
                        norm1(b + 1, part)
                    if which == 2 and not first:
                        norm2(b - 1, part)
                    if (which, part) == (1, 0) and b >= 2:
                        input2_low(b - 2)

            def input2_low(c):
                pool.wait_ge(xn_hi, c + 1)
                pool.tensor_tensor(xhl[:, 1, :], xn, xhl[:, 0, :], ALU.subtract).then_inc(xn_lo, 1)

            norm1(0, 0)
            norm1(0, 1)
            pool.wait_ge(mod_cp, B + 1)
            norm1(0, 2)
            pool.wait_ge(zero_in, 16)
            pool.wait_ge(late_in, 16 * NLATE)
            pool.wait_ge(w_hi, 1)
            pool.tensor_tensor(wsplit[:, :, 1, :], wraw, wsplit[:, :, 0, :], ALU.subtract).then_inc(w_lo, 1)
            norms(0, True, False)
            pool.wait_ge(w_out, 16)
            for b in range(1, B):
                norms(b, False, b == B - 1)

            def rotated(c, n, base, p):
                rows = HD if c == 0 else P
                t = (0, 1, 0)[c]
                last = max(VEC_AT[e] for e in PROJ_V if (e[0] == "k" if c == 0 else e[0] in "qr" and e[1] == c - 1))
                pool.wait_ge(side_V, base + last + 1)
                pool.tensor_tensor(rp1[0:rows, t, :], rp1[0:rows, t, :], rp2[0:rows, t, :], ALU.add).then_inc(r_sum, 1)

            def low_half(c, n, p):
                t = (0, 1, 0)[c]
                pool.wait_ge(r_hi, 3 * n + c + 1)
                if c == 0:
                    pool.tensor_tensor(kC[0:HD, p, :], rp1[0:HD, t, :], kB[0:HD, p, :], ALU.subtract).then_inc(r_lo, 1)
                else:
                    pool.tensor_tensor(qlo[:, c - 1, :], rp1[:, t, :], qhi[:, c - 1, :], ALU.subtract).then_inc(r_lo, 1)

            PROJ_V = [e for e in PROJ.values() if e[0] in "kqr"]
            VEC_AT = {e: i for i, e in enumerate(x for x in PROLOGUE if reader(x) == "V")}
            norm2(B - 1, 0)
            pool.wait_ge(n2_P, N2P * (B - 1) + 2)
            pool.memset(kB[HD:HD + 1, :, :], 1.0).then_inc(ones_set, 1)
            pool.wait_ge(ones_set, 3)
            norm2(B - 1, 1)
            input2_low(B - 2)
            rotated(0, 0, 0, 0)
            norm2(B - 1, 2)
            low_half(0, 0, 0)
            norm2(B - 1, 3)
            rotated(1, 0, 0, 0)
            norm2(B - 1, 4)
            low_half(1, 0, 0)
            rotated(2, 0, 0, 0)
            norm2(B - 1, 5)
            low_half(2, 0, 0)
            input2_low(B - 1)

            def pool_round(it, p, first, last):
                VEC_AT.clear()
                VEC_AT.update({e: i for i, e in enumerate(x for x in flat(side_work(first, last)) if reader(x) == "V")})
                for s in range(SPR):
                    if s not in LOW_V:
                        pool.wait_ge(b_hi, it * SPR + s + 1)
                        pool.tensor_tensor(pl[:, s % 4, :], pf[:, s % 4, :], ph[:, s % 4, :], ALU.subtract).then_inc(lo_P, 1)
                    if not last:
                        if s in SUM_AT:
                            rotated(SUM_AT[s], it + 1, start(it, "V"), 1 - p)
                        if s in LOW_AT:
                            low_half(LOW_AT[s], it + 1, 1 - p)

            pool_round(0, 0, True, False)
            with pool.Fori(1, NKV - 1, 2) as it:
                pool_round(it, 1, False, False)
                pool_round(it + 1, 0, False, False)
            pool_round(NKV - 1, 1, False, True)
            for k in range(2):
                if k == 0:
                    pool.wait_ge(side_V, start(NKV, "V"))
                else:
                    pool.wait_ge(side_V, start(NKV, "V") + count(EPILOGUE, "V"))
                src = hres[:, 2 * k + 1, :, :]
                pool.tensor_tensor(rsq[k], src, src, ALU.mult).then_inc(rt_sq, 1)
            pool.wait_ge(rt_var, 1)
            for b in range(B):
                pool.tensor_tensor(rstd4[:, b, :], st4[:, b, 1, :], mhalf, ALU.pow).then_inc(rt_rstd, 1)

            pool.wait_ge(e_slot, 1)
            pool.wait_ge(zero_in, 16)
            hff = hf[:, :, :, :].rearrange("p b j d -> p (b j) d")
            for t in range(NTT):
                pool.indirect_dma_start(rows_in, bass.IndirectOffsetOnAxis(slot[:, t:t + 1], 0), hff[:, t, :], None
                                        ).then_inc(scat, 16)
            with pool.Fori(0, ROUNDS) as rr:
                for k in range(SLOTS):
                    pool.wait_ge(m_yc, rr * SLOTS + k + 1)
                    pool.sem_inc(waited, 1)
                    pool.indirect_dma_start(rows_out, bass.IndirectOffsetOnAxis(back[:, k:k + 1], 0), m_yv[:, k, :], None
                                            ).then_inc(m_out[k], 16)

            for b in range(2):
                pool.wait_ge(weighted, b + 1)
                pool.tensor_tensor(yg[b], yg[b], hres[:, b, :, :], ALU.add).then_inc(fin_P, 1)

        @block.scalar
        def _(act):
            def attend(s, a, it, scale):
                def turned(st_, c):
                    sx, lo, n = s.chunks[c]
                    act.wait_ge(a.T, it * s.nchunks + c + 1)
                    act.activation(probT[:, sx % 3, lo * P:(lo + n) * P], psT[:, 0, 0:n * P], ACT.Copy).then_inc(a.TA, 1)

                done = 0
                for k in range(s.n + 2):
                    if k < s.n:
                        act.wait_ge(a.M, it * s.n + k + 1)
                        w = s.width[k] * P
                        act.activation(prob[:, k % 3, 0:w], psS[:, k % 2, 0:w], ACT.Exp,
                                       bias=(nmax if scale == 1.0 else nmaxs)[:, k % 4:k % 4 + 1], scale=scale,
                                       accum_out=sums[:, k:k + 1]).then_inc(a.E, 1)
                    if k >= 2:
                        for c in range(s.first[k - 2], s.first[k - 1]):
                            if c % 2 == 0:
                                turned(k - 2, c)

            act.wait_ge(const_in, 16 * NCONST)
            act.activation(ce[:, :], cs[:, :], ACT.Exp, scale=-1.0).then_inc(mod_e, 1)

            def qkv_in(b):
                act.wait_ge(n1_t, b + 1)
                act.activation(hT, psS[:, 0, :], ACT.Copy).then_inc(n1_T, 1)
                act.wait_ge(a_qkv, 3 * b + 1)
                act.activation(qT, psS[:, 1, :], ACT.Copy).then_inc(a_qkv_cp, 1)
                act.wait_ge(a_qkv, 3 * b + 2)
                act.activation(kT, psS[:, 0, :], ACT.Copy).then_inc(a_qkv_cp, 1)
                act.wait_ge(a_qkv, 3 * b + 3)
                act.activation(va.rearrange("p j d -> p (j d)"), psTf, ACT.Copy).then_inc(a_qkv_cp, 1)

            def input2(c, stored, bank=psO[:, :, :].rearrange("d a n -> d (a n)")):
                act.wait_ge(n2_t, c + 1)
                if stored:
                    act.wait_ge(xn_out, 16 * c)
                    act.wait_ge(xn_lo, c)
                act.activation(xn.rearrange("d (p j) -> d j p", j=NT),
                               bank.rearrange("d (j p) -> d j p", p=P),
                               ACT.Copy).then_inc(n2_T, 1)
                act.wait_ge(n2_T, c + 1)
                act.activation(xhl[:, 0, :], xn, ACT.Copy).then_inc(xn_hi, 1)

            act.wait_ge(wraw_in, 16)
            act.activation(wsplit[:, :, 0, :], wraw, ACT.Copy).then_inc(w_hi, 1)
            qkv_in(0)
            attend(stepsA, attA, 0, A_SCALE)
            qkv_in(1)
            for b in range(1, B - 1):
                attend(stepsA, attA, b, A_SCALE)
                qkv_in(b + 1)
                input2(b - 1, b > 1)
            attend(stepsA, attA, B - 1, A_SCALE)
            input2(B - 2, True)
            input2(B - 1, True, psS[:, 0, :])

            def read(e, bank, full, p):
                act.wait_ge(side_full, full)
                src = side_banks[bank]
                if e[0] == "turn":
                    c, h = divmod(e[1], 2)
                    ins = act.activation(aT[:, c, h * 512:(h + 1) * 512], src, ACT.Copy)
                else:
                    g = (e[1] + 1) % 2
                    ins = act.activation(hrow[:, g, :], src[0:NT, 0:P], ACT.Copy)
                ins.then_inc(side_A, 1)

            p0 = list(PROLOGUE)
            for i, e in enumerate(p0):
                if reader(e) == "A":
                    read(e, i % SB, i + 1, 0)

            def high_probs(it, s):
                act.wait_ge(b_exp, it * SPR + s + 1)
                act.activation(ph[:, s % 4, :], pf[:, s % 4, :], ACT.Copy).then_inc(b_hi, 1)

            def low_outputs(it, p, g, bank):
                m = len(OBANK[bank])
                act.wait_ge(b_out, 3 * (it * G + g) + bank + 1)
                o = out_banks[bank][:, 0:m * VW].rearrange("p (i d) -> p i d", d=VW)
                act.activation(att[:, p, 3 * bank:3 * bank + m, g * HD:(g + 1) * HD], o[:, :, HD + 2:VW],
                               ACT.Copy).then_inc(b_low, 1)

            def act_round(it, p, first, last):
                steps = side_work(first, last)
                i = 0
                for s in range(SPR):
                    act.wait_ge(b_scores, it * SPR + s + 1)
                    act.activation(pf[:, s % 4, :], score_banks[s % 2], ACT.Exp).then_inc(b_exp, 1)
                    if s > 0:
                        high_probs(it, s - 1)
                    elif not first:
                        high_probs(it - 1, SPR - 1)
                    for e in steps[s]:
                        if reader(e) == "A":
                            read(e, i % SB, start(it) + i + 1, 1 - p)
                        i += 1
                    h, c = divmod(s, SPH)
                    if c == 6:
                        low_outputs(it, p, h, 0)
                    elif c in (0, 3) and h > 0:
                        low_outputs(it, p, h - 1, 1 + c // 3)
                    elif c in (0, 3) and not first:
                        low_outputs(it - 1, 1 - p, G - 1, 1 + c // 3)

            act.wait_ge(xn_out, 16 * B)
            act_round(0, 0, True, False)
            with act.Fori(1, NKV - 1, 2) as it:
                act_round(it, 1, False, False)
                act_round(it + 1, 0, False, False)
            act_round(NKV - 1, 1, False, True)
            high_probs(NKV - 1, SPR - 1)
            for bank in (1, 2):
                low_outputs(NKV - 1, 1, G - 1, bank)
            for i, e in enumerate(EPILOGUE):
                if reader(e) == "A":
                    read(e, i % SB, start(NKV) + i + 1, 0)

            for b in range(B):
                act.wait_ge(rt_t, b + 1)
                if b >= 2:
                    act.wait_ge(rt_mm, b - 1)
                act.activation(hfT[:, b % 2, :], psS[:, b % 2, :], ACT.Copy).then_inc(rt_T, 1)
            act.wait_ge(rt_d, 1)
            act.activation(sm2[:, :], sm1[:, :], ACT.Exp).then_inc(rt_e, 1)

            with act.Fori(0, ROUNDS) as rr:
                for k in range(SLOTS):
                    act.wait_ge(m_u, rr * SLOTS + k + 1)
                    act.activation(m_hv[:, k % 4, :], m_uv[:, k % 4, :], ACT.Gelu).then_inc(m_h, 1)

        @block.tensor
        def _(pe):
            def attend(s, a, it, scores, values):
                def turn(k):
                    pe.wait_ge(a.E, it * s.n + k + 1)
                    for c in range(s.first[k], s.first[k + 1]):
                        _, lo, n = s.chunks[c]
                        if c >= 2:
                            half = s.emptied(c, c % 2)
                            cnt = s.emptied(s.nchunks, c % 2)
                            pe.wait_ge((a.TA, a.TV)[c % 2], it * cnt + half)
                        for j in range(n):
                            last = pe.transpose(psT[:, c % 2, j * P:(j + 1) * P],
                                                prob[:, k % 3, (lo + j) * P:(lo + j + 1) * P], ident)
                        last.then_inc(a.T, 1)

                def pv(k):
                    cl = s.first[k + 1]
                    for q in range(2):
                        cnt = s.emptied(s.nchunks, q)
                        n = s.emptied(cl, q)
                        if n:
                            pe.wait_ge((a.TA, a.TV)[q], it * cnt + n)
                    values(k)

                for k in range(s.n + 3):
                    if k < s.n:
                        if k >= 2:
                            pe.wait_ge(a.E, it * s.n + k - 1)
                        scores(k).then_inc(a.S, 1)
                    if 2 <= k < s.n + 2:
                        turn(k - 2)
                    if k >= 3:
                        pv(k - 3)

            pe.wait_ge(const_in, 16 * NCONST)
            for b in range(B):
                pe.wait_ge(mod_lhs, b + 1)
                if b >= 2:
                    pe.wait_ge(mod_cp, b - 1)
                for h in range(2):
                    mm = pe.matmul(psS[:, b % 2, h * 512:h * 512 + 3 * D], scB[:, b, :], wm[:, h * 3 * D:(h + 1) * 3 * D],
                                   start=True, stop=True)
                mm.then_inc(mod_mm, 1)

            def qkv_of(b):
                pe.wait_ge(n1_P, N1P * (b + 1))
                for j in range(NT):
                    last = pe.transpose(psS[:, 0, j * P:(j + 1) * P], n1[:, j, :], ident)
                last.then_inc(n1_t, 1)
                pe.wait_ge(n1_T, b + 1)
                for k, dst in ((0, psS[:, 1, :]), (1, psS[:, 0, :])):
                    for h in range(2):
                        mm = pe.matmul(dst[:, h * 512:(h + 1) * 512], wqkv[:, k * D:(k + 1) * D], hT[:, h * 512:(h + 1) * 512],
                                       start=True, stop=True)
                    mm.then_inc(a_qkv, 1)
                for j in range(NT):
                    mm = pe.matmul(psTf[:, j * P:(j + 1) * P], hT[:, j * P:(j + 1) * P], wqkv[:, 2 * D:3 * D], start=True, stop=True)
                mm.then_inc(a_qkv, 1)

            def turn_input2(c, used, bank=None):
                pe.wait_ge(a_proj_used, used)
                pe.wait_ge(n2_P, N2P * (c + 1))
                for j in range(NT):
                    dst = psO[:, j // 4, (j % 4) * P:(j % 4 + 1) * P] if bank is None else bank[:, j * P:(j + 1) * P]
                    last = pe.transpose(dst, n2[:, j, :], ident)
                last.then_inc(n2_t, 1)
                pe.wait_ge(n2_T, c + 1)

            def attention(b):
                pe.wait_ge(a_qkv_cp, 3 * b + 3)

                def scoresA(i):
                    for h in range(2):
                        mm = pe.matmul(psS[:, i % 2, h * 512:(h + 1) * 512], qT[:, i * P:(i + 1) * P],
                                       kT[:, h * 512:(h + 1) * 512], start=True, stop=True)
                    return mm

                def projA(i):
                    pe.wait_ge(a_onorm, b * NT + i + 1)
                    pe.matmul(psO[:, i % 2, 256:256 + D], Oj[:, i % 2, :], wproj[:, :], start=True, stop=True).then_inc(a_proj, 1)

                def valuesA(i):
                    if i >= 2:
                        pe.wait_ge(a_proj_used, b * NT + i - 1)
                    for j in range(NT):
                        mm = pe.matmul(psO[:, i % 2, 0:D], probT[:, i % 3, j * P:(j + 1) * P], va[:, j, :],
                                       start=(j == 0), stop=(j == NT - 1))
                    mm.then_inc(attA.PV, 1)
                    if i >= 1:
                        projA(i - 1)

                attend(stepsA, attA, b, scoresA, valuesA)
                projA(NT - 1)

            pe.wait_ge(late_in, 16 * NLATE)
            qkv_of(0)
            attention(0)
            qkv_of(1)
            with pe.Fori(1, B - 1) as b:
                attention(b)
                qkv_of(b + 1)
                turn_input2(b - 1, NT * (b + 1))
            attention(B - 1)
            turn_input2(B - 2, NT * B)

            def fill(e, bank, p, n):
                dst = side_banks[bank]
                kind = e[0]
                if kind in "kqrv":
                    if e == ("k", 0):
                        pe.wait_ge(loads_in[p], 32 * (n // 2) + 32)
                    halves = ((0, 0), (0, 1), (1, 0))
                    if kind == "v":
                        for j in range(NT):
                            for k, (a, c) in enumerate(halves):
                                mm = pe.matmul(dst[:, j * HD:(j + 1) * HD], xs[:, p, a, j * P:(j + 1) * P],
                                               wkv[:, p, c, W_V:W_V + HD], start=(k == 0), stop=(k == 2))
                        return mm
                    h = e[-1]
                    w0 = W_K if kind == "k" else (2 * e[1] + (kind == "r")) * P
                    for k, (c, a) in enumerate(halves):
                        mm = pe.matmul(dst, wkv[:, p, c, w0:w0 + P], xs[:, p, a, h * 512:(h + 1) * 512],
                                       start=(k == 0), stop=(k == 2))
                    return mm
                if kind == "max":
                    g, i, h = (e[1] + 1) % G, e[2], e[3]
                    if g == 0 and (i, h) == PIECES[0]:
                        pe.wait_ge(qk_in, 144 * n + 144)
                    w = min(4, i + 1 - 4 * h) * P
                    diag = h == i // 4
                    mm = pe.matmul(dst[:, 0:w], qA[:, p, g, i * P:(i + 1) * P], kC[:, p, h * 512:h * 512 + w],
                                   start=True, stop=not diag)
                    if diag:
                        mm = pe.matmul(dst[:, w - P:w], identh[:, :], maskh[:, :], start=False, stop=True)
                    return mm
                if kind == "row":
                    g = (e[1] + 1) % G
                    pe.wait_ge(max_ready, n * G + g + 1)
                    return pe.transpose(dst[0:NT, 0:P], hmax[:, g % 2, :], ident)
                if kind == "turn":
                    c, h = divmod(e[1], 2)
                    for i in range(4):
                        mm = pe.transpose(dst[:, i * P:(i + 1) * P], att[:, p, 4 * h + i, c * P:(c + 1) * P], ident)
                    return mm
                for j in range(4):
                    for c in range(2):
                        mm = pe.matmul(dst[:, j * D:(j + 1) * D],
                                       aT[:, c, :].rearrange("f (p j) -> f j p", j=NT)[:, 4 * e[1] + j, :],
                                       wo[:, p, c * D:(c + 1) * D], start=(c == 0), stop=(c == 1))
                return mm

            def before(entries, i, base):
                if i < SB:
                    for eng, sm in (("V", side_V), ("A", side_A)):
                        if not (isinstance(base[eng], int) and base[eng] == 0):
                            pe.wait_ge(sm, base[eng])
                    return
                eng = reader(entries[i - SB])
                pe.wait_ge({"V": side_V, "A": side_A}[eng], base[eng] + count(entries[:i - SB + 1], eng))

            def side(entries, i, base, p, it):
                e = entries[i]
                before(entries, i, base)
                bank = i % SB
                nxt = e[0] in ("k", "q", "r", "v") or (e[0] in ("max", "row") and e[1] == G - 1)
                prev = e[0] in ("turn", "out")
                if prev:
                    if e == ("turn", 0):
                        pe.wait_ge(b_norm, 3 * G * it)
                        pe.wait_ge(wo_in[1 - p], 16 * ((it + 1) // 2))
                    if e == ("out", 0):
                        k = entries.index(("turn", 3))
                        for eng, sm in (("V", side_V), ("A", side_A)):
                            pe.wait_ge(sm, base[eng] + count(entries[:k + 1], eng))
                mm = fill(e, bank, (1 - p) if (nxt or prev) else p, it + 1 if nxt else it)
                mm.then_inc(side_full, 1)
                if e == ("r", 1, 1):
                    pe.wait_ge(side_full, base["n"] + i + 1)
                    pe.sem_inc(projected, 1)
                if e == ("out", 1):
                    pe.wait_ge(side_full, base["n"] + i + 1)
                    pe.sem_inc(wo_used, 1)

            def scoresB(it, p, s):
                g, c = divmod(s, SPH)
                if c == 0:
                    pe.wait_ge(row_in, 16 * (it * G + g) + 16)
                for j, i0, n, at in segments(c):
                    dst = score_banks[s % 2][:, at * P:(at + n) * P]
                    diag = i0 == j
                    pe.matmul(dst, kA[:, p, j * P:(j + 1) * P], qA[:, p, g, i0 * P:(i0 + n) * P], start=True, stop=False)
                    mm = pe.matmul(dst, kB[0:HD + 1, p, j * P:(j + 1) * P], qB[0:HD + 1, p, g, i0 * P:(i0 + n) * P],
                                   start=False, stop=not diag)
                    if diag:
                        mm = pe.matmul(dst[:, 0:P], identh[:, :], maskt[:, :], start=False, stop=True)
                mm.then_inc(b_scores, 1)

            def values_parts(it, p, s):
                g, c = divmod(s, SPH)

                def part(lo, hi):
                    for n in range(lo, hi):
                        at = 4 * c + n
                        j, i = BLOCKS[at]
                        bank = i // 3
                        first = BLOCKS[at - 1][1] // 3 != bank or at == 0
                        last = at == len(BLOCKS) - 1 or BLOCKS[at + 1][1] // 3 != bank
                        if first and not (isinstance(it, int) and it == 0 and g == 0):
                            pe.wait_ge(b_read, 3 * (it * G + g) - 2 + bank)
                        dst = out_banks[bank][:, (i % 3) * VW:(i % 3 + 1) * VW]
                        pe.matmul(dst, ph[:, s % 4, n * P:(n + 1) * P], vb[:, p, j, :],
                                  start=first, stop=False, skip_group_check=True)
                        mm = pe.matmul(dst[:, 0:HD + 1], pl[:, s % 4, n * P:(n + 1) * P], vb[:, p, j, 0:HD + 1],
                                       start=False, stop=last, skip_group_check=True)
                        if last:
                            mm.then_inc(b_out, 1)

                def first_part():
                    eng = "V" if s in LOW_V else "P"
                    pe.wait_ge({"V": lo_V, "P": lo_P}[eng], lows(it, s, eng) + 1)
                    part(0, 2)

                return [first_part, lambda: part(2, 4)]

            zero = {"V": 0, "A": 0, "n": 0}
            for i in range(len(PROLOGUE)):
                if PROLOGUE[i][0] == "max" and PROLOGUE[i - 1][0] != "max":
                    turn_input2(B - 1, NT * B, psS[:, 0, :])
                    pe.wait_ge(ones_set, 3)
                side(PROLOGUE, i, zero, 1, -1)

            def pe_round(it, p, first, last):
                steps = side_work(first, last)
                work = flat(steps)
                base = {"V": start(it, "V"), "A": start(it, "A"), "n": start(it)}
                i = 0
                for s in range(SPR):
                    if s >= 2 or not first:
                        pe.wait_ge(b_exp, it * SPR + s - 1)
                    scoresB(it, p, s)
                    n = len(steps[s])
                    todo = [lambda k=k: side(work, k, base, p, it) for k in range(i, i + n)]
                    i += n
                    parts = []
                    if s >= 3:
                        parts = values_parts(it, p, s - 3)
                    elif not first:
                        parts = values_parts(it - 1, 1 - p, SPR + s - 3)
                    if n == 1:
                        order = parts[0:1] + parts[1:2] + todo
                    else:
                        order = todo[0:1] + parts[0:1] + todo[1:2] + parts[1:2] + todo[2:]
                    for f in order:
                        f()

            pe_round(0, 0, True, False)
            with pe.Fori(1, NKV - 1, 2) as it:
                pe_round(it, 1, False, False)
                pe_round(it + 1, 0, False, False)
            pe_round(NKV - 1, 1, False, True)
            for s in range(SPR - 3, SPR):
                for f in values_parts(NKV - 1, 1, s):
                    f()
            base = {"V": start(NKV, "V"), "A": start(NKV, "A"), "n": start(NKV)}
            for i in range(len(EPILOGUE)):
                side(EPILOGUE, i, base, 0, NKV)

            def turn_rows(b):
                pe.wait_ge(rt_ready, b + 1)
                if b >= 2:
                    pe.wait_ge(rt_T, b - 1)
                for j in range(NT):
                    last = pe.transpose(psS[:, b % 2, j * P:(j + 1) * P], hf[:, b, j, 0:D], ident)
                last.then_inc(rt_t, 1)

            turn_rows(0)
            for b in range(B):
                if b < B - 1:
                    turn_rows(b + 1)
                pe.wait_ge(rt_T, b + 1)
                for j in range(NT):
                    n = b * NT + j
                    mm = pe.matmul(psT[:, 0, n * E:(n + 1) * E], hfT[:, b % 2, j * P:(j + 1) * P], rw[:, :],
                                   start=True, stop=True)
                mm.then_inc(rt_mm, 1)
            pe.wait_ge(rt_sum, 1)
            pe.matmul(psO[:, 0, 0:B * 16], earlier[:, :], row_sum16[:, :], start=True, stop=True)
            pe.matmul(psO[:, 1, 0:B * 16], every[:, :], row_sum16[:, :], start=True, stop=True).then_inc(rt_cnt, 1)
            pe.wait_ge(e_oh, 1)
            pe.matmul(psS[:, 0, 0:NE], earlier[:, :], ohm16[:, :], start=True, stop=True)
            pe.matmul(psS[:, 1, 0:NE], every[:, :], ohm16[:, :], start=True, stop=True).then_inc(e_rank, 1)
            pe.wait_ge(e_slot, 1)

            def step(rr, k, ahead, behind):
                t = rr * SLOTS + k
                if ahead:
                    k2 = (k + 2) % SLOTS
                    pe.wait_ge(tile_in[k2], 16 * (rr + (k + 2) // SLOTS + 1))
                    pe.wait_ge(m_xTc, t + 1)
                    pe.transpose(psT[:, k % 2, 0:P], m_xs(k2), ident).then_inc(m_xT, 1)
                else:
                    pe.wait_ge(m_xTc, t + 1)
                pe.wait_ge(weights_in[k], 16 * (rr + 1))
                if behind or k >= 4:
                    pe.wait_ge(m_u, t - 3)
                for c in range(4):
                    mm = pe.matmul(psE(k % 4)[:, c * P:(c + 1) * P], m_w(k)[:, c * P:(c + 1) * P], m_xTs[:, k % 4, :],
                                   start=True, stop=True)
                mm.then_inc(m_ab, 1)
                if behind or k >= 3:
                    second(t - 3, (k - 3) % SLOTS, behind or k >= 5)

            def second(t, k, reused):
                pe.wait_ge(m_h, t + 1)
                if reused:
                    pe.wait_ge(m_yc, t - 1)
                for c in range(2):
                    mm = pe.matmul(psO[:, k % 2, 0:P], m_hv[:, k % 4, c * P:(c + 1) * P],
                                   m_w(k)[:, 2 * HID + c * D:2 * HID + (c + 1) * D], start=(c == 0), stop=(c == 1))
                mm.then_inc(m_y, 1)

            for k in range(2):
                pe.wait_ge(tile_in[k], 16)
                pe.transpose(psT[:, k, 0:P], m_xs(k), ident).then_inc(m_xT, 1)
            for k in range(SLOTS):
                step(0, k, True, False)
            with pe.Fori(1, ROUNDS - 1) as rr:
                for k in range(SLOTS):
                    step(rr, k, True, True)
            for k in range(SLOTS):
                step(ROUNDS - 1, k, k < SLOTS - 2, True)
            for t in range(ETILES - 3, ETILES):
                second(t, t % SLOTS, True)

        @block.vector
        def _(v):
            class Chain:
                def __init__(self, s, start, per):
                    self.s, self.start, self.n, self.per = s, start, 0, per

                def __call__(self, ins):
                    self.n += 1
                    ins.then_inc(self.s, 1)
                    v.wait_ge(self.s, self.start + self.n)

                def end(self):
                    assert self.n == self.per, (self.n, self.per)

            def attend(s, a, it, scale, norm):
                for k in range(s.n + 2):
                    if k < s.n:
                        w = s.width[k] * P
                        v.wait_ge(a.S, it * s.n + k + 1)
                        ins = v.tensor_reduce(nmax[:, k % 4:k % 4 + 1], psS[:, k % 2, 0:w], AX.X, ALU.max, negate=True)
                        if scale != 1.0:
                            ins.then_inc(vecr, 1)
                            v.wait_ge(vecr, it * s.n + k + 1)
                            ins = v.tensor_scalar(nmaxs[:, k % 4:k % 4 + 1], nmax[:, k % 4:k % 4 + 1], scale, None, ALU.mult)
                        ins.then_inc(a.M, 1)
                    if k >= 2:
                        for c in range(s.first[k - 2], s.first[k - 1]):
                            if c % 2 == 1:
                                sx, lo, n = s.chunks[c]
                                v.wait_ge(a.T, it * s.nchunks + c + 1)
                                v.tensor_copy(probT[:, sx % 3, lo * P:(lo + n) * P], psT[:, 1, 0:n * P]).then_inc(a.TV, 1)
                    norm(k)

            def centred(n, per, c, src, dst, st, part):
                at = per * c
                if part == 0:
                    v.tensor_reduce(st[:, 0, :], src, AX.X, ALU.add).then_inc(n, 1)
                    v.wait_ge(n, at + 1)
                    v.tensor_scalar(st[:, 1, :], st[:, 0, :], -1.0 / D, None, ALU.mult).then_inc(n, 1)
                else:
                    v.wait_ge(n, at + 2)
                    v.tensor_tensor(dst, src, bc_tok(st[:, 1, :]), ALU.add).then_inc(n, 1)

            def variance(n, at, sq, st, eps):
                v.tensor_reduce(st[:, 2, :], sq, AX.X, ALU.add).then_inc(n, 1)
                v.wait_ge(n, at + 1)
                v.tensor_scalar(st[:, 3, :], st[:, 2, :], 1.0 / D, eps, ALU.mult, ALU.add).then_inc(n, 1)

            def norm1(c, part):
                if part < 2:
                    if part == 0:
                        v.wait_ge(xnat_in, 16 * c + 16)
                    centred(n1_V, N1V, c, x_nat, n1, st1, part)
                elif part == 2:
                    v.wait_ge(n1_P, N1P * c + 1)
                    variance(n1_V, N1V * c + 3, sq1, st1, LN_EPS)
                else:
                    v.wait_ge(n1_P, N1P * c + 2)
                    v.tensor_tensor(n1, n1, bc_tok(rstd1[:, :]), ALU.mult).then_inc(n1_V, 1)

            def norm2(c, part):
                if part < 2:
                    if part == 0:
                        v.wait_ge(n2_P, N2P * c + 2)
                    centred(n2_V, N2V, c, x1[:, c, :, :], n2, st2, part)
                elif part == 2:
                    v.wait_ge(n2_P, N2P * c + 3)
                    variance(n2_V, N2V * c + 3, sq2, st2, LN_EPS)
                elif part == 3:
                    v.wait_ge(n2_P, N2P * c + 4)
                    v.tensor_tensor(n2, n2, bc_tok(rstd2[:, :]), ALU.mult).then_inc(n2_V, 1)
                elif part == 4:
                    v.wait_ge(n2_P, N2P * c + 7)
                    variance(n2_V, N2V * c + 6, sq2, st2, RMS_EPS)
                else:
                    v.wait_ge(n2_P, N2P * c + 8)
                    v.tensor_tensor(n2, hres[:, c, :, :], bc_tok(rstd2[:, :]), ALU.mult).then_inc(n2_V, 1)

            NORM_AT = {0: (1, 0), 1: (1, 1), 2: (2, 0), 3: (2, 1), 4: (1, 2), 5: (2, 2), 6: (1, 3), 7: (2, 3)}

            def attention(b, first, last):
                def normA(k):
                    i = k - 3
                    if 0 <= i < NT:
                        v.wait_ge(attA.PV, b * NT + i + 1)
                        v.reciprocal(rsum[:, i:i + 1], sums[:, i:i + 1]).then_inc(veck, 1)
                        v.wait_ge(veck, b * NT + i + 1)
                        v.tensor_scalar(Oj[:, i % 2, :], psO[:, i % 2, 0:D], rsum[:, i:i + 1], None, ALU.mult).then_inc(a_onorm, 1)
                    i = k - 4
                    if 0 <= i < NT:
                        v.wait_ge(a_proj, b * NT + i + 1)
                        v.tensor_tensor(x1[:, b, i, :], psO[:, i % 2, 256:256 + D], bpb[:, :], ALU.add).then_inc(a_proj_used, 1)
                    which, part = NORM_AT.get(k, (0, 0))
                    if which == 1 and not last:
                        norm1(b + 1, part)
                    if which == 2 and not first:
                        norm2(b - 1, part)

                attend(stepsA, attA, b, A_SCALE, normA)
                normA(NT + 2)
                normA(NT + 3)
                if not first:
                    norm2(b - 1, 4)
                    norm2(b - 1, 5)

            NVEC = 11
            ch = Chain(vec, 0, NVEC)
            v.wait_ge(const_in, 16 * NCONST)
            v.wait_ge(mod_e, 1)
            ch(v.tensor_scalar(ce[:, :], ce[:, :], 1.0, None, ALU.add))
            ch(v.reciprocal(ce[:, :], ce[:, :]))
            ch(v.tensor_tensor(cs[:, :], cs[:, :], ce[:, :], ALU.mult))
            v.wait_ge(e_z, 2)
            for b in range(B):
                v.tensor_scalar(scB[:, b, :], scB[:, b, :], cs[:, b:b + 1], None, ALU.add).then_inc(mod_lhs, 1)
            norm1(0, 0)
            norm1(0, 1)
            v.tensor_copy(identh[:, :], ident)
            v.tensor_copy(maskh[:, :], maskf)
            v.tensor_copy(maskt[:, :], masktf)
            v.tensor_scalar(earlier[:, :], maskf, 0.0, None, ALU.is_lt)
            v.memset(vb[:, :, :, HD], 1.0).then_inc(ones_set, 1)
            v.memset(vb[:, :, :, HD + 1], 0.0).then_inc(ones_set, 1)
            v.wait_ge(e_z, 3)
            v.tensor_copy(empty[:, :, D], empty_no).then_inc(fill_ready, 1)
            norm1(0, 2)
            for b in range(B):
                v.wait_ge(mod_mm, b + 1)
                v.tensor_copy(mod[:, b, :].rearrange("p (h n) -> p h n", h=2),
                              psS[:, b % 2, :].rearrange("p (h n) -> p h n", h=2)[:, :, 0:3 * D]).then_inc(mod_cp, 1)
            norm1(0, 3)
            v.wait_ge(mod_cp, B)
            for k in (2, 5):
                gate = mod[:, :, k * D:(k + 1) * D]
                ch(v.tensor_scalar(gneg[:, :, :], gate, 0.0, 2.0, ALU.is_ge, ALU.mult))
                ch(v.tensor_scalar(scB[:, :, :], gate, -1.0, 0.25, ALU.mult, ALU.max))
                ch(v.tensor_tensor(scB[:, :, :], scB[:, :, :], gate, ALU.max))
                ch(v.scalar_tensor_tensor(gate, gneg[:, :, :], -1.0, scB[:, :, :], ALU.add, ALU.mult))
            ch.end()
            for k in (1, 4):
                ins = v.tensor_scalar(mod[:, :, k * D:(k + 1) * D], mod[:, :, k * D:(k + 1) * D], 1.0, None, ALU.add)
            ins.then_inc(mod_cp, 1)
            v.wait_ge(mod_cp, B + 1)
            v.wait_ge(late_in, 16 * NLATE)
            attention(0, True, False)
            with v.Fori(1, B - 1) as b:
                attention(b, False, False)
            attention(B - 1, False, True)
            norm2(B - 1, 0)
            v.wait_ge(n2_t, B - 1)
            norm2(B - 1, 1)

            v.wait_ge(ones_set, 3)
            v.memset(pmax[:, :, :, :], -3e38).then_inc(ones_set, 1)
            v.wait_ge(ones_set, 4)

            def read(e, bank, full, p, it, own):
                v.wait_ge(side_full, full)
                src = side_banks[bank]
                kind = e[0]
                if kind == "k":
                    h = slice(e[1] * 512, (e[1] + 1) * 512)
                    v.tensor_tensor(rp1[0:HD, 0, h], src[0:HD, :], cosb[0:HD, 1, h], ALU.mult)
                    ins = v.tensor_tensor(rp2[0:HD, 0, h], src[HD:P, :], sinb[HD:P, 1, h], ALU.mult)
                elif kind == "v":
                    both = src.rearrange("p (j d) -> p j d", d=HD)
                    v.tensor_copy(vb[:, p, :, 0:HD], both).then_inc(v_hi, 1)
                    v.wait_ge(v_hi, it + 1)
                    ins = v.tensor_tensor(vb[:, p, :, HD + 2:VW], both, vb[:, p, :, 0:HD], ALU.subtract)
                elif kind in "qr":
                    h = slice(e[2] * 512, (e[2] + 1) * 512)
                    dst, tab = (rp1, cosb) if kind == "q" else (rp2, sinb)
                    if e == ("q", 1, 0):
                        v.wait_ge(r_lo, 3 * it + 1)
                    ins = v.tensor_tensor(dst[:, 1 - e[1], h], src, tab[:, 0, h], ALU.mult)
                elif kind == "max":
                    g, i, h = (e[1] + 1) % G, e[2], e[3]
                    w = min(4, i + 1 - 4 * h) * P
                    ins = v.tensor_reduce(pmax[:, g % 2, i, h:h + 1], src[:, 0:w], AX.X, ALU.max)
                else:
                    row = (it // HKV if not isinstance(it, int) else it // HKV)
                    dst = hres[:, row, 4 * e[1]:4 * e[1] + 4, :].rearrange("p j d -> p (j d)")
                    ins = v.tensor_tensor(dst, dst, src, ALU.add)
                ins.then_inc(side_V, 1)
                if kind == "max" and (e[2], e[3]) == PIECES[-1]:
                    g = (e[1] + 1) % G
                    v.wait_ge(side_V, own + 1)
                    v.tensor_reduce(hmax[:, g % 2, :], pmax[:, g % 2, :, :], AX.X, ALU.max, negate=True).then_inc(max_ready, 1)

            def norm(it, p, g, bank, part):
                n = 3 * (it * G + g) + bank
                m = len(OBANK[bank])
                at = slice(3 * bank, 3 * bank + m)
                o = out_banks[bank][:, 0:m * VW].rearrange("p (i d) -> p i d", d=VW)
                dst = att[:, p, at, g * HD:(g + 1) * HD]
                if part == 1:
                    v.wait_ge(b_low, n + 1)
                    v.reciprocal(oinv[:, at], o[:, :, HD]).then_inc(b_sum, 1)
                    v.tensor_tensor(dst, dst, o[:, :, 0:HD], ALU.add).then_inc(b_read, 1)
                elif part == 2:
                    v.wait_ge(b_sum, n + 1)
                    v.wait_ge(b_read, n + 1)
                    v.tensor_tensor(dst, dst, oinv[:, at].unsqueeze(2).to_broadcast([P, m, HD]), ALU.mult).then_inc(b_norm, 1)

            def low_probs(it, s):
                v.wait_ge(b_hi, it * SPR + s + 1)
                v.tensor_tensor(pl[:, s % 4, :], pf[:, s % 4, :], ph[:, s % 4, :], ALU.subtract).then_inc(lo_V, 1)

            def high_half(c, n, p):
                v.wait_ge(r_sum, 3 * n + c + 1)
                t = (0, 1, 0)[c]
                if c == 0:
                    v.tensor_copy(kB[0:HD, p, :], rp1[0:HD, t, :]).then_inc(r_hi, 1)
                else:
                    v.tensor_copy(qhi[:, c - 1, :], rp1[:, t, :]).then_inc(r_hi, 1)

            own = 0
            for i, e in enumerate(PROLOGUE):
                if reader(e) == "V":
                    read(e, i % SB, i + 1, 0, 0, own)
                    own += 1
                if e in HIGH_AFTER:
                    high_half(HIGH_AFTER[e], 0, 0)
                if e in NORM_AFTER:
                    norm2(B - 1, NORM_AFTER[e])

            def vec_round(it, p, first, last):
                steps = side_work(first, last)
                i, own = 0, 0
                for s in range(SPR):
                    h, c = divmod(s, SPH)
                    between = []
                    if s >= 1 and s - 1 in LOW_V:
                        between.append(lambda s=s: low_probs(it, s - 1))
                    if s == 0 and not first and SPR - 1 in LOW_V:
                        between.append(lambda: low_probs(it - 1, SPR - 1))
                    if c >= 6:
                        between.append(lambda h=h, c=c: norm(it, p, h, 0, c % 3))
                    elif h > 0:
                        between.append(lambda h=h, c=c: norm(it, p, h - 1, 1 + c // 3, c % 3))
                    elif not first:
                        between.append(lambda c=c: norm(it - 1, 1 - p, G - 1, 1 + c // 3, c % 3))
                    if s in HIGH_AT and not last:
                        between.append(lambda s=s: high_half(HIGH_AT[s], it + 1, 1 - p))
                    for e in steps[s]:
                        if reader(e) == "V":
                            n = it - 1 if e[0] == "out" else it + 1
                            read(e, i % SB, start(it) + i + 1, 1 - p, n, start(it, "V") + own)
                            own += 1
                            if between:
                                between.pop(0)()
                        i += 1
                    for f in between:
                        f()

            vec_round(0, 0, True, False)
            with v.Fori(1, NKV - 1, 2) as it:
                vec_round(it, 1, False, False)
                vec_round(it + 1, 0, False, False)
            vec_round(NKV - 1, 1, False, True)
            for bank in (1, 2):
                for part in range(3):
                    norm(NKV - 1, 1, G - 1, bank, part)
            own = 0
            for i, e in enumerate(EPILOGUE):
                if reader(e) == "V":
                    read(e, i % SB, start(NKV) + i + 1, 0, NKV - 1, start(NKV, "V") + own)
                    own += 1
            v.wait_ge(side_V, start(NKV, "V") + count(EPILOGUE, "V"))

            ch = Chain(vecc, 0, 71)
            for b in range(B):
                src = hres[:, b, :, :]
                if b % 2 == 0:
                    ch(v.tensor_tensor(wk1[:, :, :], src, src, ALU.mult))
                    ch(v.tensor_reduce(st4[:, b, 0, :], wk1[:, :, :], AX.X, ALU.add))
                else:
                    v.wait_ge(rt_sq, b // 2 + 1)
                    ch(v.tensor_reduce(st4[:, b, 0, :], rsq[b // 2], AX.X, ALU.add))
            v.tensor_copy(hf[:, :, :, D], token_no.rearrange("p (b j) -> p b j", b=B))
            v.tensor_scalar(st4[:, :, 1, :], st4[:, :, 0, :], 1.0 / D, RMS_EPS, ALU.mult, ALU.add).then_inc(rt_var, 1)
            for b in range(B):
                v.wait_ge(rt_rstd, b + 1)
                ch(v.tensor_tensor(wk1[:, :, :], hres[:, b, :, :], bc_tok(rstd4[:, b, :]), ALU.mult))
                v.tensor_tensor(hf[:, b, :, 0:D], wk1[:, :, :], bc_row(gb2[:, :]), ALU.mult).then_inc(rt_ready, 1)
                v.wait_ge(rt_ready, b + 1)

            v.wait_ge(rt_mm, B)
            ch(v.tensor_tensor(lg, psT[:, 0, 0:NE].rearrange("p (n e) -> p n e", e=E),
                               rbb[:, :].unsqueeze(1).to_broadcast([P, NTT, E]), ALU.add))
            for n in range(NTT):
                ins = v.max(v8[:, n, :], lg[:, n, :])
            ch(ins)
            v.tensor_tensor(sm1[:, :], v8[:, :, 1], v8[:, :, 0], ALU.subtract).then_inc(rt_d, 1)
            for n in range(NTT):
                ins = v.max_index(ix[:, n, :], v8[:, n, :], lg[:, n, :])
            ch(ins)
            ch(v.tensor_copy(ixf, ix[:, :, 0:TOPK]))
            ch(v.tensor_tensor(oh.rearrange("p n k e -> p (n k) e"), iota8.unsqueeze(1).to_broadcast([P, NTT * TOPK, E]),
                               ixf.rearrange("p n k -> p (n k)").unsqueeze(2).to_broadcast([P, NTT * TOPK, E]), ALU.is_equal))

            ohb = oh.rearrange("p (b j) k e -> p b j (k e)", b=B)
            cntb = cnt.rearrange("p (b j) k e -> p b j (k e)", b=B)
            ch(v.tensor_reduce(row_sum, ohb.rearrange("p b j a -> p b a j"), AX.X, ALU.add))
            v.tensor_copy(row_sum16[:, :], row_sum.rearrange("p b a -> p (b a)")).then_inc(rt_sum, 1)
            v.wait_ge(rt_e, 1)
            ch(v.tensor_scalar(sm1[:, :], sm2[:, :], 1.0, None, ALU.add))
            ch(v.reciprocal(sc[:, :, 0], sm1[:, :]))
            v.tensor_tensor(sc[:, :, 1], sm2[:, :], sc[:, :, 0], ALU.mult)
            v.wait_ge(rt_cnt, 1)
            for b in range(B):
                if b == 0:
                    ch(v.memset(carry[:, 0, :], 0.0))
                else:
                    ch(v.tensor_tensor(carry[:, b, :], carry[:, b - 1, :], psO[:, 1, (b - 1) * 16:b * 16], ALU.add))
            ch(v.tensor_tensor(start_c, carry[:, :, :], psO[:, 0, 0:B * 16].rearrange("p (b a) -> p b a", b=B), ALU.add))
            for j in range(NT):
                ch(v.tensor_tensor(cntb[:, :, j, :], start_c if j == 0 else cntb[:, :, j - 1, :], ohb[:, :, j, :], ALU.add))
            ch(v.tensor_tensor(cnt[:, :, 1, :], cnt[:, :, 1, :], cnt[:, :, 0, :], ALU.add))
            ch(v.scalar_tensor_tensor(em.rearrange("p n k e -> p (n k e)"), cnt.rearrange("p n k e -> p (n k e)"), float(CAP),
                                      oh.rearrange("p n k e -> p (n k e)"), ALU.is_lt, ALU.mult))
            ch(v.tensor_tensor(ea.rearrange("p n k e -> p (n k) e"), em.rearrange("p n k e -> p (n k) e"),
                               iota8.unsqueeze(1).to_broadcast([P, NTT * TOPK, E]), ALU.mult))
            ch(v.tensor_reduce(asg.rearrange("p n k -> p (n k)"), ea.rearrange("p n k e -> p (n k) e"), AX.X, ALU.add))
            allexp = expert[:, :, :].rearrange("p b j -> p (b j)")
            ch(v.tensor_reduce(allexp, asg, AX.X, ALU.max))

            ch(v.tensor_tensor(ohm, iota8.unsqueeze(2).to_broadcast([P, E, NTT]), allexp.unsqueeze(1).to_broadcast([P, E, NTT]),
                               ALU.is_equal))
            v.tensor_copy(ohm16[:, :], ohm.rearrange("p e n -> p (e n)")).then_inc(e_oh, 1)
            ch(v.tensor_reduce(tk.rearrange("p n k -> p (n k)"), em.rearrange("p n k e -> p (n k) e"), AX.X, ALU.add))
            ch(v.tensor_tensor(asg2, sc, tk, ALU.mult))
            v.tensor_reduce(wy[:, :, :].rearrange("p b j -> p (b j)"), asg2, AX.X, ALU.add)
            ch(v.tensor_tensor(ixf, sc, asg2, ALU.subtract))
            ch(v.tensor_reduce(wx[:, :, :].rearrange("p b j -> p (b j)"), ixf, AX.X, ALU.add))
            v.wait_ge(e_rank, 1)
            in_tile = psS[:, 0, 0:NE].rearrange("p (e n) -> p e n", e=E)
            of_tile = psS[:, 1, 0:NE].rearrange("p (e n) -> p e n", e=E)
            for e in range(E):
                ins = v.tensor_tensor_scan(upto[:, e, :], ones32[:, :], of_tile[:, e, :], 0.0, ALU.mult, ALU.add)
            ch(ins)
            ch(v.tensor_tensor(few, k128.unsqueeze(1).to_broadcast([P, E, 32]),
                               upto[:, :, NTT - 1:NTT].to_broadcast([P, E, 32]), ALU.is_lt))
            ch(v.tensor_reduce(ntile[:, :], few, AX.X, ALU.add))
            ch(v.tensor_tensor_scan(tend[:, :], ones32[:, 0:E], ntile[:, :], 0.0, ALU.mult, ALU.add))
            ch(v.tensor_tensor(base[:, :], tend[:, :], ntile[:, :], ALU.subtract))
            ch(v.tensor_scalar(base[:, :], base[:, :], float(P), None, ALU.mult))
            v.tensor_tensor(past, tile_no.unsqueeze(2).to_broadcast([P, ETILES, E]),
                            tend[:, :].unsqueeze(1).to_broadcast([P, ETILES, E]), ALU.is_ge)
            ch(v.tensor_tensor(past_e, upto, of_tile, ALU.subtract))
            ch(v.tensor_tensor(past_e, past_e, in_tile, ALU.add))
            ch(v.tensor_tensor(past_e, past_e, base[:, :].unsqueeze(2).to_broadcast([P, E, NTT]), ALU.add))
            ch(v.tensor_tensor(past_e, past_e, ohm, ALU.mult))
            ch(v.tensor_reduce(slotf[:, :], past_e.rearrange("p e n -> p n e"), AX.X, ALU.add))
            v.tensor_reduce(past7[:, :], past, AX.X, ALU.add)
            ch(v.tensor_copy(slot[:, :], slotf[:, :]))
            v.tensor_scalar(texp[:, :], past7[0:1, :], float(E - 1), None, ALU.min).then_inc(e_slot, 1)

            for b in range(B):
                r = hres[:, b, :, :]
                ch(v.tensor_tensor(wk1[:, :, :], hf[:, b, :, 0:D], bc_tok(wx[:, b, :]), ALU.mult))
                ch(v.tensor_tensor(r, r, wk1[:, :, :], ALU.add))
                ch(v.tensor_tensor(r, r, bc_mod(b, 5), ALU.mult))
                ch(v.tensor_tensor(r, r, x1[:, b, :, :], ALU.add))

            def rows(k, stored):
                turned, copied = psT[:, k % 2, 0:P], m_xTs[:, k % 4, :]
                k %= SLOTS
                if stored is not None:
                    v.wait_ge(m_out[k], 16 * stored)
                v.tensor_copy(back[:, k:k + 1], exp_xs[:, k * DW + D:(k + 1) * DW])
                v.tensor_copy(copied, turned).then_inc(m_xTc, 1)

            def outputs(t, k):
                v.wait_ge(m_y, t + 1)
                v.tensor_copy(m_yv[:, k, :], psO[:, k % 2, 0:P]).then_inc(m_yc, 1)

            def step(rr, k, ahead, behind):
                t = rr * SLOTS + k
                v.wait_ge(m_ab, t + 1)
                v.tensor_copy(m_av[:, k % 4, :], psE(k % 4)[:, 0:HID]).then_inc(m_a, 1)
                if ahead:
                    v.wait_ge(m_xT, t + 3)
                    rows(k + 2, rr + (k + 2) // SLOTS if behind or k + 2 >= SLOTS else None)
                v.wait_ge(m_a, t + 1)
                v.tensor_tensor(m_uv[:, k % 4, :], psE(k % 4)[:, HID:2 * HID], m_av[:, k % 4, :], ALU.mult).then_inc(m_u, 1)
                if behind or k >= 3:
                    outputs(t - 3, (k - 3) % SLOTS)

            for k in range(2):
                v.wait_ge(m_xT, k + 1)
                rows(k, None)
            for k in range(SLOTS):
                step(0, k, True, False)
            with v.Fori(1, ROUNDS - 1) as rr:
                for k in range(SLOTS):
                    step(rr, k, True, True)
            for k in range(SLOTS):
                step(ROUNDS - 1, k, k < SLOTS - 2, True)
            for t in range(ETILES - 3, ETILES):
                outputs(t, t % SLOTS)

            for b in range(B):
                v.wait_ge(gath[b], 16)
                for j in range(NT):
                    ins = v.scalar_tensor_tensor(yg[b][:, j, :], yg[b][:, j, :], wy[:, b, j:j + 1], mod[:, b, 5 * D:6 * D],
                                                 ALU.mult, ALU.mult)
                if b < 2:
                    ins.then_inc(weighted, 1)
                else:
                    ch(ins)
                    v.tensor_tensor(yg[b], yg[b], hres[:, b, :, :], ALU.add).then_inc(fin, 1)
            ch.end()


def kernel(**inputs):
    import concourse.bacc as _bacc
    from concourse.bass_utils import run_bass_kernel_spmd as _run

    inp = {k: np.asarray(v) for k, v in inputs.items()}

    def row(a):
        return np.ascontiguousarray(a.reshape(-1))

    half = HD // 2
    turned = np.concatenate([np.arange(half, HD), np.arange(half)])

    def heads(w, hs, rot):
        cols = np.concatenate([h * HD + (turned if rot else np.arange(HD)) for h in hs])
        return w[:, cols]

    wq, wk, wv, wo = (inp["L0_ffn_" + n] for n in ("wq", "wk", "wv", "wo"))
    w_kv, w_o = [], []
    for h in range(HKV):
        pairs = [(h, HKV + h), (2 * HKV + h, 3 * HKV + h)]
        w_kv.append(np.concatenate([heads(wq, pairs[0], False), heads(wq, pairs[0], True), heads(wq, pairs[1], False),
                                    heads(wq, pairs[1], True), heads(wk, [h], False), heads(wk, [h], True),
                                    heads(wv, [h], False)], axis=1))
    for h in range(HKV):
        rows = [np.concatenate([wo[q * HD:(q + 1) * HD] for q in pr]) for pr in ((h, HKV + h), (2 * HKV + h, 3 * HKV + h))]
        w_o.append(np.concatenate(rows, axis=1))
    w1, w2, w3 = (inp["L0_ffn_" + n] for n in ("w1", "w2", "w3"))
    w_exp = np.concatenate([w2, w1, w3[:, 0:P], w3[:, P:2 * P]], axis=2)

    thetas = 10000.0 ** (-np.arange(0, HD, 2, dtype=np.float32) / HD)
    ticks = np.outer(np.arange(S, dtype=np.float32), thetas)
    cos, sin = (np.tile(f(ticks), (1, 4)).T for f in (np.cos, np.sin))
    sign = np.where(np.arange(P) % HD < half, -1.0, 1.0)[:, None].astype(np.float32)
    scale = np.array([1.0 / np.sqrt(HD), 1.0], np.float32)[None, :, None]
    q = np.arange(P)
    consts = np.zeros((P, 3 * P + 48 + 2 * ETILES + NTT), np.float32)
    consts[:, 0:P] = np.eye(P)
    consts[:, P:2 * P] = np.where(q[None, :] > q[:, None], -1e30, 0.0)
    consts[:, 2 * P:3 * P] = consts[:, P:2 * P].T
    consts[:, 3 * P:3 * P + 8] = -0.5
    consts[:, 3 * P + 8:3 * P + 16] = np.arange(8)
    consts[:, 3 * P + 16:3 * P + 48] = np.arange(32) * P
    c = 3 * P + 48
    consts[:, c:c + ETILES] = np.arange(ETILES)
    t = np.arange(NTT)[None, :]
    consts[:, c + ETILES:c + ETILES + NTT] = t // NT * S + q[:, None] * NT + t % NT
    consts[:, c + ETILES + NTT:] = NTOK + np.arange(ETILES)[None, :] * P + q[:, None]

    arrays = {
        "x": inp["L0_attn_x"], "cT": inp["L0_c"].T, "wmod": inp["L0_wmod"], "w_qkvT": inp["L0_attn_w_qkv"].T,
        "w_projT": inp["L0_attn_w_proj"].T, "b_proj": row(inp["L0_attn_b_proj"]), "g1": row(inp["L0_ffn_g1"]),
        "g2": row(inp["L0_ffn_g2"]), "w_kv": np.stack(w_kv), "w_o": np.stack(w_o),
        "router_w": inp["L0_ffn_router_w"], "router_b": row(inp["L0_ffn_router_b"]), "w_exp": w_exp,
        "consts": consts, "cos_t": (cos[:, None, :] * scale).astype(np.float32),
        "sin_t": ((sin * sign)[:, None, :] * scale).astype(np.float32),
    }
    arrays = {k: np.ascontiguousarray(v) for k, v in arrays.items()}
    nc = _bacc.Bacc("TRN2", target_bir_lowering=False, num_devices=1)
    args = {k: nc.dram_tensor(k + "_dram", v.shape, mybir.dt.from_np(v.dtype), kind="ExternalInput").ap()
            for k, v in arrays.items()}
    out = nc.dram_tensor("out_dram", (B, S, D), F32, kind="ExternalOutput").ap()
    build(nc, *args.values(), out)
    r = _run(nc, [{k + "_dram": v for k, v in arrays.items()}], core_ids=[0])
    return r.results[0]["out_dram"]
```
